# Optimizing a Trainium2 kernel written in Bass

```python
import numpy as np
import jax
import jax.numpy as jnp

def _softmax(x, axis=-1):
    return jax.nn.softmax(x, axis=axis)

def _gelu(x):
    return jax.nn.gelu(x, approximate=True)

def _silu(x):
    return jax.nn.silu(x)

def _sigmoid(x):
    return jax.nn.sigmoid(x)

def _layernorm(x, axis=-1, eps=1e-05):
    m = jnp.mean(x, axis=axis, keepdims=True)
    v = jnp.var(x, axis=axis, keepdims=True)
    return (x - m) / jnp.sqrt(v + eps)

def _scatter_add(tgt, idx, src, axis=0):
    return tgt.at[idx].add(src)

def _segment_sum(src, seg, n):
    return jax.ops.segment_sum(src, seg, n)
kernel_name = 'mk_adj_preln_d4_adj_r2_e5e4aa'

def setup_inputs(seed: int=0):
    np.random.seed(seed)
    _w = jnp.asarray

    def _rec_inputs():
        import jax
        import jax.numpy as jnp
        _gk = jax.random.key(seed)
        x = -0.0005207 + 1.001 * jax.random.normal(jax.random.fold_in(_gk, 1), (4096, 256), jnp.float32)
        _w = (1.0 + jnp.arange(4096, dtype=jnp.float32)) ** (-0.5)
        _w = _w / _w.mean()
        _pij = jnp.clip(0.000488281 * _w[:, None] * _w[None, :], 0.0, 1.0)
        _a = jax.random.uniform(jax.random.fold_in(_gk, 2), (4096, 4096)) < _pij
        adj = _a.astype(jnp.int32)
        return (x, adj)
    x, adj = _rec_inputs()

    def _L0_gnn_setup():
        import jax, jax.numpy as jnp
        import numpy as np
        N, IN_DIM, OUT_DIM = (2048, 256, 256)
        H, D = (8, OUT_DIM // 8)
        ALPHA = 0.2
        NEG = -9000000000000000.0
        EPS = 1e-05
        key = jax.random.key(seed)
        k1, k2, k3, k4 = jax.random.split(key, 4)
        x = jax.random.normal(k1, (N, IN_DIM), dtype=jnp.float32)
        adj = jax.random.randint(k2, (N, N), 0, 2, dtype=jnp.int32)
        W = jax.random.normal(k3, (OUT_DIM, IN_DIM), dtype=jnp.float32) / np.sqrt(IN_DIM)
        a = jax.random.normal(k4, (2 * D,), dtype=jnp.float32) / np.sqrt(2 * D)
        gamma = jnp.ones((OUT_DIM,), dtype=jnp.float32)
        beta = jnp.zeros((OUT_DIM,), dtype=jnp.float32)
        return {'x': x, 'adj': adj, 'W': W, 'a': a, 'gamma': gamma, 'beta': beta}
    _L0_gnn_all = _L0_gnn_setup()
    _L0_gnn_in = {k: v for k, v in _L0_gnn_all.items() if k in ('W', 'a', 'gamma', 'beta')}
    del _L0_gnn_all

    def _L1_gnn_setup():
        import jax, jax.numpy as jnp
        import numpy as np
        N_X, N_NEIGH, D_IN, D_HID, D_OUT = (4096, 4096, 256, 32, 128)
        NEG_BIG = -9000000000000000.0
        key = jax.random.key(seed)
        ks = jax.random.split(key, 16)
        s_in = 1.0 / np.sqrt(D_IN)
        s_hid = 1.0 / np.sqrt(D_HID)
        return {'x': jax.random.normal(ks[0], (N_X, D_IN), jnp.float32), 'neigh': jax.random.normal(ks[1], (N_NEIGH, D_IN), jnp.float32), 'adj': jax.random.randint(ks[2], (N_X, N_NEIGH), 0, 2, jnp.int32), 'Wx1': jax.random.uniform(ks[3], (D_IN, D_HID), jnp.float32, -s_in, s_in), 'bx1': jnp.zeros((D_HID,), jnp.float32), 'Wx2': jax.random.uniform(ks[4], (D_HID, D_HID), jnp.float32, -s_hid, s_hid), 'bx2': jnp.zeros((D_HID,), jnp.float32), 'Wn1': jax.random.uniform(ks[5], (D_IN, D_HID), jnp.float32, -s_in, s_in), 'bn1': jnp.zeros((D_HID,), jnp.float32), 'Wn2': jax.random.uniform(ks[6], (D_HID, D_HID), jnp.float32, -s_hid, s_hid), 'bn2': jnp.zeros((D_HID,), jnp.float32), 'Wv': jax.random.uniform(ks[7], (D_IN, D_OUT), jnp.float32, -s_in, s_in), 'bv': jnp.zeros((D_OUT,), jnp.float32), 'Wfx': jax.random.uniform(ks[8], (D_IN, D_OUT), jnp.float32, -s_in, s_in), 'bfx': jnp.zeros((D_OUT,), jnp.float32)}
    _L1_gnn_all = _L1_gnn_setup()
    _L1_gnn_in = {k: v for k, v in _L1_gnn_all.items() if k in ('neigh', 'Wx1', 'bx1', 'Wx2', 'bx2', 'Wn1', 'bn1', 'Wn2', 'bn2', 'Wv', 'bv', 'Wfx', 'bfx')}
    del _L1_gnn_all

    def _L2_gnn_setup():
        import jax, jax.numpy as jnp
        import numpy as np
        N, D_IN, D_OUT = (4096, 256, 256)
        key = jax.random.key(seed)
        ks = jax.random.split(key, 8)
        scale_in = 1.0 / np.sqrt(D_IN)
        scale_cat = 1.0 / np.sqrt(2 * D_OUT)
        return {'x': jax.random.normal(ks[0], (N, D_IN), dtype=jnp.float32), 'adj': jax.random.randint(ks[1], (N, N), 0, 2, dtype=jnp.int32), 'W_self': jax.random.uniform(ks[2], (D_IN, D_OUT), jnp.float32, -scale_in, scale_in), 'b_self': jax.random.uniform(ks[3], (D_OUT,), jnp.float32, -scale_in, scale_in), 'W_nb': jax.random.uniform(ks[4], (D_IN, D_OUT), jnp.float32, -scale_in, scale_in), 'b_nb': jax.random.uniform(ks[5], (D_OUT,), jnp.float32, -scale_in, scale_in), 'W_comb': jax.random.uniform(ks[6], (2 * D_OUT, D_OUT), jnp.float32, -scale_cat, scale_cat), 'b_comb': jax.random.uniform(ks[7], (D_OUT,), jnp.float32, -scale_cat, scale_cat)}
    _L2_gnn_all = _L2_gnn_setup()
    _L2_gnn_in = {k: v for k, v in _L2_gnn_all.items() if k in ('W_self', 'b_self', 'W_nb', 'b_nb', 'W_comb', 'b_comb')}
    del _L2_gnn_all

    def _L3_gnn_setup():
        import jax, jax.numpy as jnp
        import numpy as np
        N = 4096
        D_IN = 256
        D_OUT = 256
        key = jax.random.key(seed)
        k1, k2, k3, k4 = jax.random.split(key, 4)
        node_feats = jax.random.normal(k1, (N, D_IN), dtype=jnp.float32)
        adj_matrix = jax.random.randint(k2, (N, N), 0, 2, dtype=jnp.int32)
        w_self = jax.random.normal(k3, (D_OUT, D_IN), dtype=jnp.float32) * D_IN ** (-0.5)
        w_neigh = jax.random.normal(k4, (D_OUT, D_IN), dtype=jnp.float32) * D_IN ** (-0.5)
        return {'node_feats': node_feats, 'adj_matrix': adj_matrix, 'w_self': w_self, 'w_neigh': w_neigh}
    _L3_gnn_all = _L3_gnn_setup()
    _L3_gnn_in = {k: v for k, v in _L3_gnn_all.items() if k in ('w_self', 'w_neigh')}
    del _L3_gnn_all
    return {'x': x, 'adj': adj, 'L0_gnn_W': _L0_gnn_in['W'], 'L0_gnn_a': _L0_gnn_in['a'], 'L0_gnn_gamma': _L0_gnn_in['gamma'], 'L0_gnn_beta': _L0_gnn_in['beta'], 'L1_gnn_neigh': _L1_gnn_in['neigh'], 'L1_gnn_Wx1': _L1_gnn_in['Wx1'], 'L1_gnn_bx1': _L1_gnn_in['bx1'], 'L1_gnn_Wx2': _L1_gnn_in['Wx2'], 'L1_gnn_bx2': _L1_gnn_in['bx2'], 'L1_gnn_Wn1': _L1_gnn_in['Wn1'], 'L1_gnn_bn1': _L1_gnn_in['bn1'], 'L1_gnn_Wn2': _L1_gnn_in['Wn2'], 'L1_gnn_bn2': _L1_gnn_in['bn2'], 'L1_gnn_Wv': _L1_gnn_in['Wv'], 'L1_gnn_bv': _L1_gnn_in['bv'], 'L1_gnn_Wfx': _L1_gnn_in['Wfx'], 'L1_gnn_bfx': _L1_gnn_in['bfx'], 'L2_gnn_W_self': _L2_gnn_in['W_self'], 'L2_gnn_b_self': _L2_gnn_in['b_self'], 'L2_gnn_W_nb': _L2_gnn_in['W_nb'], 'L2_gnn_b_nb': _L2_gnn_in['b_nb'], 'L2_gnn_W_comb': _L2_gnn_in['W_comb'], 'L2_gnn_b_comb': _L2_gnn_in['b_comb'], 'L3_gnn_w_self': _L3_gnn_in['w_self'], 'L3_gnn_w_neigh': _L3_gnn_in['w_neigh']}

def reference(x, adj, L0_gnn_W, L0_gnn_a, L0_gnn_gamma, L0_gnn_beta, L1_gnn_neigh, L1_gnn_Wx1, L1_gnn_bx1, L1_gnn_Wx2, L1_gnn_bx2, L1_gnn_Wn1, L1_gnn_bn1, L1_gnn_Wn2, L1_gnn_bn2, L1_gnn_Wv, L1_gnn_bv, L1_gnn_Wfx, L1_gnn_bfx, L2_gnn_W_self, L2_gnn_b_self, L2_gnn_W_nb, L2_gnn_b_nb, L2_gnn_W_comb, L2_gnn_b_comb, L3_gnn_w_self, L3_gnn_w_neigh):
    import jax
    import jax.numpy as jnp

    def _L0_gnn_ref(x, adj, W, a, gamma, beta):
        import jax, jax.numpy as jnp
        import numpy as np
        N, IN_DIM, OUT_DIM = (2048, 256, 256)
        H, D = (8, OUT_DIM // 8)
        ALPHA = 0.2
        NEG = -9000000000000000.0
        EPS = 1e-05
        n = x.shape[0]
        Wh = (x @ W.T).reshape(n, H, D)
        a_src, a_dst = (a[:D], a[D:])
        s_src = jnp.einsum('jhd,d->jh', Wh, a_src)
        s_dst = jnp.einsum('ihd,d->ih', Wh, a_dst)
        e = jax.nn.leaky_relu(s_dst[:, None, :] + s_src[None, :, :], negative_slope=ALPHA)
        e = jnp.where((adj > 0)[:, :, None], e, NEG)
        attn = jax.nn.softmax(e, axis=1)
        h_prime = jnp.einsum('ijh,jhd->ihd', attn, Wh).reshape(n, H * D)
        mean = jnp.mean(h_prime, axis=0)
        var = jnp.var(h_prime, axis=0)
        h_prime = gamma * (h_prime - mean) * jax.lax.rsqrt(var + EPS) + beta
        return jax.nn.relu(h_prime)

    def _L1_gnn_ref(x, neigh, adj, Wx1, bx1, Wx2, bx2, Wn1, bn1, Wn2, bn2, Wv, bv, Wfx, bfx):
        import jax, jax.numpy as jnp
        import numpy as np
        N_X, N_NEIGH, D_IN, D_HID, D_OUT = (4096, 4096, 256, 32, 128)
        NEG_BIG = -9000000000000000.0
        neib_att = jnp.tanh(neigh @ Wn1 + bn1) @ Wn2 + bn2
        value = neigh @ Wv + bv
        x_att = jnp.tanh(x @ Wx1 + bx1) @ Wx2 + bx2
        ws = jnp.einsum('nh,mh->nm', x_att, neib_att)
        ws = jax.nn.leaky_relu(ws, negative_slope=0.01)
        ws = jnp.where(adj > 0, ws, jnp.float32(NEG_BIG))
        ws = jax.nn.softmax(ws, axis=1)
        agg_neib = ws @ value
        out = jnp.concatenate([x @ Wfx + bfx, agg_neib], axis=1)
        return out

    def _L2_gnn_ref(x, adj, W_self, b_self, W_nb, b_nb, W_comb, b_comb):
        import jax, jax.numpy as jnp
        import numpy as np
        N, D_IN, D_OUT = (4096, 256, 256)
        mask = (adj > 0).astype(x.dtype)
        deg = jnp.sum(mask, axis=1, keepdims=True)
        agg = mask @ x / jnp.maximum(deg, 1.0)
        self_f = x @ W_self + b_self
        nb_f = agg @ W_nb + b_nb
        combined = jnp.concatenate([self_f, nb_f], axis=-1)
        out = combined @ W_comb + b_comb
        return jax.nn.relu(out)

    def _L3_gnn_ref(node_feats, adj_matrix, w_self, w_neigh):
        import jax, jax.numpy as jnp
        import numpy as np
        N = 4096
        D_IN = 256
        D_OUT = 256
        adj_f = adj_matrix.astype(node_feats.dtype)
        s = adj_f @ node_feats[:, 0]
        has_neigh = jnp.sum(adj_matrix, axis=1) > 0
        s = jnp.where(has_neigh, s, jnp.zeros_like(s))
        neigh_term = s[:, None] * jnp.sum(w_neigh, axis=1)[None, :]
        return jax.nn.relu(node_feats @ w_self.T + neigh_term)
    h = jnp.maximum(_layernorm(x, axis=-1), 0.0)
    x = x + _L0_gnn_ref(h, adj, L0_gnn_W, L0_gnn_a, L0_gnn_gamma, L0_gnn_beta)
    h = jnp.maximum(_layernorm(x, axis=-1), 0.0)
    x = x + _L1_gnn_ref(h, L1_gnn_neigh, adj, L1_gnn_Wx1, L1_gnn_bx1, L1_gnn_Wx2, L1_gnn_bx2, L1_gnn_Wn1, L1_gnn_bn1, L1_gnn_Wn2, L1_gnn_bn2, L1_gnn_Wv, L1_gnn_bv, L1_gnn_Wfx, L1_gnn_bfx)
    h = jnp.maximum(_layernorm(x, axis=-1), 0.0)
    x = x + _L2_gnn_ref(h, adj, L2_gnn_W_self, L2_gnn_b_self, L2_gnn_W_nb, L2_gnn_b_nb, L2_gnn_W_comb, L2_gnn_b_comb)
    h = jnp.maximum(_layernorm(x, axis=-1), 0.0)
    x = x + _L3_gnn_ref(h, adj, L3_gnn_w_self, L3_gnn_w_neigh)
    return x

_drawn_inputs = setup_inputs


def setup_inputs(seed=0):
    import zlib

    import numpy as np

    out = dict(_drawn_inputs(seed))
    spreads = {'L0_gnn_gamma': (1.0, 0.2),
     'L0_gnn_beta': (0.0, 0.1),
     'L1_gnn_bx1': (0.0, 0.8),
     'L1_gnn_bx2': (0.0, 0.8),
     'L1_gnn_bn1': (0.0, 0.8),
     'L1_gnn_bn2': (0.0, 0.8),
     'L1_gnn_bv': (0.0, 0.1),
     'L1_gnn_bfx': (0.0, 0.1)}
    factors = {'L1_gnn_Wx1': 3.473,
     'L1_gnn_Wx2': 3.768,
     'L1_gnn_Wn1': 3.254,
     'L1_gnn_Wn2': 3.278,
     'L2_gnn_b_self': 8.0,
     'L2_gnn_b_nb': 6.242,
     'L2_gnn_b_comb': 4.84}
    for name, (base, spread) in spreads.items():
        noise = np.random.default_rng([zlib.crc32(name.encode()), seed]).standard_normal(out[name].shape)
        drawn = base * np.exp(spread * noise) if base else spread * noise
        out[name] = jnp.asarray(drawn.astype(out[name].dtype))
    for name, factor in factors.items():
        out[name] = (out[name] * factor).astype(out[name].dtype)
    return out
```

```python
from contextlib import ExitStack

import concourse.bass as bass
from concourse import mybir

ALU = mybir.AluOpType
ACT = mybir.ActivationFunctionType
F32 = mybir.dt.float32
BF16 = mybir.dt.bfloat16
I32 = mybir.dt.int32
U32 = mybir.dt.uint32
AX = mybir.AxisListType

P = 128
N = 4096
D = 256
NT = N // P
SLOTS = 8
ITEM_CHUNKS = SLOTS
GROUP = 4
SETS = 4
PAD = GROUP * SETS
MAX_CHUNKS = NT * (N // SLOTS) * ITEM_CHUNKS + PAD
WORDS = 3
HEADS = 8
DH = D // HEADS
HID = 32
OUT1 = 128
H0 = HEADS * (DH + 1)
ROW0 = H0 + HEADS
H1 = OUT1 + 1
ROW1 = H1 + HID
EPS = 1e-5
NEVER = 9e15
W_J, W_TILE = 0, 2
H_ROW, H_SLOT = 2, 3
NOWHERE = 2 * N


class Steps:

    def __init__(self, eng, m):
        self.eng, self.m, self.sem, self.reg = eng, m, m.vec_steps, m.vec_count

    def done(self, ins):
        ins.then_inc(self.sem, 1)
        self.m.vec_open += 1
        return ins

    def wait(self):
        self.eng.wait_ge(self.sem, self.eng.snap(self.reg) + self.m.vec_open)

    def fold(self):
        if self.m.vec_open:
            self.eng.reg_add(self.reg, self.reg, self.m.vec_open)
        self.m.vec_open = 0


class Mem:
    pass


def constants(nc, m, sem):
    const_iota = sem("const_iota")
    const_base = sem("const_base")
    const_done = sem("const_done")
    with nc.Block() as block:
        @block.gpsimd
        def _(pool):
            nc.gpsimd.iota(m.iota_row_i[:, :], pattern=[[1, P]], base=0, channel_multiplier=0).then_inc(const_iota, 1)
            nc.gpsimd.iota(m.iota_col_i[:, :], pattern=[[1, 1]], base=0, channel_multiplier=1).then_inc(const_iota, 1)
            nc.gpsimd.memset(m.ident[:, :], 0.0).then_inc(const_base, 1)
            nc.gpsimd.memset(m.tri[:, :], 1.0).then_inc(const_base, 1)
            nc.gpsimd.memset(m.ones[:, :], 1.0)
            pool.wait_ge(const_base, 2)
            nc.gpsimd.affine_select(out=m.ident[:, :], in_=m.ident[:, :], compare_op=ALU.not_equal, fill=1.0,
                                    base=0, pattern=[[-1, P]], channel_multiplier=1)
            nc.gpsimd.affine_select(out=m.tri[:, :], in_=m.tri[:, :], compare_op=ALU.is_gt, fill=0.0,
                                    base=0, pattern=[[1, P]], channel_multiplier=-1)

        @block.vector
        def _(dve):
            dve.reg_mov(m.vec_count, 0)
            dve.wait_ge(const_iota, 2)
            nc.vector.tensor_copy(m.iota_row[:, :], m.iota_row_i[:, :])
            nc.vector.tensor_copy(m.iota_col[:, :], m.iota_col_i[:, :])


def scan(nc, m, sem, psum, adj, edges):
    adj_in = [sem(f"adj_in{i}") for i in range(2)]
    adj_free = [sem(f"adj_free{i}") for i in range(2)]
    deg_ready = sem("deg_ready")
    deg_row_ready = sem("deg_row_ready")
    rounds_ready = sem("rounds_ready")
    rounds_taken = sem("rounds_taken")
    count_ready = sem("count_ready")
    prefix_ready = sem("prefix_ready")
    chunks_ready = sem("chunks_ready")
    chunks_taken = sem("chunks_taken")
    place_ready = sem("place_ready")
    spread_ready = sem("spread_ready")
    record_ready = sem("record_ready")
    record_stored = sem("record_stored")

    with ExitStack() as ctx:
        def sb(name, shape, dt):
            return ctx.enter_context(nc.sbuf_tensor(name, shape, dt))
        A = [sb(f"adj{i}", [P, N], I32) for i in range(2)]
        junk = sb("scan_junk", [P, N], BF16)
        degc = [sb(f"degc{i}", [P, 1], F32) for i in range(2)]
        left = sb("left", [P, 1], F32)
        cnt = sb("cnt", [P, 1], F32)
        vals = sb("vals", [P, SLOTS], F32)
        J = sb("J", [P, SLOTS], U32)
        rowinfo = sb("rowinfo", [P, 12], F32)
        small = sb("scan_small", [P, 16], F32)
        ints = sb("scan_ints", [P, 4], I32)
        tile_no = sb("tile_no", [P, 1], F32)
        R1 = sb("R1", [P, P], F32)
        R = sb("R", [P, P], F32)
        pick = sb("pick", [P, SLOTS], F32)
        rec = sb("rec", [P, ITEM_CHUNKS, WORDS], I32)
        reci = rec[:, :, :]
        rech = rec[:, :, :].bitcast(BF16)
        ps_deg, ps_pre, ps_info = psum[0], psum[1], psum[2]
        mx, mx2, nchf, ncsum, jf = (small[:, i:i + 1] for i in range(5))

        with nc.Block() as block:
            @block.sync
            def _(sp):
                for i in range(2):
                    sp.sem_inc(adj_free[i], 1)
                with sp.Fori(0, NT // 2) as t2:
                    for i in range(2):
                        sp.wait_ge(adj_free[i], t2 + 1)
                        sp.dma_start(A[i][:, :], adj[bass.ds(t2 * (2 * P) + i * P, P), :]).then_inc(adj_in[i], 16)

            @block.scalar
            def _(act):
                act.sem_inc(deg_ready, 1)
                with act.Fori(0, NT // 2) as t2:
                    for i in range(2):
                        act.wait_ge(deg_ready, t2 * 2 + (i + 1))
                        act.wait_ge(adj_in[i], t2 * 16 + 16)
                        act.wait_ge(adj_free[i], t2 + 1)
                        nc.scalar.activation(junk[:, :], A[i][:, :], ACT.Copy, accum_out=degc[i][:, :]).then_inc(deg_ready, 1)

            @block.tensor
            def _(pe):
                with pe.register("scan_nr") as nr, pe.register("scan_nch") as nch, pe.register("scan_items") as items, \
                        pe.register("scan_chunks") as chunks:
                    pe.reg_mov(items, 0)
                    pe.reg_mov(chunks, 0)

                    def item():
                        it = pe.snap(items)
                        pe.wait_ge(count_ready, it + 1)
                        nc.tensor.matmul(ps_pre[:, 0:1], m.tri[:, :], cnt[:, :], start=True, stop=True)
                        nc.tensor.matmul(ps_pre[:, 1:2], m.ones[:, :], cnt[:, :], start=True, stop=True).then_inc(prefix_ready, 1)
                        pe.wait_ge(chunks_ready, it + 1)
                        pe.sem_inc(m.tick, 1)
                        pe.reg_load(nch, ints[0:1, 1:2])
                        pe.sem_inc(chunks_taken, 1)
                        with pe.Fori(0, pe.snap(nch, min_val=1, max_val=ITEM_CHUNKS)):
                            pe.wait_ge(place_ready, pe.snap(chunks) + 1)
                            nc.tensor.matmul(ps_info[:, 0:12], R[:, :], rowinfo[:, :], start=True, stop=True).then_inc(spread_ready, 1)
                            pe.reg_add(chunks, chunks, 1)
                        pe.reg_add(items, items, 1)

                    with pe.Fori(0, NT // 2) as t2:
                        for i in range(2):
                            pe.wait_ge(deg_ready, t2 * 2 + (i + 2))
                            nc.tensor.matmul(ps_deg[0:1, 0:P], degc[i][:, :], m.ident[:, :], start=True, stop=True).then_inc(deg_row_ready, 1)
                            pe.wait_ge(rounds_ready, t2 * 2 + (i + 1))
                            pe.sem_inc(m.tick, 1)
                            pe.reg_load(nr, ints[0:1, 0:1])
                            pe.sem_inc(rounds_taken, 1)
                            item()
                            n = pe.snap(nr, min_val=1, max_val=N // SLOTS)
                            with pe.If(n > 1):
                                with pe.Fori(1, n):
                                    item()

            @block.gpsimd
            def _(pool):
                with pool.register("scan_nr") as nr, pool.register("scan_nch") as nch, pool.register("scan_items") as items, \
                        pool.register("scan_chunks") as chunks:
                    pool.reg_mov(items, 0)
                    pool.reg_mov(chunks, 0)
                    pool.wait_ge(record_ready, 1)
                    pool.dma_start(edges[:, 0:ITEM_CHUNKS, :], reci).then_inc(record_stored, 16)

                    def store():
                        it = pool.snap(items)
                        pool.wait_ge(chunks_ready, it + 1)
                        pool.sem_inc(m.tick, 1)
                        pool.reg_load(nch, ints[0:1, 1:2])
                        pool.sem_inc(chunks_taken, 1)
                        pool.wait_ge(record_ready, it + 2)
                        pool.wait_ge(record_stored, it * 16 + 16)
                        pool.sem_inc(m.tick, 1)
                        at = pool.snap(chunks, min_val=0, max_val=MAX_CHUNKS - PAD)
                        pool.dma_start(edges[:, bass.ds(at, ITEM_CHUNKS), :], reci).then_inc(record_stored, 16)
                        pool.reg_add(chunks, chunks, pool.snap(nch, min_val=1, max_val=ITEM_CHUNKS))
                        pool.reg_add(items, items, 1)

                    with pool.Fori(0, NT // 2) as t2:
                        for i in range(2):
                            pool.wait_ge(rounds_ready, t2 * 2 + (i + 1))
                            pool.sem_inc(m.tick, 1)
                            pool.reg_load(nr, ints[0:1, 0:1])
                            pool.sem_inc(rounds_taken, 1)
                            store()
                            n = pool.snap(nr, min_val=1, max_val=N // SLOTS)
                            with pool.If(n > 1):
                                with pool.Fori(1, n):
                                    store()
                    it = pool.snap(items)
                    pool.wait_ge(record_ready, it + 2)
                    pool.wait_ge(record_stored, it * 16 + 16)
                    pool.sem_inc(m.tick, 1)
                    for extra in range(0, PAD, ITEM_CHUNKS):
                        if extra:
                            pool.reg_add(chunks, chunks, ITEM_CHUNKS)
                        at = pool.snap(chunks, min_val=0, max_val=MAX_CHUNKS - ITEM_CHUNKS)
                        pool.dma_start(edges[:, bass.ds(at, ITEM_CHUNKS), :], reci).then_inc(record_stored, 16)
                    pool.wait_ge(record_stored, it * 16 + 16 * (1 + PAD // ITEM_CHUNKS))
                    pool.sem_inc(m.tick, 1)

            @block.vector
            def _(dve):
                with dve.register("scan_nr") as nr, dve.register("scan_nch") as nch, dve.register("scan_items") as items, \
                        dve.register("scan_chunks") as chunks:
                    s = Steps(dve, m)
                    dve.reg_mov(items, 0)
                    dve.reg_mov(chunks, 0)
                    dve.sem_inc(chunks_taken, 2)
                    dve.sem_inc(rounds_taken, 2)
                    s.done(nc.vector.memset(rowinfo[:, 11:12], 1.0))
                    s.done(nc.vector.memset(ncsum, 0.0))
                    s.done(nc.vector.memset(tile_no[:, :], 0.0))
                    nc.vector.memset(rec[:, :, :], 0).then_inc(record_ready, 1)
                    s.done(nc.vector.tensor_scalar(rowinfo[:, 10:11], m.iota_col[:, :], 1.0, None, ALU.add))
                    s.fold()

                    def item(i, first):
                        it = dve.snap(items)
                        s.wait()
                        if not first:
                            dve.sem_inc(m.tick, 1)
                            s.done(nc.vector.match_replace(A[i][:, :], vals[:, :], A[i][:, :], 0.0))
                        ins = nc.vector.tensor_scalar(cnt[:, :], left[:, :], 0.0, float(SLOTS), ALU.max, ALU.min)
                        ins.then_inc(count_ready, 1)
                        dve.wait_ge(count_ready, it + 1)
                        s.done(nc.vector.tensor_scalar(vals[:, :], m.iota_row[:, 0:SLOTS], cnt[:, 0:1], None, ALU.is_lt))
                        s.done(nc.vector.tensor_scalar(left[:, :], left[:, :], float(SLOTS), None, ALU.subtract))
                        s.wait()
                        dve.sem_inc(m.tick, 1)
                        s.done(nc.vector.max_index(J[:, :], vals[:, :], A[i][:, :]))
                        dve.wait_ge(prefix_ready, it + 1)
                        dve.wait_ge(chunks_taken, it * 2 + 2)
                        s.done(nc.vector.tensor_scalar(nchf, ps_pre[:, 1:2], (P - 1) / 2, 1.0 / P, ALU.add, ALU.mult))
                        s.done(nc.vector.tensor_copy(rowinfo[:, 8:9], ps_pre[:, 0:1]))
                        s.done(nc.vector.tensor_tensor(rowinfo[:, 9:10], ps_pre[:, 0:1], cnt[:, :], ALU.add))
                        s.wait()
                        ins = nc.vector.tensor_scalar(ints[:, 1:2], nchf, 1.0, None, ALU.max)
                        ins.then_inc(chunks_ready, 1)
                        dve.wait_ge(chunks_ready, it + 1)
                        s.done(nc.vector.tensor_copy(nchf, ints[:, 1:2]))
                        s.done(nc.vector.tensor_copy(rowinfo[:, 0:SLOTS], J[:, :]))
                        s.wait()
                        s.done(nc.vector.tensor_tensor(ncsum, ncsum, nchf, ALU.add))
                        dve.wait_ge(record_stored, it * 16 + 16)
                        dve.sem_inc(m.tick, 1)
                        dve.reg_load(nch, ints[0:1, 1:2])
                        s.fold()
                        with dve.Fori(0, dve.snap(nch, min_val=1, max_val=ITEM_CHUNKS)) as c:
                            s.wait()
                            s.done(nc.vector.tensor_scalar(R1[:, :], m.iota_row[:, :], rowinfo[:, 8:9], None, ALU.is_ge))
                            s.wait()
                            ins = nc.vector.scalar_tensor_tensor(R[:, :], m.iota_row[:, :], rowinfo[:, 9:10], R1[:, :], ALU.is_lt, ALU.mult)
                            ins.then_inc(place_ready, 1)
                            s.done(nc.vector.tensor_scalar(reci[:, bass.ds(c, 1), W_TILE], tile_no[:, :], 0.0, None, ALU.add))
                            dve.wait_ge(spread_ready, dve.snap(chunks) + 1)
                            s.done(nc.vector.tensor_scalar(rowinfo[:, 8:10], rowinfo[:, 8:10], float(P), None, ALU.subtract))
                            s.done(nc.vector.tensor_tensor(small[:, 6:7], m.iota_col[:, :], ps_info[:, 8:9], ALU.subtract))
                            s.done(nc.vector.tensor_scalar(rech[:, bass.ds(c, 1), H_ROW], ps_info[:, 10:11], 1.0, None, ALU.subtract))
                            s.done(nc.vector.tensor_scalar(small[:, 7:8], ps_info[:, 11:12], -float(NOWHERE), float(NOWHERE), ALU.mult, ALU.add))
                            s.wait()
                            s.done(nc.vector.scalar_tensor_tensor(pick[:, :], m.iota_row[:, 0:SLOTS], small[:, 6:7], ps_info[:, 0:SLOTS], ALU.is_equal, ALU.mult, accum_out=jf))
                            s.done(nc.vector.tensor_scalar(rech[:, bass.ds(c, 1), H_SLOT], small[:, 6:7], 0.0, None, ALU.add))
                            s.wait()
                            s.done(nc.vector.tensor_tensor(reci[:, bass.ds(c, 1), W_J], jf, small[:, 7:8], ALU.add))
                            dve.reg_add(chunks, chunks, 1)
                            s.fold()
                        s.wait()
                        dve.sem_inc(record_ready, 1)
                        dve.reg_add(items, items, 1)

                    with dve.Fori(0, NT // 2) as t2:
                        for i in range(2):
                            dve.wait_ge(deg_row_ready, t2 * 2 + (i + 1))
                            s.done(nc.vector.tensor_reduce(mx[0:1, :], ps_deg[0:1, 0:P], AX.X, ALU.max))
                            s.done(nc.vector.tensor_scalar(left[:, :], degc[i][:, :], 0.0, None, ALU.add))
                            s.wait()
                            s.done(nc.vector.tensor_scalar(mx2[0:1, :], mx[0:1, :], (SLOTS - 1) / 2, 1.0 / SLOTS, ALU.add, ALU.mult))
                            dve.wait_ge(rounds_taken, t2 * 4 + (2 * i + 2))
                            s.wait()
                            ins = nc.vector.tensor_scalar(ints[0:1, 0:1], mx2[0:1, :], 1.0, None, ALU.max)
                            ins.then_inc(rounds_ready, 1)
                            s.done(nc.vector.tensor_copy(m.degree[:, bass.ds(t2 * 2 + i, 1)], degc[i][:, :]))
                            s.fold()
                            s.wait()
                            dve.wait_ge(rounds_ready, t2 * 2 + (i + 1))
                            dve.sem_inc(m.tick, 1)
                            dve.reg_load(nr, ints[0:1, 0:1])
                            item(i, True)
                            n = dve.snap(nr, min_val=1, max_val=N // SLOTS)
                            with dve.If(n > 1):
                                with dve.Fori(1, n):
                                    item(i, False)
                            s.wait()
                            dve.sem_inc(adj_free[i], 1)
                            s.done(nc.vector.tensor_scalar(tile_no[:, :], tile_no[:, :], 1.0, None, ALU.add))
                            s.fold()
                    it = dve.snap(items)
                    s.wait()
                    dve.wait_ge(chunks_taken, it * 2 + 2)
                    dve.wait_ge(record_stored, it * 16 + 16)
                    s.done(nc.vector.tensor_scalar(small[:, 5:6], ncsum, (PAD - 1) / 2, 1.0 / PAD, ALU.add, ALU.mult))
                    s.done(nc.vector.memset(reci[:, :, W_J], NOWHERE))
                    s.done(nc.vector.memset(rech[:, :, H_ROW], -1.0))
                    s.done(nc.vector.memset(rech[:, :, H_SLOT], 0.0))
                    s.done(nc.vector.memset(reci[:, :, W_TILE], 0))
                    s.wait()
                    s.done(nc.vector.tensor_scalar(m.passes[:, :], small[:, 5:6], 1.0, None, ALU.max))
                    s.wait()
                    dve.sem_inc(record_ready, 1)



def tile_of(t, number, width):
    return t[:, bass.ds(number * width, width)]


def weights(nc, m, sem, psum, a):
    w_in = sem("w_in")
    w_turned = sem("w_turned")
    w_used = sem("w_used")
    w_folded = sem("w_folded")
    w_steps = sem("w_steps")
    heads_ready = sem("heads_ready")
    n = {"in": 0}
    with ExitStack() as ctx:
        def sb(name, shape):
            return ctx.enter_context(nc.sbuf_tensor(name, shape, F32))
        W0 = sb("W0", [P, 2, D])
        Ws = sb("Ws", [P, 2, D])
        Wn = sb("Wn", [P, 2, D])
        Wc = sb("Wc", [P, 4, D])
        S3 = sb("S3", [P, 2, D])
        N3 = sb("N3", [P, 2, D])
        WsT = sb("WsT", [P, 2, D])
        WnT = sb("WnT", [P, 2, D])
        N3T = sb("N3T", [P, 2, D])
        acol = sb("acol", [P, 2])
        heads = sb("heads", [P, 2, 2 * HEADS])
        bcol = sb("bcol", [P, 2, 2])
        bcomb = sb("bcomb", [1, D])
        folded = lambda w: w.rearrange("(c p) n -> p c n", p=P)
        loads = [(W0[:, :, :], folded(a["L0_gnn_W"])), (Ws[:, :, :], folded(a["L2_gnn_W_self"])),
                 (Wn[:, :, :], folded(a["L2_gnn_W_nb"])), (Wc[:, :, :], folded(a["L2_gnn_W_comb"])),
                 (S3[:, :, :], folded(a["L3_gnn_w_self"])), (N3[:, :, :], folded(a["L3_gnn_w_neigh"])),
                 (m.Wx1[:, :, :], folded(a["L1_gnn_Wx1"])), (m.Wn1[:, :, :], folded(a["L1_gnn_Wn1"])),
                 (m.Wv[:, :, :], folded(a["L1_gnn_Wv"])), (m.Wfx[:, :, :], folded(a["L1_gnn_Wfx"])),
                 (m.Wx2[:, :], a["L1_gnn_Wx2"]), (m.Wn2[:, :], a["L1_gnn_Wn2"]),
                 (m.bias_n[0:1, 0:OUT1], a["L1_gnn_bv"][None, :]), (m.bias_n[0:1, OUT1:OUT1 + HID], a["L1_gnn_bn2"][None, :]),
                 (m.bias_x[0:1, 0:HID], a["L1_gnn_bx2"][None, :]), (m.bias_x[0:1, HID:HID + OUT1], a["L1_gnn_bfx"][None, :]),
                 (m.norm_in[0:1, 0:D], a["L0_gnn_gamma"][None, :]), (m.norm_in[0:1, D:2 * D], a["L0_gnn_beta"][None, :]),
                 (bcomb[:, :], a["L2_gnn_b_comb"][None, :])]
        thin = [(m.bx1[:, :], a["L1_gnn_bx1"][:, None]), (m.bn1[:, :], a["L1_gnn_bn1"][:, None]),
                (bcol[:, :, 0:1], a["L2_gnn_b_self"].rearrange("(c p o) -> p c o", p=P, o=1)),
                (bcol[:, :, 1:2], a["L2_gnn_b_nb"].rearrange("(c p o) -> p c o", p=P, o=1))]
        thin += [(acol[32 * g:32 * g + 32, :], a["L0_gnn_a"].rearrange("(s d) -> d s", s=2)) for g in range(4)]
        total = 16 * (len(loads) + len(thin))

        with nc.Block() as block:
            @block.sync
            def _(sp):
                for dst, src in loads:
                    sp.dma_start(dst, src).then_inc(w_in, 16)
                for dst, src in thin:
                    sp.dma_start(dst, src, allow_slow_non_contiguous=True).then_inc(w_in, 16)
                sp.wait_ge(w_in, total)

            @block.tensor
            def _(pe):
                pe.wait_ge(w_in, total)
                for b, W in enumerate((W0, Ws, Wn, S3, N3)):
                    for r in range(2):
                        for c in range(2):
                            last = nc.tensor.transpose(psum[b][:, r * D + c * P:r * D + c * P + P],
                                                       W[:, c, r * P:r * P + P], m.ident[:, :])
                    last.then_inc(w_turned, 1)
                pe.wait_ge(heads_ready, 1)
                for r in range(2):
                    for c in range(2):
                        last = nc.tensor.matmul(psum[5][:, r * 32:r * 32 + 2 * HEADS], W0[:, c, r * P:r * P + P],
                                                heads[:, c, :], start=(c == 0), stop=(c == 1))
                last.then_inc(w_turned, 1)
                pe.wait_ge(w_used, 6)
                for b, (WT, half) in enumerate(((WsT, 0), (WnT, 2))):
                    for r in range(2):
                        for c in range(2):
                            last = nc.tensor.matmul(psum[b][:, r * D:r * D + D], WT[:, c, r * P:r * P + P],
                                                    Wc[:, half + c, :], start=(c == 0), stop=(c == 1))
                    last.then_inc(w_folded, 1)
                for c in range(2):
                    for half in range(2):
                        nc.tensor.matmul(psum[2][0:1, 0:D], bcol[:, c, half:half + 1], Wc[:, 2 * half + c, :],
                                         start=(c == 0 and half == 0), stop=False)
                nc.tensor.matmul(psum[2][0:1, 0:D], m.ones[0:1, 0:1], bcomb[:, :], start=False, stop=True).then_inc(w_folded, 1)
                for c in range(2):
                    last = nc.tensor.matmul(psum[3][:, 0:D], m.ones[:, :], N3T[:, c, :], start=(c == 0), stop=(c == 1))
                last.then_inc(w_folded, 1)
                nc.tensor.matmul(psum[4][:, 0:2 * D], m.ones[0:1, :], m.norm_in[:, :], start=True, stop=True).then_inc(w_folded, 1)

            @block.vector
            def _(dve):
                nc.vector.memset(heads[:, :, :], 0.0).then_inc(w_steps, 1)
                dve.wait_ge(w_steps, 1)
                dve.wait_ge(w_in, total)
                for c in range(2):
                    for g in range(4):
                        rows, head = slice(32 * g, 32 * g + 32), 4 * c + g
                        nc.vector.tensor_copy(heads[rows, c, head:head + 1], acol[rows, 0:1])
                        last = nc.vector.tensor_copy(heads[rows, c, HEADS + head:HEADS + head + 1], acol[rows, 1:2])
                last.then_inc(heads_ready, 1)
                both = lambda t: t.rearrange("p (c n) -> p c n", c=2)
                dve.wait_ge(w_turned, 1)
                nc.vector.tensor_copy(m.W0T[:, :, 0:D], both(psum[0][:, :])).then_inc(w_used, 1)
                for b, to in ((1, WsT), (2, WnT), (3, m.S3T), (4, N3T)):
                    dve.wait_ge(w_turned, b + 1)
                    nc.vector.tensor_copy(to[:, :, :], both(psum[b][:, :])).then_inc(w_used, 1)
                dve.wait_ge(w_turned, 6)
                nc.vector.tensor_copy(m.W0T[:, :, D:D + 2 * HEADS],
                                      psum[5][:, 0:64].rearrange("p (c n) -> p c n", c=2)[:, :, 0:2 * HEADS]).then_inc(w_used, 1)
                dve.wait_ge(w_folded, 1)
                nc.vector.tensor_copy(m.W2s[:, :, :], both(psum[0][:, :]))
                dve.wait_ge(w_folded, 2)
                nc.vector.tensor_copy(m.W2n[:, :, :], both(psum[1][:, :]))
                dve.wait_ge(w_folded, 3)
                nc.vector.tensor_copy(m.bias_2[:, :], psum[2][0:1, 0:D])
                dve.wait_ge(w_folded, 4)
                nc.vector.tensor_copy(m.neigh_sum[:, :], psum[3][:, 0:D])
                dve.wait_ge(w_folded, 5)
                nc.vector.tensor_copy(m.norm[:, :], psum[4][:, 0:2 * D])


def layernorm_scale(nc, m, s, act_sem, root_ready, number):
    mv = m.mv[:, :].rearrange("p (t two) -> p t two", two=2)
    s.wait()
    nc.vector.tensor_scalar(m.var[:, :], mv[:, :, 1], EPS, None, ALU.add).then_inc(act_sem, 1)
    s.eng.wait_ge(root_ready, number)
    s.done(nc.vector.reciprocal(m.rstd[:, :], m.root[:, :]))
    s.wait()
    s.done(nc.vector.scalar_tensor_tensor(m.shift[:, :], mv[:, :, 0], -1.0, m.rstd[:, :], ALU.mult, ALU.mult))
    s.wait()


def tables(nc, m, sem, psum, x, neigh, table0, table1):
    names = ["x_in", "neigh_in", "var_ready", "root_ready", "shift_ready", "h_ready", "turned", "turned_used", "product", "tanh_ready",
             "hid_ready", "natt_ready", "row_ready", "row2_ready", "mean_ready", "summed"]
    q = {n: sem("tab_" + n) for n in names}
    row_out = [sem(f"tab_row_out{i}") for i in range(4)]
    with ExitStack() as ctx:
        def sb(name, shape):
            return ctx.enter_context(nc.sbuf_tensor(name, shape, F32))
        hb = [sb(f"hb{i}", [P, D]) for i in range(2)]
        hT = [sb(f"hT{i}", [P, 2 * P]) for i in range(2)]
        hid = [sb(f"hid{i}", [HID, P]) for i in range(2)]
        row = [sb(f"trow{i}", [P, ROW0]) for i in range(2)]
        row1 = [sb(f"trow1{i}", [P, ROW1]) for i in range(2)]
        nb = m.hbuf
        sums = sb("sums", [P, H0 + ROW1])

        with nc.Block() as block:
            @block.sync
            def _(sp):
                q4 = NT // 4
                for i in range(4):
                    sp.dma_start(m.x[:, i * q4 * D:(i + 1) * q4 * D].rearrange("p (t d) -> p t d", d=D),
                                 x[i * q4 * P:(i + 1) * q4 * P, :].rearrange("(t p) d -> p t d", p=P)).then_inc(q["x_in"], 16)
                for i in range(4):
                    sp.dma_start(nb[:, i * q4 * D:(i + 1) * q4 * D].rearrange("p (t d) -> p t d", d=D),
                                 neigh[i * q4 * P:(i + 1) * q4 * P, :].rearrange("(t p) d -> p t d", p=P)).then_inc(q["neigh_in"], 16)
                with sp.Fori(0, NT // 2) as t2:
                    for i in range(2):
                        sp.wait_ge(q["row_ready"], t2 * 2 + (i + 3))
                        sp.dma_start(table0[bass.ds((t2 * 2 + i) * P, P), :], row[i][:, :]).then_inc(row_out[i], 16)
                        sp.wait_ge(q["row2_ready"], t2 * 2 + (i + 3))
                        sp.dma_start(table1[bass.ds((t2 * 2 + i) * P, P), :], row1[i][:, :]).then_inc(row_out[2 + i], 16)
                for i in range(4):
                    sp.wait_ge(row_out[i], 8 * NT)

            @block.scalar
            def _(act):
                act.wait_ge(q["var_ready"], 1)
                nc.scalar.activation(m.root[:, :], m.var[:, :], ACT.Sqrt).then_inc(q["root_ready"], 1)
                act.wait_ge(q["shift_ready"], 1)
                act.wait_ge(q["neigh_in"], 64)
                act.sem_inc(q["turned_used"], 1)
                with act.Fori(0, NT // 2) as t2:
                    for i in range(2):
                        n = t2 * 2 + (i + 1)
                        T = t2 * 2 + i
                        act.wait_ge(q["turned_used"], (t2 * 2 + i) * 2 + 1)
                        act.sem_inc(m.tick, 1)
                        nc.scalar.activation(hb[i][:, :], tile_of(m.x, T, D), ACT.Relu, scale=m.rstd[:, bass.ds(T, 1)],
                                             bias=m.shift[:, bass.ds(T, 1)]).then_inc(q["h_ready"], 1)
                        act.wait_ge(q["turned"], n * 2 - 1)
                        nc.scalar.activation(hT[i][:, :], psum[i][:, 0:2 * P], ACT.Copy).then_inc(q["turned_used"], 1)
                        act.wait_ge(q["product"], n)
                        act.sem_inc(m.tick, 1)
                        nc.scalar.activation(hb[i][:, :], tile_of(nb, T, D), ACT.Copy).then_inc(q["h_ready"], 1)
                        act.wait_ge(q["turned"], n * 2)
                        nc.scalar.activation(hT[i][:, :], psum[i][:, 0:2 * P], ACT.Copy).then_inc(q["turned_used"], 1)
                        act.wait_ge(q["hid_ready"], n)
                        nc.scalar.activation(hid[i][:, :], psum[2 + i][0:HID, 0:P], ACT.Tanh, bias=m.bn1[:, :]).then_inc(q["tanh_ready"], 1)

            @block.tensor
            def _(pe):
                with pe.Fori(0, NT // 2) as t2:
                    for i in range(2):
                        n = t2 * 2 + (i + 1)
                        pe.wait_ge(q["h_ready"], n * 2 - 1)
                        for c in range(2):
                            last = nc.tensor.transpose(psum[i][:, c * P:c * P + P], hb[i][:, c * P:c * P + P], m.ident[:, :])
                        last.then_inc(q["turned"], 1)
                        pe.wait_ge(q["turned_used"], n * 2)
                        pe.wait_ge(q["row_ready"], n)
                        for c in range(2):
                            last = nc.tensor.matmul(psum[4 + i][:, 0:D + 2 * HEADS], hT[i][:, c * P:c * P + P], m.W0T[:, c, :],
                                                    start=(c == 0), stop=(c == 1))
                        last.then_inc(q["product"], 1)
                        pe.wait_ge(q["h_ready"], n * 2)
                        for c in range(2):
                            last = nc.tensor.transpose(psum[i][:, c * P:c * P + P], hb[i][:, c * P:c * P + P], m.ident[:, :])
                        last.then_inc(q["turned"], 1)
                        pe.wait_ge(q["turned_used"], n * 2 + 1)
                        for c in range(2):
                            last = nc.tensor.matmul(psum[2 + i][0:HID, 0:P], m.Wn1[:, c, :], hT[i][:, c * P:c * P + P],
                                                    start=(c == 0), stop=(c == 1))
                        last.then_inc(q["hid_ready"], 1)
                        pe.wait_ge(q["row2_ready"], n)
                        for c in range(2):
                            nc.tensor.matmul(psum[6 + i][:, 0:OUT1], hT[i][:, c * P:c * P + P], m.Wv[:, c, :], start=(c == 0), stop=False)
                        nc.tensor.matmul(psum[6 + i][:, 0:OUT1], m.ones[0:1, :], m.bias_n[0:1, 0:OUT1], start=False, stop=True)
                        pe.wait_ge(q["tanh_ready"], n)
                        nc.tensor.matmul(psum[6 + i][:, OUT1:OUT1 + HID], hid[i][:, :], m.Wn2[:, :], start=True, stop=False)
                        nc.tensor.matmul(psum[6 + i][:, OUT1:OUT1 + HID], m.ones[0:1, :], m.bias_n[0:1, OUT1:OUT1 + HID],
                                         start=False, stop=True).then_inc(q["natt_ready"], 1)
                pe.wait_ge(q["summed"], 2 * NT + 1)
                nc.tensor.matmul(psum[0][:, 0:H0], m.ones[:, :], sums[:, 0:H0], start=True, stop=True)
                nc.tensor.matmul(psum[1][:, 0:ROW1], m.ones[:, :], sums[:, H0:H0 + ROW1], start=True, stop=True).then_inc(q["mean_ready"], 1)

            @block.gpsimd
            def _(pool):
                nc.gpsimd.memset(sums[:, :], 0.0).then_inc(q["summed"], 1)
                with pool.Fori(0, NT // 2) as t2:
                    for i in range(2):
                        n = t2 * 2 + (i + 1)
                        pool.wait_ge(q["row_ready"], n + 2)
                        pool.wait_ge(q["summed"], n * 2 - 1)
                        pool.sem_inc(m.tick, 1)
                        nc.gpsimd.tensor_tensor(sums[:, 0:H0], sums[:, 0:H0], row[i][:, 0:H0], ALU.add).then_inc(q["summed"], 1)
                        pool.wait_ge(q["row2_ready"], n + 2)
                        pool.sem_inc(m.tick, 1)
                        nc.gpsimd.tensor_tensor(sums[:, H0:H0 + ROW1], sums[:, H0:H0 + ROW1], row1[i][:, :], ALU.add).then_inc(q["summed"], 1)

            @block.vector
            def _(dve):
                s = Steps(dve, m)
                dve.sem_inc(q["row_ready"], 2)
                dve.sem_inc(q["row2_ready"], 2)
                for i in range(2):
                    s.done(nc.vector.memset(row[i][:, :], 1.0))
                    s.done(nc.vector.memset(row1[i][:, :], 1.0))
                s.fold()
                dve.wait_ge(q["x_in"], 64)
                with dve.Fori(0, NT) as T:
                    s.wait()
                    dve.sem_inc(m.tick, 1)
                    s.done(nc.vector.bn_stats(m.stats[:, :], tile_of(m.x, T, D)))
                    s.wait()
                    dve.sem_inc(m.tick, 1)
                    s.done(nc.vector.bn_aggr(m.mv2[:, :], m.stats[:, :]))
                    s.wait()
                    s.done(nc.vector.tensor_copy(tile_of(m.mv, T, 2), m.mv2[:, :]))
                    s.fold()
                layernorm_scale(nc, m, s, q["var_ready"], q["root_ready"], 1)
                dve.sem_inc(q["shift_ready"], 1)
                s.fold()
                with dve.Fori(0, NT // 2) as t2:
                    for i in range(2):
                        n = t2 * 2 + (i + 1)
                        T = t2 * 2 + i
                        if i == 0:
                            with dve.If(t2 > 0):
                                dve.wait_ge(row_out[0], t2 * 16)
                                dve.wait_ge(row_out[1], t2 * 16)
                                dve.wait_ge(row_out[2], t2 * 16)
                                dve.wait_ge(row_out[3], t2 * 16)
                                dve.wait_ge(q["summed"], t2 * 4 + 1)
                                dve.sem_inc(m.tick, 1)
                        s.wait()
                        dve.wait_ge(q["product"], n)
                        s.done(nc.vector.tensor_copy(tile_of(m.score_i, T, HEADS), psum[4 + i][:, D + HEADS:D + 2 * HEADS]))
                        s.done(nc.vector.tensor_copy(row[i][:, H0:H0 + HEADS], psum[4 + i][:, D:D + HEADS]))
                        nc.vector.tensor_copy(row[i][:, 0:H0].rearrange("p (h d) -> p h d", h=HEADS)[:, :, 0:DH],
                                              psum[4 + i][:, 0:D].rearrange("p (h d) -> p h d", h=HEADS)).then_inc(q["row_ready"], 1)
                        dve.wait_ge(q["natt_ready"], n)
                        s.done(nc.vector.tensor_copy(row1[i][:, H1:H1 + HID], psum[6 + i][:, OUT1:OUT1 + HID]))
                        nc.vector.tensor_copy(row1[i][:, 0:OUT1], psum[6 + i][:, 0:OUT1]).then_inc(q["row2_ready"], 1)
                        s.fold()
                dve.wait_ge(q["mean_ready"], 1)
                s.done(nc.vector.tensor_scalar(m.mean0[:, :], psum[0][:, 0:H0], 1.0 / N, None, ALU.mult))
                s.done(nc.vector.tensor_scalar(m.mean1[:, :], psum[1][:, 0:ROW1], 1.0 / N, None, ALU.mult))


def grouped(t, width):
    return t[:, :].rearrange("p (u w) -> p u w", w=width)


def attend(nc, m, sem, psum, tag, edges, table, heads, width, extra, row_table, row_width, slope, running, acc):
    names = ["taken_pe", "taken_dve", "place_ready", "turned", "turned_used", "own_ready", "spread_ready", "slots_ready", "max_ready",
             "growth_ready", "top_ready", "score_ready", "weight_ready", "scaled_ready", "sum_ready", "merged", "g_clear"]
    q = {n: sem(f"{tag}_{n}") for n in names}
    rec_in = sem(f"{tag}_rec_in")
    gathered = [sem(f"{tag}_gathered{i}") for i in range(SETS)]
    hw = heads * width
    wide = hw + extra
    e1 = heads + 1
    c_slots = GROUP * row_width
    c_top = c_slots + GROUP * SLOTS * e1
    assert c_top + GROUP * heads <= 512
    with ExitStack() as ctx:
        def sb(name, shape, dt=F32):
            return [ctx.enter_context(nc.sbuf_tensor(f"{tag}_{name}{i}", shape, dt)) for i in range(SETS)]
        rec_all = ctx.enter_context(nc.sbuf_tensor(f"{tag}_rec", [P, PAD, WORDS], I32))
        rec = [rec_all[:, i * GROUP:(i + 1) * GROUP, :] for i in range(SETS)]
        G = sb("G", [P, GROUP * wide])
        GW = sb("GW", [P, GROUP * hw])
        place = sb("place", [P, GROUP * P])
        back = sb("back", [P, GROUP * P])
        slot1 = sb("slot1", [P, GROUP * SLOTS])
        z = sb("z", [P, GROUP * heads])
        zl = sb("zl", [P, GROUP * heads])
        zs = sb("zs", [P, GROUP * heads])
        wgt = sb("wgt", [P, GROUP * heads])
        spread = sb("spread", [P, GROUP * SLOTS * e1])
        absent = sb("absent", [P, GROUP * SLOTS])
        zm = sb("zm", [P, GROUP * heads * SLOTS])
        top = sb("top", [P, GROUP * heads])
        newmax = sb("newmax", [P, GROUP * heads])
        growth = sb("growth", [P, GROUP * heads])
        fade = sb("fade", [P, GROUP * heads])
        prod = sb("prod", [P, GROUP * row_width])
        bank_back = [psum[0], psum[1]]
        bank_small = [psum[2 + i] for i in range(SETS)]
        bank_sum = [psum[6], psum[7], psum[0], psum[1]]

        def tiles_of(eng, i, regs):
            for u in range(GROUP):
                eng.reg_load(regs[u], rec[i][0:1, u, W_TILE:W_TILE + 1])
            return [eng.snap(r, min_val=0, max_val=NT - 1) for r in regs]

        with nc.Block() as block:
            @block.sync
            def _(sp):
                with sp.register(f"{tag}_passes") as passes:
                    sp.reg_load(passes, m.passes[0:1, 0:1])
                    with sp.Fori(0, sp.snap(passes, min_val=1, max_val=MAX_CHUNKS // PAD)) as it:
                        sp.wait_ge(q["taken_pe"], it + 1)
                        sp.wait_ge(q["taken_dve"], it + 1)
                        sp.dma_start(rec_all[:, :, :], edges[:, bass.ds(it * PAD, PAD), :]).then_inc(rec_in, 16)

            @block.gpsimd
            def _(pool):
                with pool.register(f"{tag}_passes") as passes:
                    pool.reg_load(passes, m.passes[0:1, 0:1])
                    pool.wait_ge(q["g_clear"], SETS)
                    bound = pool.to_reg(N - 1)
                    with pool.Fori(0, pool.snap(passes, min_val=1, max_val=MAX_CHUNKS // PAD)) as it:
                        pool.wait_ge(rec_in, it * 16 + 16)
                        pool.sem_inc(m.tick, 1)
                        for i in range(SETS):
                            pool.wait_ge(q["scaled_ready"], it * SETS + (i + 1))
                            pool.sem_inc(m.tick, 1)
                            for u in range(GROUP):
                                nc.gpsimd.indirect_dma_start(
                                    G[i][:, u * wide:(u + 1) * wide], None, table[:, :],
                                    bass.IndirectOffsetOnAxis(ap=rec[i][:, u, W_J:W_J + 1].bitcast(U32), axis=0),
                                    bounds_check=N - 1, oob_is_err=False).then_inc(gathered[i], 16)

            @block.scalar
            def _(act):
                with act.register(f"{tag}_passes") as passes:
                    act.reg_load(passes, m.passes[0:1, 0:1])
                    with act.Fori(0, act.snap(passes, min_val=1, max_val=MAX_CHUNKS // PAD)) as it:
                        for i in range(SETS):
                            act.wait_ge(q["turned"], it * SETS + (i + 1))
                            nc.scalar.activation(back[i][:, :], bank_back[i % 2][:, :], ACT.Copy).then_inc(q["turned_used"], 1)
                        for i in range(SETS):
                            act.wait_ge(q["max_ready"], it * SETS + (i + 1))
                            nc.scalar.activation(fade[i][:, :], growth[i][:, :], ACT.Exp).then_inc(q["growth_ready"], 1)
                        for i in range(SETS):
                            act.wait_ge(q["score_ready"], it * SETS + (i + 1))
                            nc.scalar.activation(wgt[i][:, :], zs[i][:, :], ACT.Exp).then_inc(q["weight_ready"], 1)

            @block.tensor
            def _(pe):
                with ExitStack() as rc:
                    passes = rc.enter_context(pe.register(f"{tag}_passes"))
                    regs = [[rc.enter_context(pe.register(f"{tag}_tile{i}{u}")) for u in range(GROUP)] for i in range(SETS)]
                    pe.reg_load(passes, m.passes[0:1, 0:1])
                    with pe.Fori(0, pe.snap(passes, min_val=1, max_val=MAX_CHUNKS // PAD)) as it:
                        tiles = []
                        pe.wait_ge(rec_in, it * 16 + 16)
                        pe.sem_inc(m.tick, 1)
                        for i in range(SETS):
                            tiles.append(tiles_of(pe, i, regs[i]))
                        pe.sem_inc(q["taken_pe"], 1)
                        for i in range(SETS):
                            if i >= 2:
                                pe.wait_ge(q["turned_used"], it * SETS + (i - 1))
                            pe.wait_ge(q["place_ready"], it * SETS + (i + 1))
                            for u in range(GROUP):
                                last = nc.tensor.transpose(bank_back[i % 2][:, u * P:(u + 1) * P], place[i][:, u * P:(u + 1) * P], m.ident[:, :])
                            last.then_inc(q["turned"], 1)
                        for i in range(SETS):
                            pe.wait_ge(q["turned_used"], it * SETS + (i + 1))
                            for u in range(GROUP):
                                last = nc.tensor.matmul(bank_small[i][:, u * row_width:(u + 1) * row_width],
                                                        back[i][:, u * P:(u + 1) * P], tile_of(row_table, tiles[i][u], row_width),
                                                        start=True, stop=True)
                            last.then_inc(q["own_ready"], 1)
                        for i in range(SETS):
                            pe.wait_ge(q["spread_ready"], it * SETS + (i + 1))
                            for u in range(GROUP):
                                last = nc.tensor.matmul(bank_small[i][:, c_slots + u * SLOTS * e1:c_slots + (u + 1) * SLOTS * e1],
                                                        place[i][:, u * P:(u + 1) * P],
                                                        spread[i][:, u * SLOTS * e1:(u + 1) * SLOTS * e1], start=True, stop=True)
                            last.then_inc(q["slots_ready"], 1)
                        for i in range(SETS):
                            pe.wait_ge(q["max_ready"], it * SETS + (i + 1))
                            for u in range(GROUP):
                                last = nc.tensor.matmul(bank_small[i][:, c_top + u * heads:c_top + (u + 1) * heads],
                                                        back[i][:, u * P:(u + 1) * P], newmax[i][:, u * heads:(u + 1) * heads],
                                                        start=True, stop=True)
                            last.then_inc(q["top_ready"], 1)
                        for i in range(SETS):
                            pe.wait_ge(q["scaled_ready"], it * SETS + (i + 1 + SETS))
                            for u in range(GROUP):
                                pe.wait_ge(q["merged"], it * PAD + (i * GROUP + u + 1))
                                nc.tensor.matmul(bank_sum[u][:, 0:hw], place[i][:, u * P:(u + 1) * P],
                                                 GW[i][:, u * hw:(u + 1) * hw], start=True, stop=True).then_inc(q["sum_ready"], 1)

            @block.vector
            def _(dve):
                with ExitStack() as rc:
                    passes = rc.enter_context(dve.register(f"{tag}_passes"))
                    regs = [[rc.enter_context(dve.register(f"{tag}_tile{i}{u}")) for u in range(GROUP)] for i in range(SETS)]
                    s = Steps(dve, m)
                    dve.reg_load(passes, m.passes[0:1, 0:1])
                    for i in range(SETS):
                        nc.vector.memset(G[i][:, :], 0.0).then_inc(q["g_clear"], 1)
                    s.done(nc.vector.memset(running[:, :], -NEVER))
                    s.done(nc.vector.memset(acc[:, :], 0.0))
                    dve.sem_inc(q["scaled_ready"], SETS)
                    dve.sem_inc(q["merged"], GROUP)
                    dve.sem_inc(q["taken_dve"], 1)
                    dve.sem_inc(q["taken_pe"], 1)
                    s.fold()
                    with dve.Fori(0, dve.snap(passes, min_val=1, max_val=MAX_CHUNKS // PAD)) as it:
                        tiles = []
                        dve.wait_ge(rec_in, it * 16 + 16)
                        dve.sem_inc(m.tick, 1)
                        for i in range(SETS):
                            half = rec[i].bitcast(BF16)
                            s.wait()
                            nc.vector.tensor_tensor(grouped(place[i], P), m.iota_row[:, None, :].broadcast_to([P, GROUP, P]),
                                                    half[:, :, H_ROW:H_ROW + 1].broadcast_to([P, GROUP, P]),
                                                    ALU.is_equal).then_inc(q["place_ready"], 1)
                            s.done(nc.vector.tensor_tensor(grouped(slot1[i], SLOTS), m.iota_row[:, None, 0:SLOTS].broadcast_to([P, GROUP, SLOTS]),
                                                           half[:, :, H_SLOT:H_SLOT + 1].broadcast_to([P, GROUP, SLOTS]), ALU.is_equal))
                        for i in range(SETS):
                            tiles.append(tiles_of(dve, i, regs[i]))
                        for i in range(SETS):
                            g3 = grouped(G[i], wide)
                            dve.wait_ge(gathered[i], it * (16 * GROUP) + 16 * GROUP)
                            dve.wait_ge(q["own_ready"], it * SETS + (i + 1))
                            own = bank_small[i][:, 0:GROUP * row_width].rearrange("p (u w) -> p u w", w=row_width)
                            if row_width == heads:
                                s.wait()
                                s.done(nc.vector.tensor_tensor(grouped(z[i], heads), own, g3[:, :, hw:hw + heads], ALU.add))
                            else:
                                s.wait()
                                s.done(nc.vector.tensor_tensor(grouped(prod[i], row_width), own, g3[:, :, hw:hw + row_width], ALU.mult))
                                s.wait()
                                s.done(nc.vector.tensor_reduce(z[i][:, :], grouped(prod[i], row_width), AX.X, ALU.add))
                            s.wait()
                            s.done(nc.vector.scalar_tensor_tensor(zl[i][:, :], z[i][:, :], slope, z[i][:, :], ALU.mult, ALU.max))
                            sp4 = spread[i][:, :].rearrange("p (u k e) -> p u k e", u=GROUP, e=e1)
                            hot = slot1[i][:, :].rearrange("p (u k o) -> p u k o", u=GROUP, o=1)
                            s.done(nc.vector.tensor_copy(sp4[:, :, :, heads:heads + 1], hot))
                            s.wait()
                            nc.vector.tensor_tensor(sp4[:, :, :, 0:heads], zl[i][:, :].rearrange("p (u o h) -> p u o h", u=GROUP, o=1)
                                                    .broadcast_to([P, GROUP, SLOTS, heads]),
                                                    hot.broadcast_to([P, GROUP, SLOTS, heads]), ALU.mult).then_inc(q["spread_ready"], 1)
                        dve.wait_ge(q["spread_ready"], it * SETS + SETS)
                        dve.sem_inc(q["taken_dve"], 1)
                        for i in range(SETS):
                            dve.wait_ge(q["slots_ready"], it * SETS + (i + 1))
                            el = bank_small[i][:, c_slots:c_top].rearrange("p (u k e) -> p u k e", u=GROUP, e=e1)
                            s.done(nc.vector.tensor_scalar(absent[i][:, :].rearrange("p (u k o) -> p u k o", u=GROUP, o=1),
                                                           el[:, :, :, heads:heads + 1], 1.0, NEVER, ALU.subtract, ALU.mult))
                            s.wait()
                            s.done(nc.vector.tensor_tensor(zm[i][:, :].rearrange("p (u h k) -> p u h k", u=GROUP, k=SLOTS),
                                                           el[:, :, :, 0:heads].rearrange("p u k h -> p u h k"),
                                                           absent[i][:, :].rearrange("p (u o k) -> p u o k", u=GROUP, o=1)
                                                           .broadcast_to([P, GROUP, heads, SLOTS]), ALU.add))
                            s.wait()
                            s.done(nc.vector.tensor_reduce(top[i][:, :], zm[i][:, :].rearrange("p (a k) -> p a k", k=SLOTS), AX.X, ALU.max))
                            for u in range(GROUP):
                                cols = slice(u * heads, (u + 1) * heads)
                                mine = tile_of(running, tiles[i][u], heads)
                                s.wait()
                                s.done(nc.vector.tensor_tensor(newmax[i][:, cols], mine, top[i][:, cols], ALU.max))
                                s.wait()
                                s.done(nc.vector.tensor_tensor(growth[i][:, cols], mine, newmax[i][:, cols], ALU.subtract))
                                s.wait()
                                ins = nc.vector.tensor_scalar(mine, newmax[i][:, cols], 0.0, None, ALU.add)
                                if u < GROUP - 1:
                                    s.done(ins)
                                else:
                                    ins.then_inc(q["max_ready"], 1)
                            dve.wait_ge(q["max_ready"], it * SETS + (i + 1))
                        for i in range(SETS):
                            dve.wait_ge(q["top_ready"], it * SETS + (i + 1))
                            s.done(nc.vector.tensor_tensor(z[i][:, :], zl[i][:, :], bank_small[i][:, c_top:c_top + GROUP * heads], ALU.subtract))
                            s.wait()
                            nc.vector.tensor_scalar(zs[i][:, :], z[i][:, :], 0.0, None, ALU.min).then_inc(q["score_ready"], 1)
                        for i in range(SETS):
                            dve.wait_ge(q["weight_ready"], it * SETS + (i + 1))
                            g3 = grouped(G[i], wide)
                            if heads == 1:
                                src = g3[:, :, 0:hw]
                                dst = grouped(GW[i], hw)
                                w = wgt[i][:, :].rearrange("p (u o) -> p u o", o=1).broadcast_to([P, GROUP, hw])
                            else:
                                src = g3[:, :, 0:hw].rearrange("p u (h d) -> p u h d", h=heads)
                                dst = GW[i][:, :].rearrange("p (u h d) -> p u h d", u=GROUP, h=heads)
                                w = wgt[i][:, :].rearrange("p (u h o) -> p u h o", u=GROUP, o=1).broadcast_to([P, GROUP, heads, width])
                            nc.vector.tensor_tensor(dst, src, w, ALU.mult).then_inc(q["scaled_ready"], 1)
                        for i in range(SETS):
                            dve.wait_ge(q["growth_ready"], it * SETS + (i + 1))
                            for u in range(GROUP):
                                mine = tile_of(acc, tiles[i][u], hw)
                                dve.wait_ge(q["merged"], it * PAD + (i * GROUP + u + GROUP))
                                if heads == 1:
                                    dve.wait_ge(q["sum_ready"], it * PAD + (i * GROUP + u + 1))
                                    ins = nc.vector.scalar_tensor_tensor(mine, mine, fade[i][:, u:u + 1], bank_sum[u][:, 0:hw], ALU.mult, ALU.add)
                                else:
                                    m3 = mine.rearrange("p (h d) -> p h d", h=heads)
                                    f = fade[i][:, u * heads:(u + 1) * heads].rearrange("p (h o) -> p h o", o=1).broadcast_to([P, heads, width])
                                    s.done(nc.vector.tensor_tensor(m3, m3, f, ALU.mult))
                                    dve.wait_ge(q["sum_ready"], it * PAD + (i * GROUP + u + 1))
                                    s.wait()
                                    ins = nc.vector.tensor_tensor(mine, mine, bank_sum[u][:, 0:hw], ALU.add)
                                ins.then_inc(q["merged"], 1)
                        dve.wait_ge(q["merged"], it * PAD + (PAD + GROUP))
                        dve.sem_inc(m.tick, 1)
                        s.fold()


def gather_sum(nc, m, sem, psum, tag, edges, table, width, acc):
    q = {n: sem(f"{tag}_{n}") for n in ["taken", "place_ready", "sum_ready", "merged", "g_clear"]}
    rec_in = sem(f"{tag}_rec_in")
    gathered = [sem(f"{tag}_gathered{i}") for i in range(SETS)]
    with ExitStack() as ctx:
        def sb(name, shape, dt=F32):
            return [ctx.enter_context(nc.sbuf_tensor(f"{tag}_{name}{i}", shape, dt)) for i in range(SETS)]
        rec_all = ctx.enter_context(nc.sbuf_tensor(f"{tag}_rec", [P, PAD, WORDS], I32))
        rec = [rec_all[:, i * GROUP:(i + 1) * GROUP, :] for i in range(SETS)]
        G = sb("G", [P, GROUP * width])
        place = sb("place", [P, GROUP * P])

        def bank(i, u):
            return psum[i % 2 * GROUP + u][:, 0:width]

        with nc.Block() as block:
            @block.sync
            def _(sp):
                with sp.register(f"{tag}_passes") as passes:
                    sp.reg_load(passes, m.passes[0:1, 0:1])
                    with sp.Fori(0, sp.snap(passes, min_val=1, max_val=MAX_CHUNKS // PAD)) as it:
                        sp.wait_ge(q["taken"], it + 1)
                        sp.wait_ge(q["sum_ready"], it * SETS + SETS)
                        sp.dma_start(rec_all[:, :, :], edges[:, bass.ds(it * PAD, PAD), :]).then_inc(rec_in, 16)

            @block.gpsimd
            def _(pool):
                with pool.register(f"{tag}_passes") as passes:
                    pool.reg_load(passes, m.passes[0:1, 0:1])
                    pool.wait_ge(q["g_clear"], SETS)
                    with pool.Fori(0, pool.snap(passes, min_val=1, max_val=MAX_CHUNKS // PAD)) as it:
                        pool.wait_ge(rec_in, it * 16 + 16)
                        pool.sem_inc(m.tick, 1)
                        for i in range(SETS):
                            pool.wait_ge(q["sum_ready"], it * SETS + (i + 1))
                            pool.sem_inc(m.tick, 1)
                            for u in range(GROUP):
                                nc.gpsimd.indirect_dma_start(
                                    G[i][:, u * width:(u + 1) * width], None, table[:, :],
                                    bass.IndirectOffsetOnAxis(ap=rec[i][:, u, W_J:W_J + 1].bitcast(U32), axis=0),
                                    bounds_check=N - 1, oob_is_err=False).then_inc(gathered[i], 16)

            @block.tensor
            def _(pe):
                with pe.register(f"{tag}_passes") as passes:
                    pe.reg_load(passes, m.passes[0:1, 0:1])
                    pe.sem_inc(q["sum_ready"], SETS)
                    with pe.Fori(0, pe.snap(passes, min_val=1, max_val=MAX_CHUNKS // PAD)) as it:
                        for i in range(SETS):
                            pe.wait_ge(q["place_ready"], it * SETS + (i + 1))
                            pe.wait_ge(gathered[i], it * (16 * GROUP) + 16 * GROUP)
                            pe.wait_ge(q["merged"], it * SETS + (i + 1))
                            for u in range(GROUP):
                                last = nc.tensor.matmul(bank(i, u), place[i][:, u * P:(u + 1) * P],
                                                        G[i][:, u * width:(u + 1) * width], start=True, stop=True)
                            last.then_inc(q["sum_ready"], 1)

            @block.vector
            def _(dve):
                with ExitStack() as rc:
                    passes = rc.enter_context(dve.register(f"{tag}_passes"))
                    regs = [[rc.enter_context(dve.register(f"{tag}_tile{i}{u}")) for u in range(GROUP)] for i in range(SETS)]
                    s = Steps(dve, m)
                    dve.reg_load(passes, m.passes[0:1, 0:1])
                    for i in range(SETS):
                        nc.vector.memset(G[i][:, :], 0.0).then_inc(q["g_clear"], 1)
                    s.done(nc.vector.memset(acc[:, :], 0.0))
                    dve.sem_inc(q["merged"], 2)
                    dve.sem_inc(q["taken"], 1)
                    s.fold()
                    with dve.Fori(0, dve.snap(passes, min_val=1, max_val=MAX_CHUNKS // PAD)) as it:
                        tiles = []
                        dve.wait_ge(rec_in, it * 16 + 16)
                        dve.sem_inc(m.tick, 1)
                        for i in range(SETS):
                            for u in range(GROUP):
                                dve.reg_load(regs[i][u], rec[i][0:1, u, W_TILE:W_TILE + 1])
                            tiles.append([dve.snap(r, min_val=0, max_val=NT - 1) for r in regs[i]])
                            half = rec[i].bitcast(BF16)
                            s.wait()
                            nc.vector.tensor_tensor(grouped(place[i], P), m.iota_row[:, None, :].broadcast_to([P, GROUP, P]),
                                                    half[:, :, H_ROW:H_ROW + 1].broadcast_to([P, GROUP, P]),
                                                    ALU.is_equal).then_inc(q["place_ready"], 1)
                        dve.wait_ge(q["place_ready"], it * SETS + SETS)
                        dve.sem_inc(q["taken"], 1)
                        for i in range(SETS):
                            s.wait()
                            dve.wait_ge(q["sum_ready"], it * SETS + (i + 1 + SETS))
                            for u in range(GROUP):
                                mine = tile_of(acc, tiles[i][u], width)
                                if u:
                                    s.wait()
                                ins = nc.vector.tensor_tensor(mine, mine, bank(i, u), ALU.add)
                                if u < GROUP - 1:
                                    s.done(ins)
                                else:
                                    ins.then_inc(q["merged"], 1)
                            dve.wait_ge(q["merged"], it * SETS + (i + 1 + 2))
                        s.fold()


def tile_stats(nc, m, s, T):
    s.wait()
    s.eng.sem_inc(m.tick, 1)
    s.done(nc.vector.bn_stats(m.stats[:, :], tile_of(m.x, T, D)))
    s.wait()
    s.eng.sem_inc(m.tick, 1)
    s.done(nc.vector.bn_aggr(m.mv2[:, :], m.stats[:, :]))
    s.wait()
    s.done(nc.vector.tensor_copy(tile_of(m.mv, T, 2), m.mv2[:, :]))


def column_sums(nc, pe, out, ones, ready, offset, tile, done):
    pe.wait_ge(ready, offset + 1)
    nc.tensor.matmul(out, ones, tile(0), start=True, stop=False)
    with pe.Fori(1, NT - 1) as T:
        pe.wait_ge(ready, T + (offset + 1))
        nc.tensor.matmul(out, ones, tile(T), start=False, stop=False)
    pe.wait_ge(ready, offset + NT)
    nc.tensor.matmul(out, ones, tile(NT - 1), start=False, stop=True).then_inc(done, 1)


def after0(nc, m, sem, psum, acc):
    names = ["out_ready", "sum_ready", "centred", "squared", "square_ready", "var_ready", "root_ready", "scaled", "scaled_used", "norm_ready",
             "shift_ready", "h_ready", "turned", "turned_used", "hid_ready", "tanh_ready", "product", "product_used"]
    q = {n: sem("a0_" + n) for n in names}
    with ExitStack() as ctx:
        def sb(name, shape):
            return ctx.enter_context(nc.sbuf_tensor("a0_" + name, shape, F32))
        hb = [sb(f"hb{i}", [P, D]) for i in range(2)]
        hT = [sb(f"hT{i}", [P, 2 * P]) for i in range(2)]
        hid = [sb(f"hid{i}", [HID, P]) for i in range(2)]
        sq = [sb(f"sq{i}", [P, D]) for i in range(2)]
        bn = [sb(f"bn{i}", [P, D]) for i in range(2)]
        den = sb("den", [P, NT * HEADS])
        rden = sb("rden", [P, NT * HEADS])
        mean = sb("mean", [P, D])
        var = sb("var", [P, D])
        root = sb("root", [P, D])
        gain = sb("gain", [P, D])
        acc4 = acc[:, :].rearrange("p (t h d) -> p t h d", t=NT, h=HEADS)
        acc3 = acc[:, :].rearrange("p (a d) -> p a d", d=DH + 1)

        with nc.Block() as block:
            @block.tensor
            def _(pe):
                column_sums(nc, pe, psum[0][:, 0:D], m.ones[:, :], q["out_ready"], 0, lambda T: tile_of(m.hbuf, T, D), q["sum_ready"])
                with pe.Fori(0, NT // 2) as t2:
                    for i in range(2):
                        pe.wait_ge(q["squared"], t2 * 2 + (i + 3))
                        nc.tensor.matmul(psum[1][:, 0:D], m.ones[:, :], sq[i][:, :], start=True, stop=True).then_inc(q["square_ready"], 1)
                        pe.wait_ge(q["norm_ready"], t2 * 2 + (i + 1))
                with pe.Fori(0, NT // 2) as t2:
                    for i in range(2):
                        n = t2 * 2 + (i + 1)
                        pe.wait_ge(q["h_ready"], n)
                        for c in range(2):
                            last = nc.tensor.transpose(psum[i][:, c * P:c * P + P], hb[i][:, c * P:c * P + P], m.ident[:, :])
                        last.then_inc(q["turned"], 1)
                        pe.wait_ge(q["turned_used"], n)
                        for c in range(2):
                            last = nc.tensor.matmul(psum[2 + i][0:HID, 0:P], m.Wx1[:, c, :], hT[i][:, c * P:c * P + P],
                                                    start=(c == 0), stop=(c == 1))
                        last.then_inc(q["hid_ready"], 1)
                        pe.wait_ge(q["product_used"], n)
                        for c in range(2):
                            nc.tensor.matmul(psum[4 + i][:, HID:HID + OUT1], hT[i][:, c * P:c * P + P], m.Wfx[:, c, :], start=(c == 0), stop=False)
                        nc.tensor.matmul(psum[4 + i][:, HID:HID + OUT1], m.ones[0:1, :], m.bias_x[0:1, HID:HID + OUT1], start=False, stop=True)
                        pe.wait_ge(q["tanh_ready"], n)
                        nc.tensor.matmul(psum[4 + i][:, 0:HID], hid[i][:, :], m.Wx2[:, :], start=True, stop=False)
                        nc.tensor.matmul(psum[4 + i][:, 0:HID], m.ones[0:1, :], m.bias_x[0:1, 0:HID],
                                         start=False, stop=True).then_inc(q["product"], 1)

            @block.scalar
            def _(act):
                act.sem_inc(q["squared"], 2)
                with act.Fori(0, NT // 2) as t2:
                    for i in range(2):
                        act.wait_ge(q["centred"], t2 * 2 + (i + 1))
                        act.sem_inc(m.tick, 1)
                        nc.scalar.activation(sq[i][:, :], tile_of(m.hbuf, t2 * 2 + i, D), ACT.Square).then_inc(q["squared"], 1)
                        act.wait_ge(q["norm_ready"], t2 * 2 + (i + 1))
                        act.sem_inc(m.tick, 1)
                act.wait_ge(q["var_ready"], 1)
                nc.scalar.activation(root[:, :], var[:, :], ACT.Sqrt).then_inc(q["root_ready"], 1)
                act.wait_ge(q["var_ready"], 2)
                nc.scalar.activation(m.root[:, :], m.var[:, :], ACT.Sqrt).then_inc(q["root_ready"], 1)
                act.wait_ge(q["shift_ready"], 1)
                with act.Fori(0, NT // 2) as t2:
                    for i in range(2):
                        n = t2 * 2 + (i + 1)
                        T = t2 * 2 + i
                        act.sem_inc(m.tick, 1)
                        nc.scalar.activation(hb[i][:, :], tile_of(m.x, T, D), ACT.Relu, scale=m.rstd[:, bass.ds(T, 1)],
                                             bias=m.shift[:, bass.ds(T, 1)]).then_inc(q["h_ready"], 1)
                        act.wait_ge(q["turned"], n)
                        nc.scalar.activation(hT[i][:, :], psum[i][:, 0:2 * P], ACT.Copy).then_inc(q["turned_used"], 1)
                        act.wait_ge(q["hid_ready"], n)
                        nc.scalar.activation(hid[i][:, :], psum[2 + i][0:HID, 0:P], ACT.Tanh, bias=m.bx1[:, :]).then_inc(q["tanh_ready"], 1)

            @block.gpsimd
            def _(pool):
                pool.wait_ge(q["scaled_used"], 1)
                with pool.Fori(0, NT // 2) as t2:
                    for i in range(2):
                        pool.wait_ge(q["scaled_used"], t2 * 2 + (i + 1))
                        pool.sem_inc(m.tick, 1)
                        nc.gpsimd.tensor_tensor(bn[i][:, :], tile_of(m.hbuf, t2 * 2 + i, D), gain[:, :], ALU.mult).then_inc(q["scaled"], 1)

            @block.vector
            def _(dve):
                s = Steps(dve, m)
                s.done(nc.vector.tensor_scalar(m.empty[:, :], m.degree[:, :], 0.0, None, ALU.is_equal))
                s.wait()
                s.done(nc.vector.tensor_tensor(den[:, :].rearrange("p (t h o) -> p t h o", t=NT, o=1), acc4[:, :, :, DH:DH + 1],
                                               m.empty[:, :].rearrange("p (t h o) -> p t h o", h=1, o=1).broadcast_to([P, NT, HEADS, 1]), ALU.add))
                s.wait()
                s.done(nc.vector.reciprocal(rden[:, :], den[:, :]))
                s.wait()
                s.done(nc.vector.tensor_tensor(m.hbuf[:, :].rearrange("p (a d) -> p a d", d=DH), acc3[:, :, 0:DH],
                                               rden[:, :].rearrange("p (a o) -> p a o", o=1).broadcast_to([P, NT * HEADS, DH]), ALU.mult))
                s.fold()
                with dve.Fori(0, NT) as T:
                    mine = tile_of(m.hbuf, T, D).rearrange("p (h d) -> p h d", h=HEADS)
                    s.wait()
                    nc.vector.scalar_tensor_tensor(mine, m.mean0[:, :].rearrange("p (h d) -> p h d", h=HEADS)[:, :, 0:DH],
                                                   m.empty[:, bass.ds(T, 1)], mine, ALU.mult, ALU.add).then_inc(q["out_ready"], 1)
                dve.wait_ge(q["sum_ready"], 1)
                s.done(nc.vector.tensor_scalar(mean[:, :], psum[0][:, 0:D], 1.0 / N, None, ALU.mult))
                s.done(nc.vector.memset(var[:, :], 0.0))
                s.fold()
                with dve.Fori(0, NT // 2) as t2:
                    for i in range(2):
                        n = t2 * 2 + (i + 1)
                        s.wait()
                        mine = tile_of(m.hbuf, t2 * 2 + i, D)
                        nc.vector.tensor_tensor(mine, mine, mean[:, :], ALU.subtract).then_inc(q["centred"], 1)
                        dve.wait_ge(q["square_ready"], n)
                        nc.vector.tensor_tensor(var[:, :], var[:, :], psum[1][:, 0:D], ALU.add).then_inc(q["norm_ready"], 1)
                        dve.wait_ge(q["norm_ready"], n)
                        dve.sem_inc(m.tick, 1)
                s.done(nc.vector.tensor_scalar(var[:, :], var[:, :], 1.0 / N, EPS, ALU.mult, ALU.add))
                s.wait()
                dve.sem_inc(q["var_ready"], 1)
                dve.wait_ge(q["root_ready"], 1)
                s.done(nc.vector.reciprocal(mean[:, :], root[:, :]))
                s.wait()
                s.done(nc.vector.tensor_tensor(gain[:, :], mean[:, :], m.norm[:, 0:D], ALU.mult))
                s.wait()
                dve.sem_inc(q["scaled_used"], 2)
                s.fold()
                with dve.Fori(0, NT // 2) as t2:
                    for i in range(2):
                        n = t2 * 2 + (i + 1)
                        T = t2 * 2 + i
                        mine = tile_of(m.x, T, D)
                        s.wait()
                        dve.wait_ge(q["scaled"], n)
                        s.done(nc.vector.tensor_tensor(bn[i][:, :], bn[i][:, :], m.norm[:, D:2 * D], ALU.add))
                        s.wait()
                        nc.vector.scalar_tensor_tensor(mine, bn[i][:, :], 0.0, mine, ALU.max, ALU.add).then_inc(q["scaled_used"], 1)
                        dve.wait_ge(q["scaled_used"], n + 2)
                        dve.sem_inc(m.tick, 1)
                        tile_stats(nc, m, s, T)
                        s.fold()
                layernorm_scale(nc, m, s, q["var_ready"], q["root_ready"], 2)
                dve.sem_inc(q["shift_ready"], 1)
                dve.sem_inc(q["product_used"], 2)
                s.fold()
                with dve.Fori(0, NT // 2) as t2:
                    for i in range(2):
                        T = t2 * 2 + i
                        s.wait()
                        dve.wait_ge(q["product"], t2 * 2 + (i + 1))
                        s.done(nc.vector.tensor_copy(tile_of(m.row1, T, HID), psum[4 + i][:, 0:HID]))
                        mine = m.x[:, bass.ds(T * D, OUT1)]
                        nc.vector.tensor_tensor(mine, mine, psum[4 + i][:, HID:HID + OUT1], ALU.add).then_inc(q["product_used"], 1)
                        s.fold()


def after1(nc, m, sem, acc, table2):
    q = {n: sem("a1_" + n) for n in ["var_ready", "root_ready", "shift_ready", "h_ready", "stored"]}
    with ExitStack() as ctx:
        den = ctx.enter_context(nc.sbuf_tensor("a1_den", [P, NT], F32))
        rden = ctx.enter_context(nc.sbuf_tensor("a1_rden", [P, NT], F32))
        parts = 4
        each = NT // parts
        with nc.Block() as block:
            @block.scalar
            def _(act):
                act.wait_ge(q["var_ready"], 1)
                nc.scalar.activation(m.root[:, :], m.var[:, :], ACT.Sqrt).then_inc(q["root_ready"], 1)
                act.wait_ge(q["shift_ready"], 1)
                with act.Fori(0, NT) as T:
                    act.sem_inc(m.tick, 1)
                    nc.scalar.activation(tile_of(m.hbuf, T, D), tile_of(m.x, T, D), ACT.Relu, scale=m.rstd[:, bass.ds(T, 1)],
                                         bias=m.shift[:, bass.ds(T, 1)]).then_inc(q["h_ready"], 1)

            @block.sync
            def _(sp):
                for i in range(parts):
                    sp.wait_ge(q["h_ready"], (i + 1) * each)
                    sp.dma_start(table2[i * each * P:(i + 1) * each * P, :].rearrange("(t p) d -> p t d", p=P),
                                 m.hbuf[:, i * each * D:(i + 1) * each * D].rearrange("p (t d) -> p t d", d=D)).then_inc(q["stored"], 16)
                sp.wait_ge(q["stored"], 16 * parts)

            @block.vector
            def _(dve):
                s = Steps(dve, m)
                acc3 = acc[:, :].rearrange("p (t w) -> p t w", w=H1)
                s.done(nc.vector.tensor_tensor(den[:, :].rearrange("p (t o) -> p t o", o=1), acc3[:, :, OUT1:H1],
                                               m.empty[:, :].rearrange("p (t o) -> p t o", o=1), ALU.add))
                s.wait()
                s.done(nc.vector.reciprocal(rden[:, :], den[:, :]))
                s.fold()
                with dve.Fori(0, NT) as T:
                    mine = m.x[:, bass.ds(T * D + OUT1, OUT1)]
                    s.wait()
                    s.done(nc.vector.scalar_tensor_tensor(mine, acc[:, bass.ds(T * H1, OUT1)], rden[:, bass.ds(T, 1)], mine, ALU.mult, ALU.add))
                    s.wait()
                    s.done(nc.vector.scalar_tensor_tensor(mine, m.mean1[:, 0:OUT1], m.empty[:, bass.ds(T, 1)], mine, ALU.mult, ALU.add))
                    tile_stats(nc, m, s, T)
                    s.fold()
                layernorm_scale(nc, m, s, q["var_ready"], q["root_ready"], 1)
                dve.sem_inc(q["shift_ready"], 1)


def after2(nc, m, sem, psum, acc, table3):
    names = ["mean_ready", "pair_ready", "turned", "turned_used", "product", "product_used", "var_ready", "root_ready", "shift_ready", "h_ready",
             "turned3", "turned3_used", "product3", "product3_used", "column", "column_turned", "column_ready", "stored"]
    q = {n: sem("a2_" + n) for n in names}
    with ExitStack() as ctx:
        def sb(name, shape):
            return ctx.enter_context(nc.sbuf_tensor("a2_" + name, shape, F32))
        pair = [sb(f"pair{i}", [P, 2 * D]) for i in range(2)]
        pairT = [sb(f"pairT{i}", [P, 2 * D]) for i in range(2)]
        rdeg = sb("rdeg", [P, NT])
        deg1 = sb("deg1", [P, NT])
        col = sb("col", [P, NT])
        colT = sb("colT", [NT, P])
        with nc.Block() as block:
            @block.sync
            def _(sp):
                sp.wait_ge(q["column_ready"], 1)
                sp.dma_start(table3.rearrange("(t p) o -> t (p o)", p=P), colT[:, :]).then_inc(q["stored"], 16)
                sp.wait_ge(q["stored"], 16)

            @block.scalar
            def _(act):
                act.wait_ge(q["mean_ready"], 1)
                act.sem_inc(q["pair_ready"], 2)
                with act.Fori(0, NT // 2) as t2:
                    for i in range(2):
                        n = t2 * 2 + (i + 1)
                        T = t2 * 2 + i
                        act.wait_ge(q["turned_used"], n)
                        act.sem_inc(m.tick, 1)
                        nc.scalar.activation(pair[i][:, 0:D], tile_of(m.hbuf, T, D), ACT.Copy)
                        nc.scalar.activation(pair[i][:, D:2 * D], tile_of(acc, T, D), ACT.Copy, scale=rdeg[:, bass.ds(T, 1)]).then_inc(q["pair_ready"], 1)
                act.wait_ge(q["var_ready"], 1)
                nc.scalar.activation(m.root[:, :], m.var[:, :], ACT.Sqrt).then_inc(q["root_ready"], 1)
                act.wait_ge(q["shift_ready"], 1)
                with act.Fori(0, NT // 2) as t2:
                    for i in range(2):
                        n = t2 * 2 + (i + 1)
                        T = t2 * 2 + i
                        act.wait_ge(q["column"], n)
                        act.sem_inc(m.tick, 1)
                        nc.scalar.activation(pair[i][:, 0:D], tile_of(m.x, T, D), ACT.Relu, scale=m.rstd[:, bass.ds(T, 1)],
                                             bias=m.shift[:, bass.ds(T, 1)]).then_inc(q["h_ready"], 1)
                        act.wait_ge(q["turned3"], n)
                        nc.scalar.activation(pairT[i][:, 0:D], psum[i][:, 0:D], ACT.Copy).then_inc(q["turned3_used"], 1)

            @block.tensor
            def _(pe):
                with pe.Fori(0, NT // 2) as t2:
                    for i in range(2):
                        n = t2 * 2 + (i + 1)
                        pe.wait_ge(q["pair_ready"], n + 2)
                        for c in range(4):
                            last = nc.tensor.transpose(psum[i][:, c * P:c * P + P], pair[i][:, c * P:c * P + P], m.ident[:, :])
                        last.then_inc(q["turned"], 1)
                        pe.wait_ge(q["turned_used"], n + 2)
                        pe.wait_ge(q["product_used"], n)
                        for c in range(4):
                            w = (m.W2s, m.W2n)[c // 2][:, c % 2, :]
                            nc.tensor.matmul(psum[2 + i][:, 0:D], pairT[i][:, c * P:c * P + P], w, start=(c == 0), stop=False)
                        nc.tensor.matmul(psum[2 + i][:, 0:D], m.ones[0:1, :], m.bias_2[:, :], start=False, stop=True).then_inc(q["product"], 1)
                with pe.Fori(0, NT // 2) as t2:
                    for i in range(2):
                        n = t2 * 2 + (i + 1)
                        pe.wait_ge(q["h_ready"], n)
                        for c in range(2):
                            last = nc.tensor.transpose(psum[i][:, c * P:c * P + P], pair[i][:, c * P:c * P + P], m.ident[:, :])
                        last.then_inc(q["turned3"], 1)
                        pe.wait_ge(q["turned3_used"], n)
                        pe.wait_ge(q["product3_used"], n)
                        for c in range(2):
                            last = nc.tensor.matmul(psum[2 + i][:, 0:D], pairT[i][:, c * P:c * P + P], m.S3T[:, c, :], start=(c == 0), stop=(c == 1))
                        last.then_inc(q["product3"], 1)
                pe.wait_ge(q["column"], NT + 2)
                nc.tensor.matmul(psum[4][0:NT, 0:P], col[:, :], m.ident[:, :], start=True, stop=True).then_inc(q["column_turned"], 1)

            @block.vector
            def _(dve):
                s = Steps(dve, m)
                s.done(nc.vector.tensor_scalar(deg1[:, :], m.degree[:, :], 1.0, None, ALU.max))
                s.wait()
                nc.vector.reciprocal(rdeg[:, :], deg1[:, :]).then_inc(q["mean_ready"], 1)
                dve.sem_inc(q["turned_used"], 2)
                dve.sem_inc(q["product_used"], 2)
                s.fold()
                with dve.Fori(0, NT // 2) as t2:
                    for i in range(2):
                        n = t2 * 2 + (i + 1)
                        T = t2 * 2 + i
                        mine = tile_of(m.x, T, D)
                        dve.wait_ge(q["turned"], n)
                        nc.vector.tensor_copy(pairT[i][:, :], psum[i][:, :]).then_inc(q["turned_used"], 1)
                        dve.wait_ge(q["product"], n)
                        nc.vector.scalar_tensor_tensor(mine, psum[2 + i][:, 0:D], 0.0, mine, ALU.max, ALU.add).then_inc(q["product_used"], 1)
                        dve.wait_ge(q["product_used"], n + 2)
                        dve.sem_inc(m.tick, 1)
                        tile_stats(nc, m, s, T)
                        s.fold()
                layernorm_scale(nc, m, s, q["var_ready"], q["root_ready"], 1)
                dve.sem_inc(q["shift_ready"], 1)
                dve.sem_inc(q["product3_used"], 2)
                dve.sem_inc(q["column"], 2)
                with dve.Fori(0, NT // 2) as t2:
                    for i in range(2):
                        n = t2 * 2 + (i + 1)
                        T = t2 * 2 + i
                        dve.wait_ge(q["h_ready"], n)
                        nc.vector.tensor_copy(col[:, bass.ds(T, 1)], pair[i][:, 0:1]).then_inc(q["column"], 1)
                        dve.wait_ge(q["product3"], n)
                        nc.vector.tensor_copy(tile_of(m.hbuf, T, D), psum[2 + i][:, 0:D]).then_inc(q["product3_used"], 1)
                dve.wait_ge(q["column_turned"], 1)
                nc.vector.tensor_copy(colT[:, :], psum[4][0:NT, 0:P]).then_inc(q["column_ready"], 1)


def after3(nc, m, sem, acc, out):
    q = {n: sem("a3_" + n) for n in ["x_ready", "stored"]}
    parts = 4
    each = NT // parts
    with nc.Block() as block:
        @block.sync
        def _(sp):
            for i in range(parts):
                sp.wait_ge(q["x_ready"], (i + 1) * each)
                sp.dma_start(out[i * each * P:(i + 1) * each * P, :].rearrange("(t p) d -> p t d", p=P),
                             m.x[:, i * each * D:(i + 1) * each * D].rearrange("p (t d) -> p t d", d=D)).then_inc(q["stored"], 16)
            sp.wait_ge(q["stored"], 16 * parts)

        @block.vector
        def _(dve):
            s = Steps(dve, m)
            with dve.Fori(0, NT) as T:
                mine = tile_of(m.x, T, D)
                own = tile_of(m.hbuf, T, D)
                s.done(nc.vector.scalar_tensor_tensor(own, m.neigh_sum[:, :], acc[:, bass.ds(T, 1)], own, ALU.mult, ALU.add))
                s.wait()
                nc.vector.scalar_tensor_tensor(mine, own, 0.0, mine, ALU.max, ALU.add).then_inc(q["x_ready"], 1)
                s.fold()


def build(nc, a, out):
    def scratch(name, shape, dt=F32):
        return nc.dram_tensor(name, shape, dt, kind="Internal").ap()
    edges = scratch("edges", (P, MAX_CHUNKS, WORDS), I32)
    table0 = scratch("table0", (N, ROW0))
    table1 = scratch("table1", (N, ROW1))
    table2 = scratch("table2", (N, D))
    table3 = scratch("table3", (N, 1))
    with ExitStack() as ctx:
        m = Mem()
        def sem(name):
            return ctx.enter_context(nc.semaphore(name))
        def keep(name, shape, dt=F32):
            return ctx.enter_context(nc.sbuf_tensor(name, shape, dt))
        m.iota_row_i = keep("iota_row_i", [P, P], I32)
        m.iota_col_i = keep("iota_col_i", [P, 1], I32)
        m.iota_row = keep("iota_row", [P, P])
        m.iota_col = keep("iota_col", [P, 1])
        m.ident = keep("ident", [P, P])
        m.tri = keep("tri", [P, P])
        m.ones = keep("ones", [P, P])
        m.degree = keep("degree", [P, NT])
        m.passes = keep("passes", [P, 1], I32)
        m.x = keep("x", [P, NT * D])
        m.hbuf = keep("hbuf", [P, NT * D])
        m.acc = keep("acc", [P, NT * H0])
        m.W0T = keep("W0T", [P, 2, D + 2 * HEADS])
        m.Wx1 = keep("Wx1", [P, 2, HID])
        m.Wx2 = keep("Wx2", [HID, HID])
        m.Wn1 = keep("Wn1", [P, 2, HID])
        m.Wn2 = keep("Wn2", [HID, HID])
        m.Wv = keep("Wv", [P, 2, OUT1])
        m.Wfx = keep("Wfx", [P, 2, OUT1])
        m.W2s = keep("W2s", [P, 2, D])
        m.W2n = keep("W2n", [P, 2, D])
        m.S3T = keep("S3T", [P, 2, D])
        m.bias_n = keep("bias_n", [1, OUT1 + HID])
        m.bias_x = keep("bias_x", [1, OUT1 + HID])
        m.norm_in = keep("norm_in", [1, 2 * D])
        m.norm = keep("norm", [P, 2 * D])
        m.bias_2 = keep("bias_2", [1, D])
        m.neigh_sum = keep("neigh_sum", [P, D])
        m.bx1 = keep("bx1", [HID, 1])
        m.bn1 = keep("bn1", [HID, 1])
        m.mv = keep("mv", [P, NT * 2])
        m.mv2 = keep("mv2", [P, 2])
        m.stats = keep("stats", [P, 6])
        m.var = keep("var", [P, NT])
        m.root = keep("root", [P, NT])
        m.rstd = keep("rstd", [P, NT])
        m.shift = keep("shift", [P, NT])
        m.score_i = keep("score_i", [P, NT * HEADS])
        m.row1 = keep("row1", [P, NT * HID])
        m.mean0 = keep("mean0", [P, H0])
        m.mean1 = keep("mean1", [P, ROW1])
        m.empty = keep("empty", [P, NT])
        m.running = keep("running", [P, NT * HEADS])
        psum = [ctx.enter_context(nc.psum_tensor(f"bank{i}", [P, 512], F32)) for i in range(8)]
        m.tick = sem("tick")
        m.vec_steps = sem("vec_steps")
        m.vec_open = 0
        m.vec_count = ctx.enter_context(nc.vector.register("vec_count"))
        constants(nc, m, sem)
        weights(nc, m, sem, psum, a)
        tables(nc, m, sem, psum, a["x"], a["L1_gnn_neigh"], table0, table1)
        scan(nc, m, sem, psum, a["adj"], edges)
        attend(nc, m, sem, psum, "l0", edges, table0, HEADS, DH + 1, HEADS, m.score_i, HEADS, 0.2, m.running, m.acc)
        after0(nc, m, sem, psum, m.acc)
        acc1 = m.acc[:, 0:NT * H1]
        attend(nc, m, sem, psum, "l1", edges, table1, 1, H1, HID, m.row1, HID, 0.01, m.running[:, 0:NT], acc1)
        after1(nc, m, sem, acc1, table2)
        acc2 = m.acc[:, 0:NT * D]
        gather_sum(nc, m, sem, psum, "l2", edges, table2, D, acc2)
        after2(nc, m, sem, psum, acc2, table3)
        acc3 = m.acc[:, 0:NT]
        gather_sum(nc, m, sem, psum, "l3", edges, table3, 1, acc3)
        after3(nc, m, sem, acc3, out)


_INS = ["x", "adj", "L0_gnn_W", "L0_gnn_a", "L0_gnn_gamma", "L0_gnn_beta", "L1_gnn_neigh", "L1_gnn_Wx1", "L1_gnn_bx1", "L1_gnn_Wx2",
        "L1_gnn_bx2", "L1_gnn_Wn1", "L1_gnn_bn1", "L1_gnn_Wn2", "L1_gnn_bn2", "L1_gnn_Wv", "L1_gnn_bv", "L1_gnn_Wfx", "L1_gnn_bfx",
        "L2_gnn_W_self", "L2_gnn_b_self", "L2_gnn_W_nb", "L2_gnn_b_nb", "L2_gnn_W_comb", "L2_gnn_b_comb", "L3_gnn_w_self",
        "L3_gnn_w_neigh"]


def kernel(**inputs):
    import numpy as _np
    import concourse.bacc as _bacc
    from concourse import mybir as _mybir
    from concourse.bass_utils import run_bass_kernel_spmd as _run

    nc = _bacc.Bacc("TRN2", target_bir_lowering=False, num_devices=1)
    arrays, args = {}, {}
    for name in _INS:
        a = _np.ascontiguousarray(inputs[name])
        arrays[f"in_{name}_dram"] = a
        args[name] = nc.dram_tensor(f"in_{name}_dram", a.shape, _mybir.dt.from_np(a.dtype), kind="ExternalInput").ap()
    out = nc.dram_tensor("out_0_dram", (N, D), F32, kind="ExternalOutput").ap()
    build(nc, args, out)
    r = _run(nc, [arrays], core_ids=[0])
    return r.results[0]["out_0_dram"]
```

```python
from contextlib import ExitStack

import concourse.bass as bass
from concourse import mybir

ALU = mybir.AluOpType
ACT = mybir.ActivationFunctionType
F32 = mybir.dt.float32
BF16 = mybir.dt.bfloat16
I32 = mybir.dt.int32
U32 = mybir.dt.uint32
AX = mybir.AxisListType

P = 128
N = 4096
D = 256
NT = N // P
SLOTS = 8
ITEM_CHUNKS = SLOTS
GROUP = 4
SETS = 4
PAD = GROUP * SETS
MAX_CHUNKS = NT * (N // SLOTS) * ITEM_CHUNKS + PAD
WORDS = 3
HEADS = 8
DH = D // HEADS
HID = 32
OUT1 = 128
H0 = HEADS * (DH + 1)
ROW0 = H0 + HEADS
H1 = OUT1 + 1
ROW1 = H1 + HID
EPS = 1e-5
NEVER = 9e15
BUFS = 4
HALF = 4
INFO = 12
I_START, I_END, I_ROW, I_ONE = 8, 9, 10, 11
W_J, W_TILE = 0, 2
H_ROW, H_SLOT = 2, 3
NOWHERE = 2 * N


class Steps:

    def __init__(self, eng, m):
        self.eng, self.m, self.sem, self.reg = eng, m, m.vec_steps, m.vec_count

    def done(self, ins):
        ins.then_inc(self.sem, 1)
        self.m.vec_open += 1
        return ins

    def wait(self):
        self.eng.wait_ge(self.sem, self.eng.snap(self.reg) + self.m.vec_open)

    def fold(self):
        if self.m.vec_open:
            self.eng.reg_add(self.reg, self.reg, self.m.vec_open)
        self.m.vec_open = 0


class Mem:
    pass


def constants(nc, m, sem):
    const_iota = sem("const_iota")
    const_base = sem("const_base")
    const_done = sem("const_done")
    with nc.Block() as block:
        @block.gpsimd
        def _(pool):
            nc.gpsimd.iota(m.iota_row_i[:, :], pattern=[[1, P]], base=0, channel_multiplier=0).then_inc(const_iota, 1)
            nc.gpsimd.iota(m.iota_col_i[:, :], pattern=[[1, 1]], base=0, channel_multiplier=1).then_inc(const_iota, 1)
            nc.gpsimd.memset(m.ident[:, :], 0.0).then_inc(const_base, 1)
            nc.gpsimd.memset(m.tri[:, :], 1.0).then_inc(const_base, 1)
            nc.gpsimd.memset(m.ones[:, :], 1.0)
            pool.wait_ge(const_base, 2)
            nc.gpsimd.affine_select(out=m.ident[:, :], in_=m.ident[:, :], compare_op=ALU.not_equal, fill=1.0,
                                    base=0, pattern=[[-1, P]], channel_multiplier=1)
            nc.gpsimd.affine_select(out=m.tri[:, :], in_=m.tri[:, :], compare_op=ALU.is_gt, fill=0.0,
                                    base=0, pattern=[[1, P]], channel_multiplier=-1)

        @block.vector
        def _(dve):
            dve.reg_mov(m.vec_count, 0)
            dve.wait_ge(const_iota, 2)
            nc.vector.tensor_copy(m.iota_row[:, :], m.iota_row_i[:, :])
            nc.vector.tensor_copy(m.iota_col[:, :], m.iota_col_i[:, :])


def tile_of(t, number, width):
    return t[:, bass.ds(number * width, width)]


def x_stats(nc, m, s, unroll=4):
    with s.eng.Fori(0, NT // unroll) as t:
        for k in range(unroll):
            T = t * unroll + k
            s.done(nc.vector.bn_stats(tile_of(m.stats, T, 6), tile_of(m.x, T, D)))
        s.fold()


def layernorm_scale(nc, m, s, var_ready, root_ready, number):
    stat = m.stats[:, :].rearrange("p (t c) -> p t c", c=6)
    s.wait()
    s.done(nc.vector.tensor_tensor(m.mean_sum[:, :], stat[:, :, 1], stat[:, :, 4], ALU.add))
    s.done(nc.vector.tensor_tensor(m.mean_gap[:, :], stat[:, :, 1], stat[:, :, 4], ALU.subtract))
    s.done(nc.vector.tensor_tensor(m.dev_sum[:, :], stat[:, :, 2], stat[:, :, 5], ALU.add))
    s.wait()
    s.done(nc.vector.tensor_tensor(m.mean_gap[:, :], m.mean_gap[:, :], m.mean_gap[:, :], ALU.mult))
    s.wait()
    s.done(nc.vector.scalar_tensor_tensor(m.dev_sum[:, :], m.mean_gap[:, :], D / 4, m.dev_sum[:, :], ALU.mult, ALU.add))
    s.wait()
    nc.vector.tensor_scalar(m.var[:, :], m.dev_sum[:, :], 1.0 / D, EPS, ALU.mult, ALU.add).then_inc(var_ready, 1)
    s.eng.wait_ge(root_ready, number)
    s.done(nc.vector.reciprocal(m.rstd[:, :], m.root[:, :]))
    s.wait()
    s.done(nc.vector.scalar_tensor_tensor(m.shift[:, :], m.mean_sum[:, :], -0.5, m.rstd[:, :], ALU.mult, ALU.mult))
    s.wait()


def weights(nc, m, sem, psum, a):
    w_in = sem("w_in")
    w_turned = sem("w_turned")
    w_used = sem("w_used")
    w_folded = sem("w_folded")
    w_steps = sem("w_steps")
    heads_ready = sem("heads_ready")
    x_in = sem("x_in")
    var_ready = sem("var_ready")
    root_ready = sem("root_ready")
    n = {"in": 0}
    with ExitStack() as ctx:
        def sb(name, shape):
            return ctx.enter_context(nc.sbuf_tensor(name, shape, F32))
        W0 = sb("W0", [P, 2, D])
        Ws = sb("Ws", [P, 2, D])
        Wn = sb("Wn", [P, 2, D])
        Wc = sb("Wc", [P, 4, D])
        S3 = sb("S3", [P, 2, D])
        N3 = sb("N3", [P, 2, D])
        WsT = sb("WsT", [P, 2, D])
        WnT = sb("WnT", [P, 2, D])
        N3T = sb("N3T", [P, 2, D])
        acol = sb("acol", [P, 2])
        heads = sb("heads", [P, 2, 2 * HEADS])
        bcol = sb("bcol", [P, 2, 2])
        bcomb = sb("bcomb", [1, D])
        folded = lambda w: w.rearrange("(c p) n -> p c n", p=P)
        loads = [(W0[:, :, :], folded(a["L0_gnn_W"])), (Ws[:, :, :], folded(a["L2_gnn_W_self"])),
                 (Wn[:, :, :], folded(a["L2_gnn_W_nb"])), (Wc[:, :, :], folded(a["L2_gnn_W_comb"])),
                 (S3[:, :, :], folded(a["L3_gnn_w_self"])), (N3[:, :, :], folded(a["L3_gnn_w_neigh"])),
                 (m.Wx1[:, :, :], folded(a["L1_gnn_Wx1"])), (m.Wn1[:, :, :], folded(a["L1_gnn_Wn1"])),
                 (m.Wv[:, :, :], folded(a["L1_gnn_Wv"])), (m.Wfx[:, :, :], folded(a["L1_gnn_Wfx"])),
                 (m.Wx2[:, :], a["L1_gnn_Wx2"]), (m.Wn2[:, :], a["L1_gnn_Wn2"]),
                 (m.bias_n[0:1, 0:OUT1], a["L1_gnn_bv"][None, :]), (m.bias_n[0:1, OUT1:OUT1 + HID], a["L1_gnn_bn2"][None, :]),
                 (m.bias_x[0:1, 0:HID], a["L1_gnn_bx2"][None, :]), (m.bias_x[0:1, HID:HID + OUT1], a["L1_gnn_bfx"][None, :]),
                 (m.norm_in[0:1, 0:D], a["L0_gnn_gamma"][None, :]), (m.norm_in[0:1, D:2 * D], a["L0_gnn_beta"][None, :]),
                 (bcomb[:, :], a["L2_gnn_b_comb"][None, :])]
        thin = [(m.bx1[:, :], a["L1_gnn_bx1"][:, None]), (m.bn1[:, :], a["L1_gnn_bn1"][:, None]),
                (bcol[:, :, 0:1], a["L2_gnn_b_self"].rearrange("(c p o) -> p c o", p=P, o=1)),
                (bcol[:, :, 1:2], a["L2_gnn_b_nb"].rearrange("(c p o) -> p c o", p=P, o=1))]
        thin += [(acol[32 * g:32 * g + 32, :], a["L0_gnn_a"].rearrange("(s d) -> d s", s=2)) for g in range(4)]
        total = 16 * (len(loads) + len(thin))

        with nc.Block() as block:
            @block.sync
            def _(sp):
                for dst, src in loads:
                    sp.dma_start(dst, src).then_inc(w_in, 16)
                for dst, src in thin:
                    sp.dma_start(dst, src, allow_slow_non_contiguous=True).then_inc(w_in, 16)
                sp.wait_ge(w_in, total)

            @block.scalar
            def _(act):
                q4 = NT // 4
                for i in range(4):
                    act.dma_start(m.x[:, i * q4 * D:(i + 1) * q4 * D].rearrange("p (t d) -> p t d", d=D),
                                  a["x"][i * q4 * P:(i + 1) * q4 * P, :].rearrange("(t p) d -> p t d", p=P)).then_inc(x_in, 16)
                act.wait_ge(var_ready, 1)
                nc.scalar.activation(m.root[:, :], m.var[:, :], ACT.Sqrt).then_inc(root_ready, 1)

            @block.tensor
            def _(pe):
                pe.wait_ge(w_in, total)
                for b, W in enumerate((W0, Ws, Wn, S3, N3)):
                    for r in range(2):
                        for c in range(2):
                            last = nc.tensor.transpose(psum[b][:, r * D + c * P:r * D + c * P + P],
                                                       W[:, c, r * P:r * P + P], m.ident[:, :])
                    last.then_inc(w_turned, 1)
                pe.wait_ge(heads_ready, 1)
                for r in range(2):
                    for c in range(2):
                        last = nc.tensor.matmul(psum[5][:, r * 32:r * 32 + 2 * HEADS], W0[:, c, r * P:r * P + P],
                                                heads[:, c, :], start=(c == 0), stop=(c == 1))
                last.then_inc(w_turned, 1)
                pe.wait_ge(w_used, 6)
                for b, (WT, half) in enumerate(((WsT, 0), (WnT, 2))):
                    for r in range(2):
                        for c in range(2):
                            last = nc.tensor.matmul(psum[b][:, r * D:r * D + D], WT[:, c, r * P:r * P + P],
                                                    Wc[:, half + c, :], start=(c == 0), stop=(c == 1))
                    last.then_inc(w_folded, 1)
                for c in range(2):
                    for half in range(2):
                        nc.tensor.matmul(psum[2][0:1, 0:D], bcol[:, c, half:half + 1], Wc[:, 2 * half + c, :],
                                         start=(c == 0 and half == 0), stop=False)
                nc.tensor.matmul(psum[2][0:1, 0:D], m.ones[0:1, 0:1], bcomb[:, :], start=False, stop=True).then_inc(w_folded, 1)
                for c in range(2):
                    last = nc.tensor.matmul(psum[3][:, 0:D], m.ones[:, :], N3T[:, c, :], start=(c == 0), stop=(c == 1))
                last.then_inc(w_folded, 1)
                nc.tensor.matmul(psum[4][:, 0:2 * D], m.ones[0:1, :], m.norm_in[:, :], start=True, stop=True).then_inc(w_folded, 1)

            @block.vector
            def _(dve):
                nc.vector.memset(heads[:, :, :], 0.0).then_inc(w_steps, 1)
                s = Steps(dve, m)
                dve.wait_ge(x_in, 64)
                x_stats(nc, m, s)
                dve.wait_ge(w_steps, 1)
                dve.wait_ge(w_in, total)
                for c in range(2):
                    for g in range(4):
                        rows, head = slice(32 * g, 32 * g + 32), 4 * c + g
                        nc.vector.tensor_copy(heads[rows, c, head:head + 1], acol[rows, 0:1])
                        last = nc.vector.tensor_copy(heads[rows, c, HEADS + head:HEADS + head + 1], acol[rows, 1:2])
                last.then_inc(heads_ready, 1)
                layernorm_scale(nc, m, s, var_ready, root_ready, 1)
                s.fold()
                both = lambda t: t.rearrange("p (c n) -> p c n", c=2)
                dve.wait_ge(w_turned, 1)
                nc.vector.tensor_copy(m.W0T[:, :, 0:D], both(psum[0][:, :])).then_inc(w_used, 1)
                for b, to in ((1, WsT), (2, WnT), (3, m.S3T), (4, N3T)):
                    dve.wait_ge(w_turned, b + 1)
                    nc.vector.tensor_copy(to[:, :, :], both(psum[b][:, :])).then_inc(w_used, 1)
                dve.wait_ge(w_turned, 6)
                nc.vector.tensor_copy(m.W0T[:, :, D:D + 2 * HEADS],
                                      psum[5][:, 0:64].rearrange("p (c n) -> p c n", c=2)[:, :, 0:2 * HEADS]).then_inc(w_used, 1)
                dve.wait_ge(w_folded, 1)
                nc.vector.tensor_copy(m.W2s[:, :, :], both(psum[0][:, :]))
                dve.wait_ge(w_folded, 2)
                nc.vector.tensor_copy(m.W2n[:, :, :], both(psum[1][:, :]))
                dve.wait_ge(w_folded, 3)
                nc.vector.tensor_copy(m.bias_2[:, :], psum[2][0:1, 0:D])
                dve.wait_ge(w_folded, 4)
                nc.vector.tensor_copy(m.neigh_sum[:, :], psum[3][:, 0:D])
                dve.wait_ge(w_folded, 5)
                nc.vector.tensor_copy(m.norm[:, :], psum[4][:, 0:2 * D])



def scan(nc, m, sem, psum, adj, edges, neigh, table0, table1):
    adj_in = [sem(f"adj_in{i}") for i in range(BUFS)]
    names = ["adj_free", "deg_ready", "deg_row_ready", "rounds_ready", "rounds_taken", "count_ready", "prefix_ready", "chunks_ready",
             "chunks_taken", "place_ready", "spread_ready", "record_ready", "record_stored",
             "h_ready", "x_turned", "x_copied", "n_turned", "n_copied", "product", "hid_ready", "tanh_ready", "natt_ready",
             "row_ready", "row1_ready", "mean_ready", "summed"]
    q = {n: sem("scan_" + n) for n in names}
    neigh_in = [sem(f"neigh_in{i}") for i in range(2)]
    row_out = [sem(f"row_out{i}") for i in range(2)]
    halves_of = ITEM_CHUNKS // HALF

    with ExitStack() as ctx:
        def sb(name, shape, dt=F32):
            return ctx.enter_context(nc.sbuf_tensor(name, shape, dt))
        A = [t[:, k * N:(k + 1) * N].bitcast(I32) for t in (m.hbuf, m.acc) for k in range(2)]
        junk = sb("scan_junk", [P, N], BF16)
        degc = [sb(f"degc{i}", [P, 1]) for i in range(BUFS)]
        left = sb("left", [P, 1])
        cnt = sb("cnt", [P, 1])
        vals = sb("vals", [P, SLOTS])
        J = sb("J", [P, SLOTS], U32)
        rowinfo = sb("rowinfo", [P, INFO])
        small = sb("scan_small", [P, 4])
        ints = sb("scan_ints", [P, 4], I32)
        tile_no = sb("tile_no", [P, 1])
        place_row_i = sb("place_row_i", [P, HALF * P], I32)
        place_row = sb("place_row", [P, HALF * P])
        place_col_i = sb("place_col_i", [P, HALF], I32)
        place_col = sb("place_col", [P, HALF])
        since = sb("since", [P, HALF * P])
        hot = sb("hot", [P, HALF * P])
        slot = sb("slot", [P, HALF])
        nowhere = sb("nowhere", [P, HALF])
        jf = sb("jf", [P, HALF])
        pick = sb("pick", [P, HALF * SLOTS])
        picked = sb("picked", [P, HALF * SLOTS])
        rec = sb("rec", [P, ITEM_CHUNKS, WORDS], I32)
        reci = rec[:, :, :]
        rech = rec[:, :, :].bitcast(BF16)
        mx, mx2, nchf, ncsum = (small[:, i:i + 1] for i in range(4))
        ps_deg, ps_pre, ps_info, ps_x, ps_n, ps_product, ps_hid, ps_row1 = psum
        info3 = ps_info[:, 0:HALF * INFO].rearrange("p (c i) -> p c i", i=INFO)

        hb = sb("hb", [P, D])
        nb = [sb(f"nb{i}", [P, D]) for i in range(2)]
        hT = sb("hT", [P, 2 * P])
        nT = sb("nT", [P, 2 * P])
        hid = sb("hid", [HID, P])
        row = [sb(f"row0_{i}", [P, ROW0]) for i in range(2)]
        row1 = [sb(f"row1_{i}", [P, ROW1]) for i in range(2)]
        sums = sb("sums", [P, H0 + ROW1])

        def groups(eng, tile):
            with eng.Fori(0, NT // BUFS - 1) as t4:
                for i in range(BUFS):
                    tile(t4 * BUFS + i, i, t4, False)
            for i in range(BUFS):
                tile(NT - BUFS + i, i, NT // BUFS - 1, True)

        with nc.Block() as block:
            @block.sync
            def _(sp):
                for i in range(BUFS):
                    sp.dma_start(A[i], adj[i * P:(i + 1) * P, :]).then_inc(adj_in[i], 16)
                for i in range(2):
                    sp.dma_start(nb[i][:, :], neigh[i * P:(i + 1) * P, :]).then_inc(neigh_in[i], 16)
                    sp.sem_inc(row_out[i], 32)

                def tile(T, i, t4, last):
                    p = i % 2
                    if not last or i < BUFS - 2:
                        sp.wait_ge(q["n_turned"], T + 1)
                        sp.dma_start(nb[p][:, :], neigh[bass.ds((T + 2) * P, P), :]).then_inc(neigh_in[p], 16)
                    sp.wait_ge(q["row_ready"], T + 2)
                    sp.dma_start(table0[bass.ds(T * P, P), :], row[p][:, :]).then_inc(row_out[p], 16)
                    if not last:
                        sp.wait_ge(q["adj_free"], T + 1)
                        sp.dma_start(A[i], adj[bass.ds((T + BUFS) * P, P), :]).then_inc(adj_in[i], 16)
                    sp.wait_ge(q["row1_ready"], T + 2)
                    sp.dma_start(table1[bass.ds(T * P, P), :], row1[p][:, :]).then_inc(row_out[p], 16)
                groups(sp, tile)
                for i in range(2):
                    sp.wait_ge(row_out[i], 32 + 16 * NT)

            @block.scalar
            def _(act):
                def h_of(T):
                    nc.scalar.activation(hb[:, :], tile_of(m.x, T, D), ACT.Relu, scale=m.rstd[:, bass.ds(T, 1)],
                                         bias=m.shift[:, bass.ds(T, 1)]).then_inc(q["h_ready"], 1)

                def degree_of(i, loaded):
                    act.wait_ge(adj_in[i], loaded)
                    nc.scalar.activation(junk[:, :], A[i], ACT.Copy, accum_out=degc[i][:, :]).then_inc(q["deg_ready"], 1)

                h_of(0)
                degree_of(0, 16)
                act.wait_ge(q["deg_ready"], 1)
                degree_of(1, 16)

                def tile(T, i, t4, last):
                    p = i % 2
                    act.wait_ge(q["x_turned"], T + 1)
                    nc.scalar.activation(hT[:, :], ps_x[:, 0:2 * P], ACT.Copy).then_inc(q["x_copied"], 1)
                    act.wait_ge(q["n_turned"], T + 1)
                    nc.scalar.activation(nT[:, :], ps_n[:, 0:2 * P], ACT.Copy).then_inc(q["n_copied"], 1)
                    act.wait_ge(q["product"], T + 1)
                    act.wait_ge(row_out[p], t4 * (16 * BUFS) + (32 * (i // 2) + 32))
                    act.wait_ge(q["summed"], T * 2 + 1)
                    act.sem_inc(m.tick, 1)
                    nc.scalar.activation(tile_of(m.score_i, T, HEADS), ps_product[:, D + HEADS:D + 2 * HEADS], ACT.Copy)
                    nc.scalar.activation(row[p][:, H0:ROW0], ps_product[:, D:D + HEADS], ACT.Copy)
                    nc.scalar.activation(row[p][:, 0:H0].rearrange("p (h d) -> p h d", h=HEADS)[:, :, 0:DH],
                                         ps_product[:, 0:D].rearrange("p (h d) -> p h d", h=HEADS), ACT.Copy).then_inc(q["row_ready"], 1)
                    if not last or i < BUFS - 1:
                        h_of(T + 1)
                    if not last or i < BUFS - 2:
                        act.wait_ge(q["deg_ready"], T + 2)
                        j = (i + 2) % BUFS
                        degree_of(j, t4 * 16 + (16 if i < BUFS - 2 else 32))
                    elif i == BUFS - 2:
                        act.sem_inc(q["deg_ready"], 1)
                    act.wait_ge(q["hid_ready"], T + 1)
                    nc.scalar.activation(hid[:, :], ps_hid[0:HID, 0:P], ACT.Tanh, bias=m.bn1[:, :]).then_inc(q["tanh_ready"], 1)
                    act.wait_ge(q["natt_ready"], T + 1)
                    nc.scalar.activation(row1[p][:, H1:ROW1], ps_row1[:, OUT1:OUT1 + HID], ACT.Copy)
                    nc.scalar.activation(row1[p][:, 0:OUT1], ps_row1[:, 0:OUT1], ACT.Copy).then_inc(q["row1_ready"], 1)
                groups(act, tile)

            @block.tensor
            def _(pe):
                with pe.register("scan_nr") as nr, pe.register("scan_nch") as nch, pe.register("scan_items") as items, \
                        pe.register("scan_halves") as halves:
                    pe.reg_mov(items, 0)
                    pe.reg_mov(halves, 0)
                    pe.sem_inc(q["n_copied"], 1)
                    pe.sem_inc(q["row_ready"], 1)
                    pe.sem_inc(q["row1_ready"], 1)

                    def degree_row(i):
                        nc.tensor.matmul(ps_deg[0:1, 0:P], degc[i][:, :], m.ident[:, :], start=True, stop=True).then_inc(q["deg_row_ready"], 1)

                    def first_products(T, i, t4):
                        p = i % 2
                        pe.wait_ge(q["h_ready"], T + 1)
                        for c in range(2):
                            last = nc.tensor.transpose(ps_x[:, c * P:c * P + P], hb[:, c * P:c * P + P], m.ident[:, :])
                        last.then_inc(q["x_turned"], 1)
                        pe.wait_ge(neigh_in[p], t4 * (8 * BUFS) + (16 * (i // 2) + 16))
                        pe.wait_ge(q["n_copied"], T + 1)
                        for c in range(2):
                            last = nc.tensor.transpose(ps_n[:, c * P:c * P + P], nb[p][:, c * P:c * P + P], m.ident[:, :])
                        last.then_inc(q["n_turned"], 1)
                        pe.wait_ge(q["x_copied"], T + 1)
                        pe.wait_ge(q["row_ready"], T + 1)
                        for c in range(2):
                            last = nc.tensor.matmul(ps_product[:, 0:D + 2 * HEADS], hT[:, c * P:c * P + P], m.W0T[:, c, :],
                                                    start=(c == 0), stop=(c == 1))
                        last.then_inc(q["product"], 1)

                    def second_products(T):
                        pe.wait_ge(q["n_copied"], T + 2)
                        for c in range(2):
                            last = nc.tensor.matmul(ps_hid[0:HID, 0:P], m.Wn1[:, c, :], nT[:, c * P:c * P + P],
                                                    start=(c == 0), stop=(c == 1))
                        last.then_inc(q["hid_ready"], 1)
                        pe.wait_ge(q["row1_ready"], T + 1)
                        for c in range(2):
                            nc.tensor.matmul(ps_row1[:, 0:OUT1], nT[:, c * P:c * P + P], m.Wv[:, c, :], start=(c == 0), stop=False)
                        nc.tensor.matmul(ps_row1[:, 0:OUT1], m.ones[0:1, :], m.bias_n[0:1, 0:OUT1], start=False, stop=True)
                        pe.wait_ge(q["tanh_ready"], T + 1)
                        nc.tensor.matmul(ps_row1[:, OUT1:OUT1 + HID], hid[:, :], m.Wn2[:, :], start=True, stop=False)
                        nc.tensor.matmul(ps_row1[:, OUT1:OUT1 + HID], m.ones[0:1, :], m.bias_n[0:1, OUT1:OUT1 + HID],
                                         start=False, stop=True).then_inc(q["natt_ready"], 1)

                    def spread():
                        pe.wait_ge(q["place_ready"], pe.snap(halves) + 1)
                        for c in range(HALF):
                            last = nc.tensor.matmul(ps_info[:, c * INFO:(c + 1) * INFO], hot[:, c * P:(c + 1) * P], rowinfo[:, :],
                                                    start=True, stop=True)
                        last.then_inc(q["spread_ready"], 1)
                        pe.reg_add(halves, halves, 1)

                    def item(beside=None):
                        it = pe.snap(items)
                        pe.wait_ge(q["count_ready"], it + 1)
                        nc.tensor.matmul(ps_pre[:, 0:1], m.tri[:, :], cnt[:, :], start=True, stop=True)
                        nc.tensor.matmul(ps_pre[:, 1:2], m.ones[:, :], cnt[:, :], start=True, stop=True).then_inc(q["prefix_ready"], 1)
                        if beside:
                            beside()
                        pe.wait_ge(q["chunks_ready"], it + 1)
                        pe.sem_inc(m.tick, 1)
                        pe.reg_load(nch, ints[0:1, 0:1])
                        pe.sem_inc(q["chunks_taken"], 1)
                        spread()
                        with pe.If(pe.snap(nch, min_val=1, max_val=ITEM_CHUNKS) > HALF):
                            spread()
                        pe.reg_add(items, items, 1)

                    pe.wait_ge(q["deg_ready"], 1)
                    degree_row(0)
                    with pe.Fori(0, NT // BUFS) as t4:
                        for i in range(BUFS):
                            T = t4 * BUFS + i

                            def beside():
                                pe.wait_ge(q["deg_ready"], T + 2)
                                pe.wait_ge(q["rounds_ready"], T + 1)
                                degree_row((i + 1) % BUFS)
                                first_products(T, i, t4)
                            item(beside)
                            pe.wait_ge(q["rounds_ready"], T + 1)
                            pe.sem_inc(m.tick, 1)
                            pe.reg_load(nr, ints[0:1, 2 + i % 2:3 + i % 2])
                            pe.sem_inc(q["rounds_taken"], 1)
                            n = pe.snap(nr, min_val=1, max_val=N // SLOTS)
                            with pe.If(n > 1):
                                with pe.Fori(1, n):
                                    item()
                            second_products(T)
                pe.wait_ge(q["summed"], 2 * NT + 3)
                nc.tensor.matmul(ps_product[:, 0:H0], m.ones[:, :], sums[:, 0:H0], start=True, stop=True)
                nc.tensor.matmul(ps_row1[:, 0:ROW1], m.ones[:, :], sums[:, H0:H0 + ROW1], start=True, stop=True).then_inc(q["mean_ready"], 1)

            @block.gpsimd
            def _(pool):
                with pool.register("scan_nr") as nr, pool.register("scan_nch") as nch, pool.register("scan_items") as items, \
                        pool.register("scan_chunks") as chunks:
                    pool.reg_mov(items, 0)
                    pool.reg_mov(chunks, 0)
                    pool.sem_inc(q["summed"], 2)
                    nc.gpsimd.iota(place_row_i[:, :], pattern=[[1, HALF * P]], base=0, channel_multiplier=0)
                    nc.gpsimd.iota(place_col_i[:, :], pattern=[[P, HALF]], base=0, channel_multiplier=1)
                    nc.gpsimd.memset(sums[:, :], 0.0).then_inc(q["summed"], 1)
                    pool.wait_ge(q["record_ready"], 1)
                    pool.dma_start(edges[:, 0:ITEM_CHUNKS, :], reci).then_inc(q["record_stored"], 16)

                    def store():
                        it = pool.snap(items)
                        pool.wait_ge(q["chunks_ready"], it + 1)
                        pool.sem_inc(m.tick, 1)
                        pool.reg_load(nch, ints[0:1, 0:1])
                        pool.sem_inc(q["chunks_taken"], 1)
                        pool.wait_ge(q["record_ready"], it + 2)
                        pool.wait_ge(q["record_stored"], it * 16 + 16)
                        pool.sem_inc(m.tick, 1)
                        at = pool.snap(chunks, min_val=0, max_val=MAX_CHUNKS - PAD)
                        pool.dma_start(edges[:, bass.ds(at, ITEM_CHUNKS), :], reci).then_inc(q["record_stored"], 16)
                        pool.reg_add(chunks, chunks, pool.snap(nch, min_val=1, max_val=ITEM_CHUNKS))
                        pool.reg_add(items, items, 1)

                    with pool.Fori(0, NT // 2) as t2:
                        for i in range(2):
                            T = t2 * 2 + i
                            store()
                            pool.wait_ge(q["rounds_ready"], T + 1)
                            pool.sem_inc(m.tick, 1)
                            pool.reg_load(nr, ints[0:1, 2 + i:3 + i])
                            pool.sem_inc(q["rounds_taken"], 1)
                            n = pool.snap(nr, min_val=1, max_val=N // SLOTS)
                            with pool.If(n > 1):
                                with pool.Fori(1, n):
                                    store()
                            pool.wait_ge(q["row_ready"], T + 2)
                            pool.wait_ge(q["summed"], T * 2 + 3)
                            pool.sem_inc(m.tick, 1)
                            nc.gpsimd.tensor_tensor(sums[:, 0:H0], sums[:, 0:H0], row[i][:, 0:H0], ALU.add).then_inc(q["summed"], 1)
                            pool.wait_ge(q["row1_ready"], T + 2)
                            pool.sem_inc(m.tick, 1)
                            nc.gpsimd.tensor_tensor(sums[:, H0:H0 + ROW1], sums[:, H0:H0 + ROW1], row1[i][:, :], ALU.add).then_inc(q["summed"], 1)
                    it = pool.snap(items)
                    pool.wait_ge(q["record_ready"], it + 2)
                    pool.wait_ge(q["record_stored"], it * 16 + 16)
                    pool.sem_inc(m.tick, 1)
                    for extra in range(0, PAD, ITEM_CHUNKS):
                        if extra:
                            pool.reg_add(chunks, chunks, ITEM_CHUNKS)
                        at = pool.snap(chunks, min_val=0, max_val=MAX_CHUNKS - ITEM_CHUNKS)
                        pool.dma_start(edges[:, bass.ds(at, ITEM_CHUNKS), :], reci).then_inc(q["record_stored"], 16)
                    pool.wait_ge(q["record_stored"], it * 16 + 16 * (1 + PAD // ITEM_CHUNKS))
                    pool.sem_inc(m.tick, 1)

            @block.vector
            def _(dve):
                with dve.register("scan_nr") as nr, dve.register("scan_nch") as nch, dve.register("scan_items") as items, \
                        dve.register("scan_halves") as halves:
                    s = Steps(dve, m)
                    dve.reg_mov(items, 0)
                    dve.reg_mov(halves, 0)
                    dve.sem_inc(q["chunks_taken"], 2)
                    dve.sem_inc(q["rounds_taken"], 2)
                    for i in range(2):
                        s.done(nc.vector.memset(row[i][:, :], 1.0))
                        s.done(nc.vector.memset(row1[i][:, :], 1.0))
                    s.done(nc.vector.memset(rowinfo[:, I_ONE:I_ONE + 1], 1.0))
                    s.done(nc.vector.memset(ncsum, 0.0))
                    s.done(nc.vector.memset(tile_no[:, :], 0.0))
                    nc.vector.memset(rec[:, :, :], 0).then_inc(q["record_ready"], 1)
                    s.done(nc.vector.tensor_scalar(rowinfo[:, I_ROW:I_ROW + 1], m.iota_col[:, :], 1.0, None, ALU.add))
                    dve.wait_ge(q["summed"], 3)
                    s.done(nc.vector.tensor_copy(place_row[:, :], place_row_i[:, :]))
                    s.done(nc.vector.tensor_copy(place_col[:, :], place_col_i[:, :]))

                    def rounds(i):
                        s.done(nc.vector.tensor_reduce(mx[0:1, :], ps_deg[0:1, 0:P], AX.X, ALU.max))
                        s.wait()
                        s.done(nc.vector.tensor_scalar(mx2[0:1, :], mx[0:1, :], (SLOTS - 1) / 2, 1.0 / SLOTS, ALU.add, ALU.mult))
                        s.wait()
                        nc.vector.tensor_scalar(ints[0:1, 2 + i % 2:3 + i % 2], mx2[0:1, :], 1.0, None, ALU.max).then_inc(q["rounds_ready"], 1)

                    def make_places():
                        s.wait()
                        s.done(nc.vector.tensor_scalar(since[:, :], place_row[:, :], rowinfo[:, I_START:I_START + 1], None, ALU.is_ge))
                        s.wait()
                        return nc.vector.scalar_tensor_tensor(hot[:, :], place_row[:, :], rowinfo[:, I_END:I_END + 1], since[:, :], ALU.is_lt, ALU.mult)

                    def records(h, it):
                        c = slice(h * HALF, (h + 1) * HALF)
                        s.wait()
                        dve.wait_ge(q["spread_ready"], dve.snap(halves) + 1)
                        if h == 0:
                            dve.wait_ge(q["record_stored"], it * 16 + 16)
                            dve.sem_inc(m.tick, 1)
                        slot3 = slot[:, :].rearrange("p (c o) -> p c o", o=1)
                        s.done(nc.vector.tensor_tensor(slot3, place_col[:, :].rearrange("p (c o) -> p c o", o=1),
                                                       info3[:, :, I_START:I_START + 1], ALU.subtract))
                        s.done(nc.vector.tensor_scalar(rech[:, c, H_ROW], info3[:, :, I_ROW], 1.0, None, ALU.subtract))
                        s.done(nc.vector.tensor_scalar(nowhere[:, :], info3[:, :, I_ONE], -float(NOWHERE), float(NOWHERE), ALU.mult, ALU.add))
                        s.wait()
                        pick3 = pick[:, :].rearrange("p (c k) -> p c k", k=SLOTS)
                        picked3 = picked[:, :].rearrange("p (c k) -> p c k", k=SLOTS)
                        s.done(nc.vector.tensor_tensor(pick3, m.iota_row[:, None, 0:SLOTS].broadcast_to([P, HALF, SLOTS]),
                                                       slot3.broadcast_to([P, HALF, SLOTS]), ALU.is_equal))
                        s.done(nc.vector.tensor_copy(rech[:, c, H_SLOT], slot[:, :]))
                        s.wait()
                        s.done(nc.vector.tensor_tensor(picked3, pick3, info3[:, :, 0:SLOTS], ALU.mult))
                        s.wait()
                        s.done(nc.vector.tensor_reduce(jf[:, :], picked3, AX.X, ALU.add))
                        s.wait()
                        s.done(nc.vector.tensor_tensor(reci[:, c, W_J], jf[:, :], nowhere[:, :], ALU.add))
                        dve.reg_add(halves, halves, 1)
                        s.fold()

                    def item(T, i, first):
                        it = dve.snap(items)
                        if not first:
                            s.wait()
                            dve.sem_inc(m.tick, 1)
                            s.done(nc.vector.match_replace(A[i], vals[:, :], A[i], 0.0))
                        remaining = degc[i][:, :] if first else left[:, :]
                        nc.vector.tensor_scalar(cnt[:, :], remaining, 0.0, float(SLOTS), ALU.max, ALU.min).then_inc(q["count_ready"], 1)
                        s.done(nc.vector.tensor_scalar(left[:, :], remaining, float(SLOTS), None, ALU.subtract))
                        dve.wait_ge(q["count_ready"], it + 1)
                        s.done(nc.vector.tensor_scalar(vals[:, :], m.iota_row[:, 0:SLOTS], cnt[:, 0:1], None, ALU.is_lt))
                        if first:
                            dve.wait_ge(q["deg_row_ready"], T + 2)
                            dve.sem_inc(m.tick, 1)
                            dve.wait_ge(q["rounds_taken"], T * 2 + 2)
                            dve.sem_inc(m.tick, 1)
                            rounds(i + 1)
                        s.wait()
                        dve.wait_ge(q["prefix_ready"], it + 1)
                        dve.wait_ge(q["chunks_taken"], it * 2 + 2)
                        s.done(nc.vector.tensor_scalar(nchf, ps_pre[:, 1:2], (P - 1) / 2, 1.0 / P, ALU.add, ALU.mult))
                        s.done(nc.vector.tensor_copy(rowinfo[:, I_START:I_START + 1], ps_pre[:, 0:1]))
                        s.done(nc.vector.tensor_tensor(rowinfo[:, I_END:I_END + 1], ps_pre[:, 0:1], cnt[:, :], ALU.add))
                        s.wait()
                        nc.vector.tensor_scalar(ints[:, 0:1], nchf, 1.0, None, ALU.max).then_inc(q["chunks_ready"], 1)
                        s.done(make_places())
                        dve.wait_ge(q["chunks_ready"], it + 1)
                        s.done(nc.vector.tensor_copy(nchf, ints[:, 0:1]))
                        s.wait()
                        s.done(nc.vector.tensor_tensor(ncsum, ncsum, nchf, ALU.add))
                        dve.reg_load(nch, ints[0:1, 0:1])
                        s.done(nc.vector.max_index(J[:, :], vals[:, :], A[i]))
                        s.wait()
                        nc.vector.tensor_copy(rowinfo[:, 0:SLOTS], J[:, :]).then_inc(q["place_ready"], 1)
                        records(0, it)
                        with dve.If(dve.snap(nch, min_val=1, max_val=ITEM_CHUNKS) > HALF):
                            s.done(nc.vector.tensor_scalar(rowinfo[:, I_START:I_END + 1], rowinfo[:, I_START:I_END + 1], float(HALF * P), None, ALU.subtract))
                            make_places().then_inc(q["place_ready"], 1)
                            records(1, it)
                        if first:
                            s.done(nc.vector.tensor_copy(reci[:, :, W_TILE], tile_no[:, :].broadcast_to([P, ITEM_CHUNKS])))
                        s.wait()
                        dve.sem_inc(q["record_ready"], 1)
                        dve.reg_add(items, items, 1)

                    dve.wait_ge(q["deg_row_ready"], 1)
                    rounds(0)
                    s.fold()
                    with dve.Fori(0, NT // BUFS) as t4:
                        for i in range(BUFS):
                            T = t4 * BUFS + i
                            item(T, i, True)
                            dve.wait_ge(q["rounds_ready"], T + 1)
                            dve.sem_inc(m.tick, 1)
                            dve.reg_load(nr, ints[0:1, 2 + i % 2:3 + i % 2])
                            s.fold()
                            n = dve.snap(nr, min_val=1, max_val=N // SLOTS)
                            with dve.If(n > 1):
                                with dve.Fori(1, n):
                                    item(T, i, False)
                                    s.fold()
                            s.wait()
                            dve.sem_inc(q["adj_free"], 1)
                            s.done(nc.vector.tensor_copy(m.degree[:, bass.ds(T, 1)], degc[i][:, :]))
                            s.done(nc.vector.tensor_scalar(tile_no[:, :], tile_no[:, :], 1.0, None, ALU.add))
                            s.fold()
                    it = dve.snap(items)
                    s.wait()
                    dve.wait_ge(q["record_stored"], it * 16 + 16)
                    s.done(nc.vector.tensor_scalar(mx, ncsum, (PAD - 1) / 2, 1.0 / PAD, ALU.add, ALU.mult))
                    s.done(nc.vector.memset(reci[:, :, W_J], NOWHERE))
                    s.done(nc.vector.memset(rech[:, :, H_ROW], -1.0))
                    s.done(nc.vector.memset(rech[:, :, H_SLOT], 0.0))
                    s.done(nc.vector.memset(reci[:, :, W_TILE], 0))
                    s.wait()
                    s.done(nc.vector.tensor_scalar(m.passes[:, :], mx, 1.0, None, ALU.max))
                    s.wait()
                    dve.sem_inc(q["record_ready"], 1)
                    dve.wait_ge(q["mean_ready"], 1)
                    s.done(nc.vector.tensor_scalar(m.mean0[:, :], ps_product[:, 0:H0], 1.0 / N, None, ALU.mult))
                    s.done(nc.vector.tensor_scalar(m.mean1[:, :], ps_row1[:, 0:ROW1], 1.0 / N, None, ALU.mult))
                    s.fold()


def grouped(t, width):
    return t[:, :].rearrange("p (u w) -> p u w", w=width)


def attend(nc, m, sem, psum, tag, edges, table, heads, width, extra, row_table, row_width, slope, running, acc):
    names = ["taken_pe", "taken_dve", "place_ready", "turned", "turned_used", "own_ready", "spread_ready", "slots_ready", "max_ready",
             "growth_ready", "top_ready", "score_ready", "weight_ready", "scaled_ready", "sum_ready", "merged", "g_clear"]
    q = {n: sem(f"{tag}_{n}") for n in names}
    rec_in = sem(f"{tag}_rec_in")
    gathered = [sem(f"{tag}_gathered{i}") for i in range(SETS)]
    hw = heads * width
    wide = hw + extra
    e1 = heads + 1
    c_slots = GROUP * row_width
    c_top = c_slots + GROUP * SLOTS * e1
    assert c_top + GROUP * heads <= 512
    with ExitStack() as ctx:
        def sb(name, shape, dt=F32):
            return [ctx.enter_context(nc.sbuf_tensor(f"{tag}_{name}{i}", shape, dt)) for i in range(SETS)]
        rec_all = ctx.enter_context(nc.sbuf_tensor(f"{tag}_rec", [P, PAD, WORDS], I32))
        rec = [rec_all[:, i * GROUP:(i + 1) * GROUP, :] for i in range(SETS)]
        G = sb("G", [P, GROUP * wide])
        GW = sb("GW", [P, GROUP * hw])
        place = sb("place", [P, GROUP * P])
        back = sb("back", [P, GROUP * P])
        slot1 = sb("slot1", [P, GROUP * SLOTS])
        z = sb("z", [P, GROUP * heads])
        zl = sb("zl", [P, GROUP * heads])
        zs = sb("zs", [P, GROUP * heads])
        wgt = sb("wgt", [P, GROUP * heads])
        spread = sb("spread", [P, GROUP * SLOTS * e1])
        absent = sb("absent", [P, GROUP * SLOTS])
        zm = sb("zm", [P, GROUP * heads * SLOTS])
        top = sb("top", [P, GROUP * heads])
        newmax = sb("newmax", [P, GROUP * heads])
        growth = sb("growth", [P, GROUP * heads])
        fade = sb("fade", [P, GROUP * heads])
        prod = sb("prod", [P, GROUP * row_width])
        bank_back = [psum[0], psum[1]]
        bank_small = [psum[2 + i] for i in range(SETS)]
        bank_sum = [psum[6], psum[7], psum[0], psum[1]]

        def tiles_of(eng, i, regs):
            for u in range(GROUP):
                eng.reg_load(regs[u], rec[i][0:1, u, W_TILE:W_TILE + 1])
            return [eng.snap(r, min_val=0, max_val=NT - 1) for r in regs]

        with nc.Block() as block:
            @block.sync
            def _(sp):
                with sp.register(f"{tag}_passes") as passes:
                    sp.reg_load(passes, m.passes[0:1, 0:1])
                    with sp.Fori(0, sp.snap(passes, min_val=1, max_val=MAX_CHUNKS // PAD)) as it:
                        sp.wait_ge(q["taken_pe"], it + 1)
                        sp.wait_ge(q["taken_dve"], it + 1)
                        sp.dma_start(rec_all[:, :, :], edges[:, bass.ds(it * PAD, PAD), :]).then_inc(rec_in, 16)

            @block.gpsimd
            def _(pool):
                with pool.register(f"{tag}_passes") as passes:
                    pool.reg_load(passes, m.passes[0:1, 0:1])
                    pool.wait_ge(q["g_clear"], SETS)
                    bound = pool.to_reg(N - 1)
                    with pool.Fori(0, pool.snap(passes, min_val=1, max_val=MAX_CHUNKS // PAD)) as it:
                        pool.wait_ge(rec_in, it * 16 + 16)
                        pool.sem_inc(m.tick, 1)
                        for i in range(SETS):
                            pool.wait_ge(q["scaled_ready"], it * SETS + (i + 1))
                            pool.sem_inc(m.tick, 1)
                            for u in range(GROUP):
                                nc.gpsimd.indirect_dma_start(
                                    G[i][:, u * wide:(u + 1) * wide], None, table[:, :],
                                    bass.IndirectOffsetOnAxis(ap=rec[i][:, u, W_J:W_J + 1].bitcast(U32), axis=0),
                                    bounds_check=N - 1, oob_is_err=False).then_inc(gathered[i], 16)

            @block.scalar
            def _(act):
                with act.register(f"{tag}_passes") as passes:
                    act.reg_load(passes, m.passes[0:1, 0:1])
                    with act.Fori(0, act.snap(passes, min_val=1, max_val=MAX_CHUNKS // PAD)) as it:
                        for i in range(SETS):
                            act.wait_ge(q["turned"], it * SETS + (i + 1))
                            nc.scalar.activation(back[i][:, :], bank_back[i % 2][:, :], ACT.Copy).then_inc(q["turned_used"], 1)
                        for i in range(SETS):
                            act.wait_ge(q["max_ready"], it * SETS + (i + 1))
                            nc.scalar.activation(fade[i][:, :], growth[i][:, :], ACT.Exp).then_inc(q["growth_ready"], 1)
                        for i in range(SETS):
                            act.wait_ge(q["score_ready"], it * SETS + (i + 1))
                            nc.scalar.activation(wgt[i][:, :], zs[i][:, :], ACT.Exp).then_inc(q["weight_ready"], 1)

            @block.tensor
            def _(pe):
                with ExitStack() as rc:
                    passes = rc.enter_context(pe.register(f"{tag}_passes"))
                    regs = [[rc.enter_context(pe.register(f"{tag}_tile{i}{u}")) for u in range(GROUP)] for i in range(SETS)]
                    pe.reg_load(passes, m.passes[0:1, 0:1])
                    with pe.Fori(0, pe.snap(passes, min_val=1, max_val=MAX_CHUNKS // PAD)) as it:
                        tiles = []
                        pe.wait_ge(rec_in, it * 16 + 16)
                        pe.sem_inc(m.tick, 1)
                        for i in range(SETS):
                            tiles.append(tiles_of(pe, i, regs[i]))
                        pe.sem_inc(q["taken_pe"], 1)
                        for i in range(SETS):
                            if i >= 2:
                                pe.wait_ge(q["turned_used"], it * SETS + (i - 1))
                            pe.wait_ge(q["place_ready"], it * SETS + (i + 1))
                            for u in range(GROUP):
                                last = nc.tensor.transpose(bank_back[i % 2][:, u * P:(u + 1) * P], place[i][:, u * P:(u + 1) * P], m.ident[:, :])
                            last.then_inc(q["turned"], 1)
                        for i in range(SETS):
                            pe.wait_ge(q["turned_used"], it * SETS + (i + 1))
                            for u in range(GROUP):
                                last = nc.tensor.matmul(bank_small[i][:, u * row_width:(u + 1) * row_width],
                                                        back[i][:, u * P:(u + 1) * P], tile_of(row_table, tiles[i][u], row_width),
                                                        start=True, stop=True)
                            last.then_inc(q["own_ready"], 1)
                        for i in range(SETS):
                            pe.wait_ge(q["spread_ready"], it * SETS + (i + 1))
                            for u in range(GROUP):
                                last = nc.tensor.matmul(bank_small[i][:, c_slots + u * SLOTS * e1:c_slots + (u + 1) * SLOTS * e1],
                                                        place[i][:, u * P:(u + 1) * P],
                                                        spread[i][:, u * SLOTS * e1:(u + 1) * SLOTS * e1], start=True, stop=True)
                            last.then_inc(q["slots_ready"], 1)
                        for i in range(SETS):
                            pe.wait_ge(q["max_ready"], it * SETS + (i + 1))
                            for u in range(GROUP):
                                last = nc.tensor.matmul(bank_small[i][:, c_top + u * heads:c_top + (u + 1) * heads],
                                                        back[i][:, u * P:(u + 1) * P], newmax[i][:, u * heads:(u + 1) * heads],
                                                        start=True, stop=True)
                            last.then_inc(q["top_ready"], 1)
                        for i in range(SETS):
                            pe.wait_ge(q["scaled_ready"], it * SETS + (i + 1 + SETS))
                            for u in range(GROUP):
                                pe.wait_ge(q["merged"], it * PAD + (i * GROUP + u + 1))
                                nc.tensor.matmul(bank_sum[u][:, 0:hw], place[i][:, u * P:(u + 1) * P],
                                                 GW[i][:, u * hw:(u + 1) * hw], start=True, stop=True).then_inc(q["sum_ready"], 1)

            @block.vector
            def _(dve):
                with ExitStack() as rc:
                    passes = rc.enter_context(dve.register(f"{tag}_passes"))
                    regs = [[rc.enter_context(dve.register(f"{tag}_tile{i}{u}")) for u in range(GROUP)] for i in range(SETS)]
                    s = Steps(dve, m)
                    dve.reg_load(passes, m.passes[0:1, 0:1])
                    for i in range(SETS):
                        nc.vector.memset(G[i][:, :], 0.0).then_inc(q["g_clear"], 1)
                    s.done(nc.vector.memset(running[:, :], -NEVER))
                    s.done(nc.vector.memset(acc[:, :], 0.0))
                    dve.sem_inc(q["scaled_ready"], SETS)
                    dve.sem_inc(q["merged"], GROUP)
                    dve.sem_inc(q["taken_dve"], 1)
                    dve.sem_inc(q["taken_pe"], 1)
                    s.fold()
                    with dve.Fori(0, dve.snap(passes, min_val=1, max_val=MAX_CHUNKS // PAD)) as it:
                        tiles = []
                        dve.wait_ge(rec_in, it * 16 + 16)
                        dve.sem_inc(m.tick, 1)
                        for i in range(SETS):
                            half = rec[i].bitcast(BF16)
                            s.wait()
                            nc.vector.tensor_tensor(grouped(place[i], P), m.iota_row[:, None, :].broadcast_to([P, GROUP, P]),
                                                    half[:, :, H_ROW:H_ROW + 1].broadcast_to([P, GROUP, P]),
                                                    ALU.is_equal).then_inc(q["place_ready"], 1)
                            s.done(nc.vector.tensor_tensor(grouped(slot1[i], SLOTS), m.iota_row[:, None, 0:SLOTS].broadcast_to([P, GROUP, SLOTS]),
                                                           half[:, :, H_SLOT:H_SLOT + 1].broadcast_to([P, GROUP, SLOTS]), ALU.is_equal))
                        for i in range(SETS):
                            tiles.append(tiles_of(dve, i, regs[i]))
                        for i in range(SETS):
                            g3 = grouped(G[i], wide)
                            dve.wait_ge(gathered[i], it * (16 * GROUP) + 16 * GROUP)
                            dve.wait_ge(q["own_ready"], it * SETS + (i + 1))
                            own = bank_small[i][:, 0:GROUP * row_width].rearrange("p (u w) -> p u w", w=row_width)
                            if row_width == heads:
                                s.wait()
                                s.done(nc.vector.tensor_tensor(grouped(z[i], heads), own, g3[:, :, hw:hw + heads], ALU.add))
                            else:
                                s.wait()
                                s.done(nc.vector.tensor_tensor(grouped(prod[i], row_width), own, g3[:, :, hw:hw + row_width], ALU.mult))
                                s.wait()
                                s.done(nc.vector.tensor_reduce(z[i][:, :], grouped(prod[i], row_width), AX.X, ALU.add))
                            s.wait()
                            s.done(nc.vector.scalar_tensor_tensor(zl[i][:, :], z[i][:, :], slope, z[i][:, :], ALU.mult, ALU.max))
                            sp4 = spread[i][:, :].rearrange("p (u k e) -> p u k e", u=GROUP, e=e1)
                            hot = slot1[i][:, :].rearrange("p (u k o) -> p u k o", u=GROUP, o=1)
                            s.done(nc.vector.tensor_copy(sp4[:, :, :, heads:heads + 1], hot))
                            s.wait()
                            nc.vector.tensor_tensor(sp4[:, :, :, 0:heads], zl[i][:, :].rearrange("p (u o h) -> p u o h", u=GROUP, o=1)
                                                    .broadcast_to([P, GROUP, SLOTS, heads]),
                                                    hot.broadcast_to([P, GROUP, SLOTS, heads]), ALU.mult).then_inc(q["spread_ready"], 1)
                        dve.wait_ge(q["spread_ready"], it * SETS + SETS)
                        dve.sem_inc(q["taken_dve"], 1)
                        for i in range(SETS):
                            dve.wait_ge(q["slots_ready"], it * SETS + (i + 1))
                            el = bank_small[i][:, c_slots:c_top].rearrange("p (u k e) -> p u k e", u=GROUP, e=e1)
                            s.done(nc.vector.tensor_scalar(absent[i][:, :].rearrange("p (u k o) -> p u k o", u=GROUP, o=1),
                                                           el[:, :, :, heads:heads + 1], 1.0, NEVER, ALU.subtract, ALU.mult))
                            s.wait()
                            s.done(nc.vector.tensor_tensor(zm[i][:, :].rearrange("p (u h k) -> p u h k", u=GROUP, k=SLOTS),
                                                           el[:, :, :, 0:heads].rearrange("p u k h -> p u h k"),
                                                           absent[i][:, :].rearrange("p (u o k) -> p u o k", u=GROUP, o=1)
                                                           .broadcast_to([P, GROUP, heads, SLOTS]), ALU.add))
                            s.wait()
                            s.done(nc.vector.tensor_reduce(top[i][:, :], zm[i][:, :].rearrange("p (a k) -> p a k", k=SLOTS), AX.X, ALU.max))
                            for u in range(GROUP):
                                cols = slice(u * heads, (u + 1) * heads)
                                mine = tile_of(running, tiles[i][u], heads)
                                s.wait()
                                s.done(nc.vector.tensor_tensor(newmax[i][:, cols], mine, top[i][:, cols], ALU.max))
                                s.wait()
                                s.done(nc.vector.tensor_tensor(growth[i][:, cols], mine, newmax[i][:, cols], ALU.subtract))
                                s.wait()
                                ins = nc.vector.tensor_scalar(mine, newmax[i][:, cols], 0.0, None, ALU.add)
                                if u < GROUP - 1:
                                    s.done(ins)
                                else:
                                    ins.then_inc(q["max_ready"], 1)
                            dve.wait_ge(q["max_ready"], it * SETS + (i + 1))
                        for i in range(SETS):
                            dve.wait_ge(q["top_ready"], it * SETS + (i + 1))
                            s.done(nc.vector.tensor_tensor(z[i][:, :], zl[i][:, :], bank_small[i][:, c_top:c_top + GROUP * heads], ALU.subtract))
                            s.wait()
                            nc.vector.tensor_scalar(zs[i][:, :], z[i][:, :], 0.0, None, ALU.min).then_inc(q["score_ready"], 1)
                        for i in range(SETS):
                            dve.wait_ge(q["weight_ready"], it * SETS + (i + 1))
                            g3 = grouped(G[i], wide)
                            if heads == 1:
                                src = g3[:, :, 0:hw]
                                dst = grouped(GW[i], hw)
                                w = wgt[i][:, :].rearrange("p (u o) -> p u o", o=1).broadcast_to([P, GROUP, hw])
                            else:
                                src = g3[:, :, 0:hw].rearrange("p u (h d) -> p u h d", h=heads)
                                dst = GW[i][:, :].rearrange("p (u h d) -> p u h d", u=GROUP, h=heads)
                                w = wgt[i][:, :].rearrange("p (u h o) -> p u h o", u=GROUP, o=1).broadcast_to([P, GROUP, heads, width])
                            nc.vector.tensor_tensor(dst, src, w, ALU.mult).then_inc(q["scaled_ready"], 1)
                        for i in range(SETS):
                            dve.wait_ge(q["growth_ready"], it * SETS + (i + 1))
                            for u in range(GROUP):
                                mine = tile_of(acc, tiles[i][u], hw)
                                dve.wait_ge(q["merged"], it * PAD + (i * GROUP + u + GROUP))
                                if heads == 1:
                                    dve.wait_ge(q["sum_ready"], it * PAD + (i * GROUP + u + 1))
                                    ins = nc.vector.scalar_tensor_tensor(mine, mine, fade[i][:, u:u + 1], bank_sum[u][:, 0:hw], ALU.mult, ALU.add)
                                else:
                                    m3 = mine.rearrange("p (h d) -> p h d", h=heads)
                                    f = fade[i][:, u * heads:(u + 1) * heads].rearrange("p (h o) -> p h o", o=1).broadcast_to([P, heads, width])
                                    s.done(nc.vector.tensor_tensor(m3, m3, f, ALU.mult))
                                    dve.wait_ge(q["sum_ready"], it * PAD + (i * GROUP + u + 1))
                                    s.wait()
                                    ins = nc.vector.tensor_tensor(mine, mine, bank_sum[u][:, 0:hw], ALU.add)
                                ins.then_inc(q["merged"], 1)
                        dve.wait_ge(q["merged"], it * PAD + (PAD + GROUP))
                        dve.sem_inc(m.tick, 1)
                        s.fold()


def gather_sum(nc, m, sem, psum, tag, edges, table, width, acc):
    q = {n: sem(f"{tag}_{n}") for n in ["taken", "place_ready", "sum_ready", "merged", "g_clear"]}
    rec_in = sem(f"{tag}_rec_in")
    gathered = [sem(f"{tag}_gathered{i}") for i in range(SETS)]
    with ExitStack() as ctx:
        def sb(name, shape, dt=F32):
            return [ctx.enter_context(nc.sbuf_tensor(f"{tag}_{name}{i}", shape, dt)) for i in range(SETS)]
        rec_all = ctx.enter_context(nc.sbuf_tensor(f"{tag}_rec", [P, PAD, WORDS], I32))
        rec = [rec_all[:, i * GROUP:(i + 1) * GROUP, :] for i in range(SETS)]
        G = sb("G", [P, GROUP * width])
        place = sb("place", [P, GROUP * P])

        def bank(i, u):
            return psum[i % 2 * GROUP + u][:, 0:width]

        with nc.Block() as block:
            @block.sync
            def _(sp):
                with sp.register(f"{tag}_passes") as passes:
                    sp.reg_load(passes, m.passes[0:1, 0:1])
                    with sp.Fori(0, sp.snap(passes, min_val=1, max_val=MAX_CHUNKS // PAD)) as it:
                        sp.wait_ge(q["taken"], it + 1)
                        sp.wait_ge(q["sum_ready"], it * SETS + SETS)
                        sp.dma_start(rec_all[:, :, :], edges[:, bass.ds(it * PAD, PAD), :]).then_inc(rec_in, 16)

            @block.gpsimd
            def _(pool):
                with pool.register(f"{tag}_passes") as passes:
                    pool.reg_load(passes, m.passes[0:1, 0:1])
                    pool.wait_ge(q["g_clear"], SETS)
                    with pool.Fori(0, pool.snap(passes, min_val=1, max_val=MAX_CHUNKS // PAD)) as it:
                        pool.wait_ge(rec_in, it * 16 + 16)
                        pool.sem_inc(m.tick, 1)
                        for i in range(SETS):
                            pool.wait_ge(q["sum_ready"], it * SETS + (i + 1))
                            pool.sem_inc(m.tick, 1)
                            for u in range(GROUP):
                                nc.gpsimd.indirect_dma_start(
                                    G[i][:, u * width:(u + 1) * width], None, table[:, :],
                                    bass.IndirectOffsetOnAxis(ap=rec[i][:, u, W_J:W_J + 1].bitcast(U32), axis=0),
                                    bounds_check=N - 1, oob_is_err=False).then_inc(gathered[i], 16)

            @block.tensor
            def _(pe):
                with pe.register(f"{tag}_passes") as passes:
                    pe.reg_load(passes, m.passes[0:1, 0:1])
                    pe.sem_inc(q["sum_ready"], SETS)
                    with pe.Fori(0, pe.snap(passes, min_val=1, max_val=MAX_CHUNKS // PAD)) as it:
                        for i in range(SETS):
                            pe.wait_ge(q["place_ready"], it * SETS + (i + 1))
                            pe.wait_ge(gathered[i], it * (16 * GROUP) + 16 * GROUP)
                            pe.wait_ge(q["merged"], it * SETS + (i + 1))
                            for u in range(GROUP):
                                last = nc.tensor.matmul(bank(i, u), place[i][:, u * P:(u + 1) * P],
                                                        G[i][:, u * width:(u + 1) * width], start=True, stop=True)
                            last.then_inc(q["sum_ready"], 1)

            @block.vector
            def _(dve):
                with ExitStack() as rc:
                    passes = rc.enter_context(dve.register(f"{tag}_passes"))
                    regs = [[rc.enter_context(dve.register(f"{tag}_tile{i}{u}")) for u in range(GROUP)] for i in range(SETS)]
                    s = Steps(dve, m)
                    dve.reg_load(passes, m.passes[0:1, 0:1])
                    for i in range(SETS):
                        nc.vector.memset(G[i][:, :], 0.0).then_inc(q["g_clear"], 1)
                    s.done(nc.vector.memset(acc[:, :], 0.0))
                    dve.sem_inc(q["merged"], 2)
                    dve.sem_inc(q["taken"], 1)
                    s.fold()
                    with dve.Fori(0, dve.snap(passes, min_val=1, max_val=MAX_CHUNKS // PAD)) as it:
                        tiles = []
                        dve.wait_ge(rec_in, it * 16 + 16)
                        dve.sem_inc(m.tick, 1)
                        for i in range(SETS):
                            for u in range(GROUP):
                                dve.reg_load(regs[i][u], rec[i][0:1, u, W_TILE:W_TILE + 1])
                            tiles.append([dve.snap(r, min_val=0, max_val=NT - 1) for r in regs[i]])
                            half = rec[i].bitcast(BF16)
                            s.wait()
                            nc.vector.tensor_tensor(grouped(place[i], P), m.iota_row[:, None, :].broadcast_to([P, GROUP, P]),
                                                    half[:, :, H_ROW:H_ROW + 1].broadcast_to([P, GROUP, P]),
                                                    ALU.is_equal).then_inc(q["place_ready"], 1)
                        dve.wait_ge(q["place_ready"], it * SETS + SETS)
                        dve.sem_inc(q["taken"], 1)
                        for i in range(SETS):
                            s.wait()
                            dve.wait_ge(q["sum_ready"], it * SETS + (i + 1 + SETS))
                            for u in range(GROUP):
                                mine = tile_of(acc, tiles[i][u], width)
                                if u:
                                    s.wait()
                                ins = nc.vector.tensor_tensor(mine, mine, bank(i, u), ALU.add)
                                if u < GROUP - 1:
                                    s.done(ins)
                                else:
                                    ins.then_inc(q["merged"], 1)
                            dve.wait_ge(q["merged"], it * SETS + (i + 1 + 2))
                        s.fold()


def column_sums(nc, pe, out, ones, ready, offset, tile, done):
    pe.wait_ge(ready, offset + 1)
    nc.tensor.matmul(out, ones, tile(0), start=True, stop=False)
    with pe.Fori(1, NT - 1) as T:
        pe.wait_ge(ready, T + (offset + 1))
        nc.tensor.matmul(out, ones, tile(T), start=False, stop=False)
    pe.wait_ge(ready, offset + NT)
    nc.tensor.matmul(out, ones, tile(NT - 1), start=False, stop=True).then_inc(done, 1)


def after0(nc, m, sem, psum, acc):
    names = ["out_ready", "sum_ready", "centred", "squared", "square_ready", "var_ready", "root_ready", "scaled", "scaled_used", "norm_ready",
             "shift_ready", "h_ready", "turned", "turned_used", "hid_ready", "tanh_ready", "product", "product_used"]
    q = {n: sem("a0_" + n) for n in names}
    with ExitStack() as ctx:
        def sb(name, shape):
            return ctx.enter_context(nc.sbuf_tensor("a0_" + name, shape, F32))
        hb = [sb(f"hb{i}", [P, D]) for i in range(2)]
        hT = [sb(f"hT{i}", [P, 2 * P]) for i in range(2)]
        hid = [sb(f"hid{i}", [HID, P]) for i in range(2)]
        sq = [sb(f"sq{i}", [P, D]) for i in range(2)]
        bn = [sb(f"bn{i}", [P, D]) for i in range(2)]
        den = sb("den", [P, NT * HEADS])
        rden = sb("rden", [P, NT * HEADS])
        mean = sb("mean", [P, D])
        var = sb("var", [P, D])
        root = sb("root", [P, D])
        gain = sb("gain", [P, D])
        acc4 = acc[:, :].rearrange("p (t h d) -> p t h d", t=NT, h=HEADS)
        acc3 = acc[:, :].rearrange("p (a d) -> p a d", d=DH + 1)

        with nc.Block() as block:
            @block.tensor
            def _(pe):
                column_sums(nc, pe, psum[0][:, 0:D], m.ones[:, :], q["out_ready"], 0, lambda T: tile_of(m.hbuf, T, D), q["sum_ready"])
                with pe.Fori(0, NT // 2) as t2:
                    for i in range(2):
                        pe.wait_ge(q["squared"], t2 * 2 + (i + 3))
                        nc.tensor.matmul(psum[1][:, 0:D], m.ones[:, :], sq[i][:, :], start=True, stop=True).then_inc(q["square_ready"], 1)
                        pe.wait_ge(q["norm_ready"], t2 * 2 + (i + 1))
                with pe.Fori(0, NT // 2) as t2:
                    for i in range(2):
                        n = t2 * 2 + (i + 1)
                        pe.wait_ge(q["h_ready"], n)
                        for c in range(2):
                            last = nc.tensor.transpose(psum[i][:, c * P:c * P + P], hb[i][:, c * P:c * P + P], m.ident[:, :])
                        last.then_inc(q["turned"], 1)
                        pe.wait_ge(q["turned_used"], n)
                        for c in range(2):
                            last = nc.tensor.matmul(psum[2 + i][0:HID, 0:P], m.Wx1[:, c, :], hT[i][:, c * P:c * P + P],
                                                    start=(c == 0), stop=(c == 1))
                        last.then_inc(q["hid_ready"], 1)
                        pe.wait_ge(q["product_used"], n)
                        for c in range(2):
                            nc.tensor.matmul(psum[4 + i][:, HID:HID + OUT1], hT[i][:, c * P:c * P + P], m.Wfx[:, c, :], start=(c == 0), stop=False)
                        nc.tensor.matmul(psum[4 + i][:, HID:HID + OUT1], m.ones[0:1, :], m.bias_x[0:1, HID:HID + OUT1], start=False, stop=True)
                        pe.wait_ge(q["tanh_ready"], n)
                        nc.tensor.matmul(psum[4 + i][:, 0:HID], hid[i][:, :], m.Wx2[:, :], start=True, stop=False)
                        nc.tensor.matmul(psum[4 + i][:, 0:HID], m.ones[0:1, :], m.bias_x[0:1, 0:HID],
                                         start=False, stop=True).then_inc(q["product"], 1)

            @block.scalar
            def _(act):
                act.sem_inc(q["squared"], 2)
                with act.Fori(0, NT // 2) as t2:
                    for i in range(2):
                        act.wait_ge(q["centred"], t2 * 2 + (i + 1))
                        act.sem_inc(m.tick, 1)
                        nc.scalar.activation(sq[i][:, :], tile_of(m.hbuf, t2 * 2 + i, D), ACT.Square).then_inc(q["squared"], 1)
                        act.wait_ge(q["norm_ready"], t2 * 2 + (i + 1))
                        act.sem_inc(m.tick, 1)
                act.wait_ge(q["var_ready"], 1)
                nc.scalar.activation(root[:, :], var[:, :], ACT.Sqrt).then_inc(q["root_ready"], 1)
                act.wait_ge(q["var_ready"], 2)
                nc.scalar.activation(m.root[:, :], m.var[:, :], ACT.Sqrt).then_inc(q["root_ready"], 1)
                act.wait_ge(q["shift_ready"], 1)
                with act.Fori(0, NT // 2) as t2:
                    for i in range(2):
                        n = t2 * 2 + (i + 1)
                        T = t2 * 2 + i
                        act.sem_inc(m.tick, 1)
                        nc.scalar.activation(hb[i][:, :], tile_of(m.x, T, D), ACT.Relu, scale=m.rstd[:, bass.ds(T, 1)],
                                             bias=m.shift[:, bass.ds(T, 1)]).then_inc(q["h_ready"], 1)
                        act.wait_ge(q["turned"], n)
                        nc.scalar.activation(hT[i][:, :], psum[i][:, 0:2 * P], ACT.Copy).then_inc(q["turned_used"], 1)
                        act.wait_ge(q["hid_ready"], n)
                        nc.scalar.activation(hid[i][:, :], psum[2 + i][0:HID, 0:P], ACT.Tanh, bias=m.bx1[:, :]).then_inc(q["tanh_ready"], 1)

            @block.gpsimd
            def _(pool):
                pool.wait_ge(q["scaled_used"], 1)
                with pool.Fori(0, NT // 2) as t2:
                    for i in range(2):
                        pool.wait_ge(q["scaled_used"], t2 * 2 + (i + 1))
                        pool.sem_inc(m.tick, 1)
                        nc.gpsimd.tensor_tensor(bn[i][:, :], tile_of(m.hbuf, t2 * 2 + i, D), gain[:, :], ALU.mult).then_inc(q["scaled"], 1)

            @block.vector
            def _(dve):
                s = Steps(dve, m)
                s.done(nc.vector.tensor_scalar(m.empty[:, :], m.degree[:, :], 0.0, None, ALU.is_equal))
                s.wait()
                s.done(nc.vector.tensor_tensor(den[:, :].rearrange("p (t h o) -> p t h o", t=NT, o=1), acc4[:, :, :, DH:DH + 1],
                                               m.empty[:, :].rearrange("p (t h o) -> p t h o", h=1, o=1).broadcast_to([P, NT, HEADS, 1]), ALU.add))
                s.wait()
                s.done(nc.vector.reciprocal(rden[:, :], den[:, :]))
                s.wait()
                s.done(nc.vector.tensor_tensor(m.hbuf[:, :].rearrange("p (a d) -> p a d", d=DH), acc3[:, :, 0:DH],
                                               rden[:, :].rearrange("p (a o) -> p a o", o=1).broadcast_to([P, NT * HEADS, DH]), ALU.mult))
                s.fold()
                with dve.Fori(0, NT) as T:
                    mine = tile_of(m.hbuf, T, D).rearrange("p (h d) -> p h d", h=HEADS)
                    s.wait()
                    nc.vector.scalar_tensor_tensor(mine, m.mean0[:, :].rearrange("p (h d) -> p h d", h=HEADS)[:, :, 0:DH],
                                                   m.empty[:, bass.ds(T, 1)], mine, ALU.mult, ALU.add).then_inc(q["out_ready"], 1)
                dve.wait_ge(q["sum_ready"], 1)
                s.done(nc.vector.tensor_scalar(mean[:, :], psum[0][:, 0:D], 1.0 / N, None, ALU.mult))
                s.done(nc.vector.memset(var[:, :], 0.0))
                s.fold()
                with dve.Fori(0, NT // 2) as t2:
                    for i in range(2):
                        n = t2 * 2 + (i + 1)
                        s.wait()
                        mine = tile_of(m.hbuf, t2 * 2 + i, D)
                        nc.vector.tensor_tensor(mine, mine, mean[:, :], ALU.subtract).then_inc(q["centred"], 1)
                        dve.wait_ge(q["square_ready"], n)
                        nc.vector.tensor_tensor(var[:, :], var[:, :], psum[1][:, 0:D], ALU.add).then_inc(q["norm_ready"], 1)
                        dve.wait_ge(q["norm_ready"], n)
                        dve.sem_inc(m.tick, 1)
                s.done(nc.vector.tensor_scalar(var[:, :], var[:, :], 1.0 / N, EPS, ALU.mult, ALU.add))
                s.wait()
                dve.sem_inc(q["var_ready"], 1)
                dve.wait_ge(q["root_ready"], 1)
                s.done(nc.vector.reciprocal(mean[:, :], root[:, :]))
                s.wait()
                s.done(nc.vector.tensor_tensor(gain[:, :], mean[:, :], m.norm[:, 0:D], ALU.mult))
                s.wait()
                dve.sem_inc(q["scaled_used"], 2)
                s.fold()
                with dve.Fori(0, NT // 2) as t2:
                    for i in range(2):
                        n = t2 * 2 + (i + 1)
                        T = t2 * 2 + i
                        mine = tile_of(m.x, T, D)
                        s.wait()
                        dve.wait_ge(q["scaled"], n)
                        s.done(nc.vector.tensor_tensor(bn[i][:, :], bn[i][:, :], m.norm[:, D:2 * D], ALU.add))
                        s.wait()
                        nc.vector.scalar_tensor_tensor(mine, bn[i][:, :], 0.0, mine, ALU.max, ALU.add).then_inc(q["scaled_used"], 1)
                        s.fold()
                dve.wait_ge(q["scaled_used"], NT + 2)
                x_stats(nc, m, s)
                layernorm_scale(nc, m, s, q["var_ready"], q["root_ready"], 2)
                dve.sem_inc(q["shift_ready"], 1)
                dve.sem_inc(q["product_used"], 2)
                s.fold()
                with dve.Fori(0, NT // 2) as t2:
                    for i in range(2):
                        T = t2 * 2 + i
                        s.wait()
                        dve.wait_ge(q["product"], t2 * 2 + (i + 1))
                        s.done(nc.vector.tensor_copy(tile_of(m.row1, T, HID), psum[4 + i][:, 0:HID]))
                        mine = m.x[:, bass.ds(T * D, OUT1)]
                        nc.vector.tensor_tensor(mine, mine, psum[4 + i][:, HID:HID + OUT1], ALU.add).then_inc(q["product_used"], 1)
                        s.fold()


def after1(nc, m, sem, acc, table2):
    q = {n: sem("a1_" + n) for n in ["var_ready", "root_ready", "shift_ready", "h_ready", "stored"]}
    with ExitStack() as ctx:
        den = ctx.enter_context(nc.sbuf_tensor("a1_den", [P, NT], F32))
        rden = ctx.enter_context(nc.sbuf_tensor("a1_rden", [P, NT], F32))
        parts = 4
        each = NT // parts
        with nc.Block() as block:
            @block.scalar
            def _(act):
                act.wait_ge(q["var_ready"], 1)
                nc.scalar.activation(m.root[:, :], m.var[:, :], ACT.Sqrt).then_inc(q["root_ready"], 1)
                act.wait_ge(q["shift_ready"], 1)
                with act.Fori(0, NT) as T:
                    act.sem_inc(m.tick, 1)
                    nc.scalar.activation(tile_of(m.hbuf, T, D), tile_of(m.x, T, D), ACT.Relu, scale=m.rstd[:, bass.ds(T, 1)],
                                         bias=m.shift[:, bass.ds(T, 1)]).then_inc(q["h_ready"], 1)

            @block.sync
            def _(sp):
                for i in range(parts):
                    sp.wait_ge(q["h_ready"], (i + 1) * each)
                    sp.dma_start(table2[i * each * P:(i + 1) * each * P, :].rearrange("(t p) d -> p t d", p=P),
                                 m.hbuf[:, i * each * D:(i + 1) * each * D].rearrange("p (t d) -> p t d", d=D)).then_inc(q["stored"], 16)
                sp.wait_ge(q["stored"], 16 * parts)

            @block.vector
            def _(dve):
                s = Steps(dve, m)
                acc3 = acc[:, :].rearrange("p (t w) -> p t w", w=H1)
                s.done(nc.vector.tensor_tensor(den[:, :].rearrange("p (t o) -> p t o", o=1), acc3[:, :, OUT1:H1],
                                               m.empty[:, :].rearrange("p (t o) -> p t o", o=1), ALU.add))
                s.wait()
                s.done(nc.vector.reciprocal(rden[:, :], den[:, :]))
                s.fold()
                with dve.Fori(0, NT) as T:
                    mine = m.x[:, bass.ds(T * D + OUT1, OUT1)]
                    s.wait()
                    s.done(nc.vector.scalar_tensor_tensor(mine, acc[:, bass.ds(T * H1, OUT1)], rden[:, bass.ds(T, 1)], mine, ALU.mult, ALU.add))
                    s.wait()
                    s.done(nc.vector.scalar_tensor_tensor(mine, m.mean1[:, 0:OUT1], m.empty[:, bass.ds(T, 1)], mine, ALU.mult, ALU.add))
                    s.fold()
                s.wait()
                dve.sem_inc(m.tick, 1)
                x_stats(nc, m, s)
                layernorm_scale(nc, m, s, q["var_ready"], q["root_ready"], 1)
                dve.sem_inc(q["shift_ready"], 1)


def after2(nc, m, sem, psum, acc, table3):
    names = ["mean_ready", "pair_ready", "turned", "turned_used", "product", "product_used", "var_ready", "root_ready", "shift_ready", "h_ready",
             "turned3", "turned3_used", "product3", "product3_used", "column", "column_turned", "column_ready", "stored"]
    q = {n: sem("a2_" + n) for n in names}
    with ExitStack() as ctx:
        def sb(name, shape):
            return ctx.enter_context(nc.sbuf_tensor("a2_" + name, shape, F32))
        pair = [sb(f"pair{i}", [P, 2 * D]) for i in range(2)]
        pairT = [sb(f"pairT{i}", [P, 2 * D]) for i in range(2)]
        rdeg = sb("rdeg", [P, NT])
        deg1 = sb("deg1", [P, NT])
        col = sb("col", [P, NT])
        colT = sb("colT", [NT, P])
        with nc.Block() as block:
            @block.sync
            def _(sp):
                sp.wait_ge(q["column_ready"], 1)
                sp.dma_start(table3.rearrange("(t p) o -> t (p o)", p=P), colT[:, :]).then_inc(q["stored"], 16)
                sp.wait_ge(q["stored"], 16)

            @block.scalar
            def _(act):
                act.wait_ge(q["mean_ready"], 1)
                act.sem_inc(q["pair_ready"], 2)
                with act.Fori(0, NT // 2) as t2:
                    for i in range(2):
                        n = t2 * 2 + (i + 1)
                        T = t2 * 2 + i
                        act.wait_ge(q["turned_used"], n)
                        act.sem_inc(m.tick, 1)
                        nc.scalar.activation(pair[i][:, 0:D], tile_of(m.hbuf, T, D), ACT.Copy)
                        nc.scalar.activation(pair[i][:, D:2 * D], tile_of(acc, T, D), ACT.Copy, scale=rdeg[:, bass.ds(T, 1)]).then_inc(q["pair_ready"], 1)
                act.wait_ge(q["var_ready"], 1)
                nc.scalar.activation(m.root[:, :], m.var[:, :], ACT.Sqrt).then_inc(q["root_ready"], 1)
                act.wait_ge(q["shift_ready"], 1)
                with act.Fori(0, NT // 2) as t2:
                    for i in range(2):
                        n = t2 * 2 + (i + 1)
                        T = t2 * 2 + i
                        act.wait_ge(q["column"], n)
                        act.sem_inc(m.tick, 1)
                        nc.scalar.activation(pair[i][:, 0:D], tile_of(m.x, T, D), ACT.Relu, scale=m.rstd[:, bass.ds(T, 1)],
                                             bias=m.shift[:, bass.ds(T, 1)]).then_inc(q["h_ready"], 1)
                        act.wait_ge(q["turned3"], n)
                        nc.scalar.activation(pairT[i][:, 0:D], psum[i][:, 0:D], ACT.Copy).then_inc(q["turned3_used"], 1)

            @block.tensor
            def _(pe):
                with pe.Fori(0, NT // 2) as t2:
                    for i in range(2):
                        n = t2 * 2 + (i + 1)
                        pe.wait_ge(q["pair_ready"], n + 2)
                        for c in range(4):
                            last = nc.tensor.transpose(psum[i][:, c * P:c * P + P], pair[i][:, c * P:c * P + P], m.ident[:, :])
                        last.then_inc(q["turned"], 1)
                        pe.wait_ge(q["turned_used"], n + 2)
                        pe.wait_ge(q["product_used"], n)
                        for c in range(4):
                            w = (m.W2s, m.W2n)[c // 2][:, c % 2, :]
                            nc.tensor.matmul(psum[2 + i][:, 0:D], pairT[i][:, c * P:c * P + P], w, start=(c == 0), stop=False)
                        nc.tensor.matmul(psum[2 + i][:, 0:D], m.ones[0:1, :], m.bias_2[:, :], start=False, stop=True).then_inc(q["product"], 1)
                with pe.Fori(0, NT // 2) as t2:
                    for i in range(2):
                        n = t2 * 2 + (i + 1)
                        pe.wait_ge(q["h_ready"], n)
                        for c in range(2):
                            last = nc.tensor.transpose(psum[i][:, c * P:c * P + P], pair[i][:, c * P:c * P + P], m.ident[:, :])
                        last.then_inc(q["turned3"], 1)
                        pe.wait_ge(q["turned3_used"], n)
                        pe.wait_ge(q["product3_used"], n)
                        for c in range(2):
                            last = nc.tensor.matmul(psum[2 + i][:, 0:D], pairT[i][:, c * P:c * P + P], m.S3T[:, c, :], start=(c == 0), stop=(c == 1))
                        last.then_inc(q["product3"], 1)
                pe.wait_ge(q["column"], NT + 2)
                nc.tensor.matmul(psum[4][0:NT, 0:P], col[:, :], m.ident[:, :], start=True, stop=True).then_inc(q["column_turned"], 1)

            @block.vector
            def _(dve):
                s = Steps(dve, m)
                s.done(nc.vector.tensor_scalar(deg1[:, :], m.degree[:, :], 1.0, None, ALU.max))
                s.wait()
                nc.vector.reciprocal(rdeg[:, :], deg1[:, :]).then_inc(q["mean_ready"], 1)
                dve.sem_inc(q["turned_used"], 2)
                dve.sem_inc(q["product_used"], 2)
                s.fold()
                with dve.Fori(0, NT // 2) as t2:
                    for i in range(2):
                        n = t2 * 2 + (i + 1)
                        T = t2 * 2 + i
                        mine = tile_of(m.x, T, D)
                        dve.wait_ge(q["turned"], n)
                        nc.vector.tensor_copy(pairT[i][:, :], psum[i][:, :]).then_inc(q["turned_used"], 1)
                        dve.wait_ge(q["product"], n)
                        nc.vector.scalar_tensor_tensor(mine, psum[2 + i][:, 0:D], 0.0, mine, ALU.max, ALU.add).then_inc(q["product_used"], 1)
                        s.fold()
                dve.wait_ge(q["product_used"], NT + 2)
                x_stats(nc, m, s)
                layernorm_scale(nc, m, s, q["var_ready"], q["root_ready"], 1)
                dve.sem_inc(q["shift_ready"], 1)
                dve.sem_inc(q["product3_used"], 2)
                dve.sem_inc(q["column"], 2)
                with dve.Fori(0, NT // 2) as t2:
                    for i in range(2):
                        n = t2 * 2 + (i + 1)
                        T = t2 * 2 + i
                        dve.wait_ge(q["h_ready"], n)
                        nc.vector.tensor_copy(col[:, bass.ds(T, 1)], pair[i][:, 0:1]).then_inc(q["column"], 1)
                        dve.wait_ge(q["product3"], n)
                        nc.vector.tensor_copy(tile_of(m.hbuf, T, D), psum[2 + i][:, 0:D]).then_inc(q["product3_used"], 1)
                dve.wait_ge(q["column_turned"], 1)
                nc.vector.tensor_copy(colT[:, :], psum[4][0:NT, 0:P]).then_inc(q["column_ready"], 1)


def after3(nc, m, sem, acc, out):
    q = {n: sem("a3_" + n) for n in ["x_ready", "stored"]}
    parts = 4
    each = NT // parts
    with nc.Block() as block:
        @block.sync
        def _(sp):
            for i in range(parts):
                sp.wait_ge(q["x_ready"], (i + 1) * each)
                sp.dma_start(out[i * each * P:(i + 1) * each * P, :].rearrange("(t p) d -> p t d", p=P),
                             m.x[:, i * each * D:(i + 1) * each * D].rearrange("p (t d) -> p t d", d=D)).then_inc(q["stored"], 16)
            sp.wait_ge(q["stored"], 16 * parts)

        @block.vector
        def _(dve):
            s = Steps(dve, m)
            with dve.Fori(0, NT) as T:
                mine = tile_of(m.x, T, D)
                own = tile_of(m.hbuf, T, D)
                s.done(nc.vector.scalar_tensor_tensor(own, m.neigh_sum[:, :], acc[:, bass.ds(T, 1)], own, ALU.mult, ALU.add))
                s.wait()
                nc.vector.scalar_tensor_tensor(mine, own, 0.0, mine, ALU.max, ALU.add).then_inc(q["x_ready"], 1)
                s.fold()


def build(nc, a, out):
    def scratch(name, shape, dt=F32):
        return nc.dram_tensor(name, shape, dt, kind="Internal").ap()
    edges = scratch("edges", (P, MAX_CHUNKS, WORDS), I32)
    table0 = scratch("table0", (N, ROW0))
    table1 = scratch("table1", (N, ROW1))
    table2 = scratch("table2", (N, D))
    table3 = scratch("table3", (N, 1))
    with ExitStack() as ctx:
        m = Mem()
        def sem(name):
            return ctx.enter_context(nc.semaphore(name))
        def keep(name, shape, dt=F32):
            return ctx.enter_context(nc.sbuf_tensor(name, shape, dt))
        m.iota_row_i = keep("iota_row_i", [P, P], I32)
        m.iota_col_i = keep("iota_col_i", [P, 1], I32)
        m.iota_row = keep("iota_row", [P, P])
        m.iota_col = keep("iota_col", [P, 1])
        m.ident = keep("ident", [P, P])
        m.tri = keep("tri", [P, P])
        m.ones = keep("ones", [P, P])
        m.degree = keep("degree", [P, NT])
        m.passes = keep("passes", [P, 1], I32)
        m.x = keep("x", [P, NT * D])
        m.hbuf = keep("hbuf", [P, NT * D])
        m.acc = keep("acc", [P, NT * H0])
        m.W0T = keep("W0T", [P, 2, D + 2 * HEADS])
        m.Wx1 = keep("Wx1", [P, 2, HID])
        m.Wx2 = keep("Wx2", [HID, HID])
        m.Wn1 = keep("Wn1", [P, 2, HID])
        m.Wn2 = keep("Wn2", [HID, HID])
        m.Wv = keep("Wv", [P, 2, OUT1])
        m.Wfx = keep("Wfx", [P, 2, OUT1])
        m.W2s = keep("W2s", [P, 2, D])
        m.W2n = keep("W2n", [P, 2, D])
        m.S3T = keep("S3T", [P, 2, D])
        m.bias_n = keep("bias_n", [1, OUT1 + HID])
        m.bias_x = keep("bias_x", [1, OUT1 + HID])
        m.norm_in = keep("norm_in", [1, 2 * D])
        m.norm = keep("norm", [P, 2 * D])
        m.bias_2 = keep("bias_2", [1, D])
        m.neigh_sum = keep("neigh_sum", [P, D])
        m.bx1 = keep("bx1", [HID, 1])
        m.bn1 = keep("bn1", [HID, 1])
        m.stats = keep("stats", [P, NT * 6])
        m.mean_sum = keep("mean_sum", [P, NT])
        m.mean_gap = keep("mean_gap", [P, NT])
        m.dev_sum = keep("dev_sum", [P, NT])
        m.var = keep("var", [P, NT])
        m.root = keep("root", [P, NT])
        m.rstd = keep("rstd", [P, NT])
        m.shift = keep("shift", [P, NT])
        m.score_i = keep("score_i", [P, NT * HEADS])
        m.row1 = keep("row1", [P, NT * HID])
        m.mean0 = keep("mean0", [P, H0])
        m.mean1 = keep("mean1", [P, ROW1])
        m.empty = keep("empty", [P, NT])
        m.running = keep("running", [P, NT * HEADS])
        psum = [ctx.enter_context(nc.psum_tensor(f"bank{i}", [P, 512], F32)) for i in range(8)]
        m.tick = sem("tick")
        m.vec_steps = sem("vec_steps")
        m.vec_open = 0
        m.vec_count = ctx.enter_context(nc.vector.register("vec_count"))
        constants(nc, m, sem)
        weights(nc, m, sem, psum, a)
        scan(nc, m, sem, psum, a["adj"], edges, a["L1_gnn_neigh"], table0, table1)
        attend(nc, m, sem, psum, "l0", edges, table0, HEADS, DH + 1, HEADS, m.score_i, HEADS, 0.2, m.running, m.acc)
        after0(nc, m, sem, psum, m.acc)
        acc1 = m.acc[:, 0:NT * H1]
        attend(nc, m, sem, psum, "l1", edges, table1, 1, H1, HID, m.row1, HID, 0.01, m.running[:, 0:NT], acc1)
        after1(nc, m, sem, acc1, table2)
        acc2 = m.acc[:, 0:NT * D]
        gather_sum(nc, m, sem, psum, "l2", edges, table2, D, acc2)
        after2(nc, m, sem, psum, acc2, table3)
        acc3 = m.acc[:, 0:NT]
        gather_sum(nc, m, sem, psum, "l3", edges, table3, 1, acc3)
        after3(nc, m, sem, acc3, out)


_INS = ["x", "adj", "L0_gnn_W", "L0_gnn_a", "L0_gnn_gamma", "L0_gnn_beta", "L1_gnn_neigh", "L1_gnn_Wx1", "L1_gnn_bx1", "L1_gnn_Wx2",
        "L1_gnn_bx2", "L1_gnn_Wn1", "L1_gnn_bn1", "L1_gnn_Wn2", "L1_gnn_bn2", "L1_gnn_Wv", "L1_gnn_bv", "L1_gnn_Wfx", "L1_gnn_bfx",
        "L2_gnn_W_self", "L2_gnn_b_self", "L2_gnn_W_nb", "L2_gnn_b_nb", "L2_gnn_W_comb", "L2_gnn_b_comb", "L3_gnn_w_self",
        "L3_gnn_w_neigh"]


def kernel(**inputs):
    import numpy as _np
    import concourse.bacc as _bacc
    from concourse import mybir as _mybir
    from concourse.bass_utils import run_bass_kernel_spmd as _run

    nc = _bacc.Bacc("TRN2", target_bir_lowering=False, num_devices=1)
    arrays, args = {}, {}
    for name in _INS:
        a = _np.ascontiguousarray(inputs[name])
        arrays[f"in_{name}_dram"] = a
        args[name] = nc.dram_tensor(f"in_{name}_dram", a.shape, _mybir.dt.from_np(a.dtype), kind="ExternalInput").ap()
    out = nc.dram_tensor("out_0_dram", (N, D), F32, kind="ExternalOutput").ap()
    build(nc, args, out)
    r = _run(nc, [arrays], core_ids=[0])
    return r.results[0]["out_0_dram"]
```

```python
from contextlib import ExitStack

import concourse.bass as bass
from concourse import mybir

ALU = mybir.AluOpType
ACT = mybir.ActivationFunctionType
F32 = mybir.dt.float32
BF16 = mybir.dt.bfloat16
I32 = mybir.dt.int32
U32 = mybir.dt.uint32
AX = mybir.AxisListType

P = 128
N = 4096
D = 256
NT = N // P
SLOTS = 8
ITEM_CHUNKS = SLOTS
GROUP = 4
SETS = 4
PAD = GROUP * SETS
TURNS = 2 * SETS
SPARE = 3 * PAD
MAX_CHUNKS = NT * (N // SLOTS) * ITEM_CHUNKS + SPARE
MAX_PASSES = MAX_CHUNKS // PAD - 2
WORDS = 3
HEADS = 8
DH = D // HEADS
HID = 32
OUT1 = 128
H0 = HEADS * (DH + 1)
ROW0 = H0 + HEADS
H1 = OUT1 + 1
ROW1 = H1 + HID
EPS = 1e-5
NEVER = 9e15
BUFS = 4
HALF = 4
INFO = 12
I_START, I_END, I_ROW, I_ONE = 8, 9, 10, 11
W_J, W_TILE = 0, 2
H_ROW, H_SLOT = 2, 3
NOWHERE = 2 * N


class Steps:

    def __init__(self, eng, m):
        self.eng, self.m, self.sem, self.reg = eng, m, m.vec_steps, m.vec_count

    def done(self, ins):
        ins.then_inc(self.sem, 1)
        self.m.vec_open += 1
        return ins

    def wait(self, back=0):
        self.eng.wait_ge(self.sem, self.eng.snap(self.reg) + (self.m.vec_open - back))

    def fold(self):
        if self.m.vec_open:
            self.eng.reg_add(self.reg, self.reg, self.m.vec_open)
        self.m.vec_open = 0


class Mem:
    pass


def constants(nc, m, sem):
    const_iota = sem("const_iota")
    const_base = sem("const_base")
    const_done = sem("const_done")
    with nc.Block() as block:
        @block.gpsimd
        def _(pool):
            nc.gpsimd.iota(m.iota_row_i[:, :], pattern=[[1, P]], base=0, channel_multiplier=0).then_inc(const_iota, 1)
            nc.gpsimd.iota(m.iota_col_i[:, :], pattern=[[1, 1]], base=0, channel_multiplier=1).then_inc(const_iota, 1)
            nc.gpsimd.memset(m.ident[:, :], 0.0).then_inc(const_base, 1)
            nc.gpsimd.memset(m.tri[:, :], 1.0).then_inc(const_base, 1)
            nc.gpsimd.memset(m.ones[:, :], 1.0)
            nc.gpsimd.memset(m.gathered_rows[:, :], 0.0)
            pool.wait_ge(const_base, 2)
            nc.gpsimd.affine_select(out=m.ident[:, :], in_=m.ident[:, :], compare_op=ALU.not_equal, fill=1.0,
                                    base=0, pattern=[[-1, P]], channel_multiplier=1).then_inc(const_done, 1)
            nc.gpsimd.affine_select(out=m.tri[:, :], in_=m.tri[:, :], compare_op=ALU.is_gt, fill=0.0,
                                    base=0, pattern=[[1, P]], channel_multiplier=-1)

        @block.vector
        def _(dve):
            dve.reg_mov(m.vec_count, 0)
            dve.wait_ge(const_iota, 2)
            nc.vector.tensor_copy(m.iota_row[:, :], m.iota_row_i[:, :])
            nc.vector.tensor_copy(m.iota_row_h[:, :], m.iota_row_i[:, :])
            nc.vector.tensor_copy(m.iota_col[:, :], m.iota_col_i[:, :])
            dve.wait_ge(const_done, 1)
            nc.vector.tensor_copy(m.ident_h[:, :], m.ident[:, :])


def tile_of(t, number, width):
    return t[:, bass.ds(number * width, width)]


def x_stats(nc, m, s, unroll=4, first=0, tiles=NT):
    with s.eng.Fori(0, tiles // unroll) as t:
        for k in range(unroll):
            T = t * unroll + (first + k)
            s.done(nc.vector.bn_stats(tile_of(m.stats, T, 6), tile_of(m.x, T, D)))
        s.fold()


def layernorm_scale(nc, m, s, number, first=0, tiles=NT):
    stat = m.stats[:, first * 6:(first + tiles) * 6].rearrange("p (t c) -> p t c", c=6)
    mean_sum, mean_gap, dev_sum, var, root, rstd, shift = (t[:, first:first + tiles] for t in (m.mean_sum, m.mean_gap, m.dev_sum, m.var, m.root, m.rstd, m.shift))
    s.wait()
    s.done(nc.vector.tensor_tensor(mean_sum, stat[:, :, 1], stat[:, :, 4], ALU.add))
    s.done(nc.vector.tensor_tensor(mean_gap, stat[:, :, 1], stat[:, :, 4], ALU.subtract))
    s.done(nc.vector.tensor_tensor(dev_sum, stat[:, :, 2], stat[:, :, 5], ALU.add))
    s.wait()
    s.done(nc.vector.tensor_tensor(mean_gap, mean_gap, mean_gap, ALU.mult))
    s.wait()
    s.done(nc.vector.scalar_tensor_tensor(dev_sum, mean_gap, D / 4, dev_sum, ALU.mult, ALU.add))
    s.wait()
    nc.vector.tensor_scalar(var, dev_sum, 1.0 / D, EPS, ALU.mult, ALU.add).then_inc(m.ln_var_ready, 1)
    s.eng.wait_ge(m.ln_root_ready, number)
    s.done(nc.vector.reciprocal(rstd, root))
    s.wait()
    s.done(nc.vector.scalar_tensor_tensor(shift, mean_sum, -0.5, rstd, ALU.mult, ALU.mult))
    s.wait()


def weights(nc, m, sem, psum, a):
    w_in = sem("w_in")
    w_turned = sem("w_turned")
    w_used = sem("w_used")
    w_folded = sem("w_folded")
    w_steps = sem("w_steps")
    heads_ready = sem("heads_ready")
    x_in = [sem(f"x_in{i}") for i in range(4)]
    n = {"in": 0}
    with ExitStack() as ctx:
        def sb(name, shape):
            return ctx.enter_context(nc.sbuf_tensor(name, shape, F32))
        W0 = sb("W0", [P, 2, D])
        Ws = sb("Ws", [P, 2, D])
        Wn = sb("Wn", [P, 2, D])
        Wc = sb("Wc", [P, 4, D])
        S3 = sb("S3", [P, 2, D])
        N3 = sb("N3", [P, 2, D])
        WsT = sb("WsT", [P, 2, D])
        WnT = sb("WnT", [P, 2, D])
        N3T = sb("N3T", [P, 2, D])
        acol = sb("acol", [P, 2])
        heads = sb("heads", [P, 2, 2 * HEADS])
        bcol = sb("bcol", [P, 2, 2])
        bcomb = sb("bcomb", [1, D])
        folded = lambda w: w.rearrange("(c p) n -> p c n", p=P)
        loads = [(W0[:, :, :], folded(a["L0_gnn_W"])), (Ws[:, :, :], folded(a["L2_gnn_W_self"])),
                 (Wn[:, :, :], folded(a["L2_gnn_W_nb"])), (Wc[:, :, :], folded(a["L2_gnn_W_comb"])),
                 (S3[:, :, :], folded(a["L3_gnn_w_self"])), (N3[:, :, :], folded(a["L3_gnn_w_neigh"])),
                 (m.Wx1[:, :, :], folded(a["L1_gnn_Wx1"])), (m.Wn1[:, :, :], folded(a["L1_gnn_Wn1"])),
                 (m.Wv[:, :, :], folded(a["L1_gnn_Wv"])), (m.Wfx[:, :, :], folded(a["L1_gnn_Wfx"])),
                 (m.Wx2[:, :], a["L1_gnn_Wx2"]), (m.Wn2[:, :], a["L1_gnn_Wn2"]),
                 (m.bias_n[0:1, 0:OUT1], a["L1_gnn_bv"][None, :]), (m.bias_n[0:1, OUT1:OUT1 + HID], a["L1_gnn_bn2"][None, :]),
                 (m.bias_x[0:1, 0:HID], a["L1_gnn_bx2"][None, :]), (m.bias_x[0:1, HID:HID + OUT1], a["L1_gnn_bfx"][None, :]),
                 (m.norm_in[0:1, 0:D], a["L0_gnn_gamma"][None, :]), (m.norm_in[0:1, D:2 * D], a["L0_gnn_beta"][None, :]),
                 (bcomb[:, :], a["L2_gnn_b_comb"][None, :])]
        thin = [(m.bx1[:, :], a["L1_gnn_bx1"][:, None]), (m.bn1[:, :], a["L1_gnn_bn1"][:, None]),
                (bcol[:, :, 0:1], a["L2_gnn_b_self"].rearrange("(c p o) -> p c o", p=P, o=1)),
                (bcol[:, :, 1:2], a["L2_gnn_b_nb"].rearrange("(c p o) -> p c o", p=P, o=1))]
        thin += [(acol[32 * g:32 * g + 32, :], a["L0_gnn_a"].rearrange("(s d) -> d s", s=2)) for g in range(4)]
        total = 16 * (len(loads) + len(thin))

        with nc.Block() as block:
            @block.sync
            def _(sp):
                for dst, src in loads:
                    sp.dma_start(dst, src).then_inc(w_in, 16)
                for dst, src in thin:
                    sp.dma_start(dst, src, allow_slow_non_contiguous=True).then_inc(w_in, 16)
                for i in range(BUFS):
                    sp.dma_start(m.adj_rows[i], a["adj"][i * P:(i + 1) * P, :]).then_inc(m.adj_in[i], 16)
                sp.wait_ge(w_in, total)

            @block.scalar
            def _(act):
                q4 = NT // 4
                for i in range(4):
                    act.dma_start(m.x[:, i * q4 * D:(i + 1) * q4 * D].rearrange("p (t d) -> p t d", d=D),
                                  a["x"][i * q4 * P:(i + 1) * q4 * P, :].rearrange("(t p) d -> p t d", p=P)).then_inc(x_in[i], 16)
                act.wait_ge(m.ln_var_ready, 1)
                nc.scalar.activation(m.root[:, :], m.var[:, :], ACT.Sqrt).then_inc(m.ln_root_ready, 1)

            @block.tensor
            def _(pe):
                pe.wait_ge(w_in, total)
                for b, W in enumerate((W0, Ws, Wn, S3, N3)):
                    for r in range(2):
                        for c in range(2):
                            last = nc.tensor.transpose(psum[b][:, r * D + c * P:r * D + c * P + P],
                                                       W[:, c, r * P:r * P + P], m.ident[:, :])
                    last.then_inc(w_turned, 1)
                pe.wait_ge(heads_ready, 1)
                for r in range(2):
                    for c in range(2):
                        last = nc.tensor.matmul(psum[5][:, r * 32:r * 32 + 2 * HEADS], W0[:, c, r * P:r * P + P],
                                                heads[:, c, :], start=(c == 0), stop=(c == 1))
                last.then_inc(w_turned, 1)
                pe.wait_ge(w_used, 6)
                for b, (WT, half) in enumerate(((WsT, 0), (WnT, 2))):
                    for r in range(2):
                        for c in range(2):
                            last = nc.tensor.matmul(psum[b][:, r * D:r * D + D], WT[:, c, r * P:r * P + P],
                                                    Wc[:, half + c, :], start=(c == 0), stop=(c == 1))
                    last.then_inc(w_folded, 1)
                for c in range(2):
                    for half in range(2):
                        nc.tensor.matmul(psum[2][0:1, 0:D], bcol[:, c, half:half + 1], Wc[:, 2 * half + c, :],
                                         start=(c == 0 and half == 0), stop=False)
                nc.tensor.matmul(psum[2][0:1, 0:D], m.ones[0:1, 0:1], bcomb[:, :], start=False, stop=True).then_inc(w_folded, 1)
                for c in range(2):
                    last = nc.tensor.matmul(psum[3][:, 0:D], m.ones[:, :], N3T[:, c, :], start=(c == 0), stop=(c == 1))
                last.then_inc(w_folded, 1)
                nc.tensor.matmul(psum[4][:, 0:2 * D], m.ones[0:1, :], m.norm_in[:, :], start=True, stop=True).then_inc(w_folded, 1)
                nc.tensor.matmul(psum[6][:, 0:HID + OUT1], m.ones[0:1, :], m.bias_x[:, :], start=True, stop=True)
                pe.wait_ge(w_used, 7)
                nc.tensor.matmul(psum[7][:, 0:D], m.ones[0:1, :], m.bias_2[:, :], start=True, stop=True).then_inc(w_folded, 1)

            @block.vector
            def _(dve):
                nc.vector.memset(heads[:, :, :], 0.0).then_inc(w_steps, 1)
                s = Steps(dve, m)
                for i in range(4):
                    dve.wait_ge(x_in[i], 16)
                    x_stats(nc, m, s, first=i * (NT // 4), tiles=NT // 4)
                dve.wait_ge(w_steps, 1)
                dve.wait_ge(w_in, total)
                for c in range(2):
                    for g in range(4):
                        rows, head = slice(32 * g, 32 * g + 32), 4 * c + g
                        nc.vector.tensor_copy(heads[rows, c, head:head + 1], acol[rows, 0:1])
                        last = nc.vector.tensor_copy(heads[rows, c, HEADS + head:HEADS + head + 1], acol[rows, 1:2])
                last.then_inc(heads_ready, 1)
                layernorm_scale(nc, m, s, 1)
                s.fold()
                both = lambda t: t.rearrange("p (c n) -> p c n", c=2)
                dve.wait_ge(w_turned, 1)
                nc.vector.tensor_copy(m.W0T[:, :, 0:D], both(psum[0][:, :])).then_inc(w_used, 1)
                for b, to in ((1, WsT), (2, WnT), (3, m.S3T), (4, N3T)):
                    dve.wait_ge(w_turned, b + 1)
                    nc.vector.tensor_copy(to[:, :, :], both(psum[b][:, :])).then_inc(w_used, 1)
                dve.wait_ge(w_turned, 6)
                nc.vector.tensor_copy(m.W0T[:, :, D:D + 2 * HEADS],
                                      psum[5][:, 0:64].rearrange("p (c n) -> p c n", c=2)[:, :, 0:2 * HEADS]).then_inc(w_used, 1)
                dve.wait_ge(w_folded, 1)
                nc.vector.tensor_copy(m.W2s[:, :, :], both(psum[0][:, :]))
                dve.wait_ge(w_folded, 2)
                nc.vector.tensor_copy(m.W2n[:, :, :], both(psum[1][:, :]))
                dve.wait_ge(w_folded, 3)
                nc.vector.tensor_copy(m.bias_2[:, :], psum[2][0:1, 0:D]).then_inc(w_used, 1)
                dve.wait_ge(w_folded, 4)
                nc.vector.tensor_copy(m.neigh_sum[:, :], psum[3][:, 0:D])
                dve.wait_ge(w_folded, 5)
                nc.vector.tensor_copy(m.norm[:, :], psum[4][:, 0:2 * D])
                dve.wait_ge(w_folded, 6)
                nc.vector.tensor_copy(m.bias_x_rows[:, :], psum[6][:, 0:HID + OUT1])
                nc.vector.tensor_copy(m.bias_2_rows[:, :], psum[7][:, 0:D])



def scan(nc, m, sem, psum, adj, edges, neigh, table0, table1):
    A, adj_in = m.adj_rows, m.adj_in
    names = ["adj_free", "deg_ready", "deg_row_ready", "rounds_ready", "rounds_taken", "count_ready", "prefix_ready", "chunks_ready",
             "chunks_taken", "place_ready", "spread_ready", "record_ready", "record_stored",
             "h_ready", "x_turned", "x_copied", "n_turned", "n_copied", "product", "hid_ready", "tanh_ready", "natt_ready",
             "row_ready", "row1_ready", "mean_ready", "summed"]
    q = {n: sem("scan_" + n) for n in names}
    neigh_in = [sem(f"neigh_in{i}") for i in range(2)]
    row_out = [sem(f"row_out{i}") for i in range(2)]
    halves_of = ITEM_CHUNKS // HALF

    with ExitStack() as ctx:
        def sb(name, shape, dt=F32):
            return ctx.enter_context(nc.sbuf_tensor(name, shape, dt))
        junk = sb("scan_junk", [P, N], BF16)
        degc = [sb(f"degc{i}", [P, 1]) for i in range(BUFS)]
        left = sb("left", [P, 1])
        cnt = sb("cnt", [P, 1])
        vals = sb("vals", [P, SLOTS])
        J = sb("J", [P, SLOTS], U32)
        rowinfo = sb("rowinfo", [P, INFO])
        small = sb("scan_small", [P, 4])
        ints = sb("scan_ints", [P, 4], I32)
        tile_no = sb("tile_no", [P, 1])
        tile_before = sb("tile_before", [P, 1])
        run_of = sb("run_of", [P, 2])
        since_half = sb("since_half", [P, HALF * P])
        place_row_i = sb("place_row_i", [P, HALF * P], I32)
        place_row = sb("place_row", [P, HALF * P])
        place_col_i = sb("place_col_i", [P, HALF], I32)
        place_col = sb("place_col", [P, HALF])
        since = sb("since", [P, HALF * P])
        hot = sb("hot", [P, HALF * P])
        slot = sb("slot", [P, HALF])
        nowhere = sb("nowhere", [P, HALF])
        jf = sb("jf", [P, HALF])
        pick = sb("pick", [P, HALF * SLOTS])
        picked = sb("picked", [P, HALF * SLOTS])
        rec = sb("rec", [P, ITEM_CHUNKS, WORDS], I32)
        reci = rec[:, :, :]
        rech = rec[:, :, :].bitcast(BF16)
        mx, mx2, nchf, ncsum = (small[:, i:i + 1] for i in range(4))
        ps_deg, ps_pre, ps_info, ps_x, ps_n, ps_product, ps_hid, ps_row1 = psum
        info3 = ps_info[:, 0:HALF * INFO].rearrange("p (c i) -> p c i", i=INFO)

        hb = sb("hb", [P, D])
        nb = [sb(f"nb{i}", [P, D]) for i in range(2)]
        hT = sb("hT", [P, 2 * P])
        nT = sb("nT", [P, 2 * P])
        hid = sb("hid", [HID, P])
        row = [sb(f"row0_{i}", [P, ROW0]) for i in range(2)]
        row1 = [sb(f"row1_{i}", [P, ROW1]) for i in range(2)]
        sums = sb("sums", [P, H0 + ROW1])

        def groups(eng, tile):
            with eng.Fori(0, NT // BUFS - 1) as t4:
                for i in range(BUFS):
                    tile(t4 * BUFS + i, i, t4, False)
            for i in range(BUFS):
                tile(NT - BUFS + i, i, NT // BUFS - 1, True)

        with nc.Block() as block:
            @block.sync
            def _(sp):
                for i in range(2):
                    sp.dma_start(nb[i][:, :], neigh[i * P:(i + 1) * P, :]).then_inc(neigh_in[i], 16)
                    sp.sem_inc(row_out[i], 32)

                def tile(T, i, t4, last):
                    p = i % 2
                    if not last or i < BUFS - 2:
                        sp.wait_ge(q["n_turned"], T + 1)
                        sp.dma_start(nb[p][:, :], neigh[bass.ds((T + 2) * P, P), :]).then_inc(neigh_in[p], 16)
                    sp.wait_ge(q["row_ready"], T + 2)
                    sp.dma_start(table0[bass.ds(T * P, P), :], row[p][:, :]).then_inc(row_out[p], 16)
                    if not last:
                        sp.wait_ge(q["adj_free"], T + 1)
                        sp.dma_start(A[i], adj[bass.ds((T + BUFS) * P, P), :]).then_inc(adj_in[i], 16)
                    sp.wait_ge(q["row1_ready"], T + 2)
                    sp.dma_start(table1[bass.ds(T * P, P), :], row1[p][:, :]).then_inc(row_out[p], 16)
                groups(sp, tile)
                for i in range(2):
                    sp.wait_ge(row_out[i], 32 + 16 * NT)

            @block.scalar
            def _(act):
                def h_of(T):
                    nc.scalar.activation(hb[:, :], tile_of(m.x, T, D), ACT.Relu, scale=m.rstd[:, bass.ds(T, 1)],
                                         bias=m.shift[:, bass.ds(T, 1)]).then_inc(q["h_ready"], 1)

                def degree_of(i, loaded):
                    act.wait_ge(adj_in[i], loaded)
                    nc.scalar.activation(junk[:, :], A[i], ACT.Copy, accum_out=degc[i][:, :]).then_inc(q["deg_ready"], 1)

                h_of(0)
                degree_of(0, 16)
                act.wait_ge(q["deg_ready"], 1)
                degree_of(1, 16)
                act.wait_ge(q["deg_ready"], 2)
                degree_of(2, 16)

                def tile(T, i, t4, last):
                    p = i % 2
                    act.wait_ge(q["x_turned"], T + 1)
                    nc.scalar.activation(hT[:, :], ps_x[:, 0:2 * P], ACT.Copy).then_inc(q["x_copied"], 1)
                    act.wait_ge(q["n_turned"], T + 1)
                    nc.scalar.activation(nT[:, :], ps_n[:, 0:2 * P], ACT.Copy).then_inc(q["n_copied"], 1)
                    act.wait_ge(q["hid_ready"], T + 1)
                    nc.scalar.activation(hid[:, :], ps_hid[0:HID, 0:P], ACT.Tanh, bias=m.bn1[:, :]).then_inc(q["tanh_ready"], 1)
                    act.wait_ge(q["product"], T + 1)
                    act.wait_ge(row_out[p], t4 * (16 * BUFS) + (32 * (i // 2) + 32))
                    act.wait_ge(q["summed"], T * 2 + 1)
                    act.sem_inc(m.tick, 1)
                    nc.scalar.activation(tile_of(m.score_i, T, HEADS), ps_product[:, D + HEADS:D + 2 * HEADS], ACT.Copy)
                    nc.scalar.activation(row[p][:, H0:ROW0], ps_product[:, D:D + HEADS], ACT.Copy)
                    nc.scalar.activation(row[p][:, 0:H0].rearrange("p (h d) -> p h d", h=HEADS)[:, :, 0:DH],
                                         ps_product[:, 0:D].rearrange("p (h d) -> p h d", h=HEADS), ACT.Copy).then_inc(q["row_ready"], 1)
                    if not last or i < BUFS - 1:
                        h_of(T + 1)
                    if not last or i < BUFS - 3:
                        act.wait_ge(q["deg_ready"], T + 3)
                        degree_of((i + 3) % BUFS, t4 * 16 + (16 if i < BUFS - 3 else 32))
                    elif i == BUFS - 3:
                        act.sem_inc(q["deg_ready"], 1)
                    act.wait_ge(q["natt_ready"], T + 1)
                    nc.scalar.activation(row1[p][:, H1:ROW1], ps_row1[:, OUT1:OUT1 + HID], ACT.Copy)
                    nc.scalar.activation(row1[p][:, 0:OUT1], ps_row1[:, 0:OUT1], ACT.Copy).then_inc(q["row1_ready"], 1)
                groups(act, tile)

            @block.tensor
            def _(pe):
                with pe.register("scan_nr") as nr, pe.register("scan_nch") as nch, pe.register("scan_items") as items, \
                        pe.register("scan_halves") as halves:
                    pe.reg_mov(items, 0)
                    pe.reg_mov(halves, 0)
                    pe.sem_inc(q["n_copied"], 1)
                    pe.sem_inc(q["row_ready"], 1)
                    pe.sem_inc(q["row1_ready"], 1)

                    def degree_row(i):
                        nc.tensor.matmul(ps_deg[0:1, 0:P], degc[i][:, :], m.ident[:, :], start=True, stop=True).then_inc(q["deg_row_ready"], 1)

                    def products(T, i, t4):
                        p = i % 2
                        pe.wait_ge(q["h_ready"], T + 1)
                        for c in range(2):
                            last = nc.tensor.transpose(ps_x[:, c * P:c * P + P], hb[:, c * P:c * P + P], m.ident[:, :])
                        last.then_inc(q["x_turned"], 1)
                        pe.wait_ge(neigh_in[p], t4 * (8 * BUFS) + (16 * (i // 2) + 16))
                        pe.wait_ge(q["n_copied"], T + 1)
                        for c in range(2):
                            last = nc.tensor.transpose(ps_n[:, c * P:c * P + P], nb[p][:, c * P:c * P + P], m.ident[:, :])
                        last.then_inc(q["n_turned"], 1)
                        pe.wait_ge(q["n_copied"], T + 2)
                        for c in range(2):
                            last = nc.tensor.matmul(ps_hid[0:HID, 0:P], m.Wn1[:, c, :], nT[:, c * P:c * P + P],
                                                    start=(c == 0), stop=(c == 1))
                        last.then_inc(q["hid_ready"], 1)
                        pe.wait_ge(q["x_copied"], T + 1)
                        pe.wait_ge(q["row_ready"], T + 1)
                        for c in range(2):
                            last = nc.tensor.matmul(ps_product[:, 0:D + 2 * HEADS], hT[:, c * P:c * P + P], m.W0T[:, c, :],
                                                    start=(c == 0), stop=(c == 1))
                        last.then_inc(q["product"], 1)

                    def last_products(T):
                        pe.wait_ge(q["row1_ready"], T + 1)
                        for c in range(2):
                            nc.tensor.matmul(ps_row1[:, 0:OUT1], nT[:, c * P:c * P + P], m.Wv[:, c, :], start=(c == 0), stop=False)
                        nc.tensor.matmul(ps_row1[:, 0:OUT1], m.ones[0:1, :], m.bias_n[0:1, 0:OUT1], start=False, stop=True)
                        pe.wait_ge(q["tanh_ready"], T + 1)
                        nc.tensor.matmul(ps_row1[:, OUT1:OUT1 + HID], hid[:, :], m.Wn2[:, :], start=True, stop=False)
                        nc.tensor.matmul(ps_row1[:, OUT1:OUT1 + HID], m.ones[0:1, :], m.bias_n[0:1, OUT1:OUT1 + HID],
                                         start=False, stop=True).then_inc(q["natt_ready"], 1)

                    def spread():
                        pe.wait_ge(q["place_ready"], pe.snap(halves) + 1)
                        for c in range(HALF):
                            last = nc.tensor.matmul(ps_info[:, c * INFO:(c + 1) * INFO], hot[:, c * P:(c + 1) * P], rowinfo[:, :],
                                                    start=True, stop=True)
                        last.then_inc(q["spread_ready"], 1)
                        pe.reg_add(halves, halves, 1)

                    def prefix():
                        nc.tensor.matmul(ps_pre[:, 0:1], m.tri[:, :], cnt[:, :], start=True, stop=True)
                        nc.tensor.matmul(ps_pre[:, 1:2], m.ones[:, :], cnt[:, :], start=True, stop=True).then_inc(q["prefix_ready"], 1)

                    def item(before=None, after=None):
                        it = pe.snap(items)
                        if before:
                            before()
                        pe.wait_ge(q["count_ready"], it + 2)
                        prefix()
                        if after:
                            after()
                        pe.wait_ge(q["chunks_ready"], it + 1)
                        pe.sem_inc(m.tick, 1)
                        pe.reg_load(nch, ints[0:1, 0:1])
                        pe.sem_inc(q["chunks_taken"], 1)
                        spread()
                        with pe.If(pe.snap(nch, min_val=1, max_val=ITEM_CHUNKS) > HALF):
                            spread()
                        pe.reg_add(items, items, 1)

                    pe.wait_ge(q["deg_ready"], 1)
                    degree_row(0)
                    pe.wait_ge(q["count_ready"], 1)
                    prefix()
                    with pe.Fori(0, NT // BUFS) as t4:
                        for i in range(BUFS):
                            T = t4 * BUFS + i

                            def next_degrees():
                                pe.wait_ge(q["deg_ready"], T + 2)
                                pe.wait_ge(q["rounds_ready"], T + 1)
                                degree_row((i + 1) % BUFS)

                            pe.wait_ge(q["rounds_ready"], T + 1)
                            pe.sem_inc(m.tick, 1)
                            pe.reg_load(nr, ints[0:1, 2 + i % 2:3 + i % 2])
                            pe.sem_inc(q["rounds_taken"], 1)
                            n = pe.snap(nr, min_val=1, max_val=N // SLOTS)
                            with pe.If(n > 1):
                                with pe.Fori(1, n):
                                    item()
                            item(next_degrees, lambda: products(T, i, t4))
                            last_products(T)
                pe.wait_ge(q["summed"], 2 * NT + 3)
                nc.tensor.matmul(ps_product[:, 0:H0], m.ones[:, :], sums[:, 0:H0], start=True, stop=True)
                nc.tensor.matmul(ps_row1[:, 0:ROW1], m.ones[:, :], sums[:, H0:H0 + ROW1], start=True, stop=True).then_inc(q["mean_ready"], 1)

            @block.gpsimd
            def _(pool):
                with pool.register("scan_nr") as nr, pool.register("scan_nch") as nch, pool.register("scan_items") as items, \
                        pool.register("scan_chunks") as chunks:
                    pool.reg_mov(items, 0)
                    pool.reg_mov(chunks, 0)
                    pool.sem_inc(q["summed"], 2)
                    nc.gpsimd.iota(place_row_i[:, :], pattern=[[1, HALF * P]], base=0, channel_multiplier=0)
                    nc.gpsimd.iota(place_col_i[:, :], pattern=[[P, HALF]], base=0, channel_multiplier=1)
                    nc.gpsimd.memset(sums[:, :], 0.0).then_inc(q["summed"], 1)
                    pool.wait_ge(q["record_ready"], 1)
                    pool.dma_start(edges[:, 0:ITEM_CHUNKS, :], reci).then_inc(q["record_stored"], 16)

                    def store():
                        it = pool.snap(items)
                        pool.wait_ge(q["chunks_ready"], it + 1)
                        pool.sem_inc(m.tick, 1)
                        pool.reg_load(nch, ints[0:1, 0:1])
                        pool.sem_inc(q["chunks_taken"], 1)
                        pool.wait_ge(q["record_ready"], it + 2)
                        pool.wait_ge(q["record_stored"], it * 16 + 16)
                        pool.sem_inc(m.tick, 1)
                        at = pool.snap(chunks, min_val=0, max_val=MAX_CHUNKS - PAD)
                        pool.dma_start(edges[:, bass.ds(at, ITEM_CHUNKS), :], reci).then_inc(q["record_stored"], 16)
                        pool.reg_add(chunks, chunks, pool.snap(nch, min_val=1, max_val=ITEM_CHUNKS))
                        pool.reg_add(items, items, 1)

                    with pool.Fori(0, NT // 2) as t2:
                        for i in range(2):
                            T = t2 * 2 + i
                            pool.wait_ge(q["rounds_ready"], T + 1)
                            pool.sem_inc(m.tick, 1)
                            pool.reg_load(nr, ints[0:1, 2 + i:3 + i])
                            pool.sem_inc(q["rounds_taken"], 1)
                            n = pool.snap(nr, min_val=1, max_val=N // SLOTS)
                            with pool.If(n > 1):
                                with pool.Fori(1, n):
                                    store()
                            store()
                            pool.wait_ge(q["row_ready"], T + 2)
                            pool.wait_ge(q["summed"], T * 2 + 3)
                            pool.sem_inc(m.tick, 1)
                            nc.gpsimd.tensor_tensor(sums[:, 0:H0], sums[:, 0:H0], row[i][:, 0:H0], ALU.add).then_inc(q["summed"], 1)
                            pool.wait_ge(q["row1_ready"], T + 2)
                            pool.sem_inc(m.tick, 1)
                            nc.gpsimd.tensor_tensor(sums[:, H0:H0 + ROW1], sums[:, H0:H0 + ROW1], row1[i][:, :], ALU.add).then_inc(q["summed"], 1)
                    it = pool.snap(items)
                    pool.wait_ge(q["record_ready"], it + 2)
                    pool.wait_ge(q["record_stored"], it * 16 + 16)
                    pool.sem_inc(m.tick, 1)
                    for extra in range(0, SPARE, ITEM_CHUNKS):
                        if extra:
                            pool.reg_add(chunks, chunks, ITEM_CHUNKS)
                        at = pool.snap(chunks, min_val=0, max_val=MAX_CHUNKS - ITEM_CHUNKS)
                        pool.dma_start(edges[:, bass.ds(at, ITEM_CHUNKS), :], reci).then_inc(q["record_stored"], 16)
                    pool.wait_ge(q["record_stored"], it * 16 + 16 * (1 + SPARE // ITEM_CHUNKS))
                    pool.sem_inc(m.tick, 1)

            @block.vector
            def _(dve):
                with dve.register("scan_nr") as nr, dve.register("scan_nch") as nch, dve.register("scan_items") as items, \
                        dve.register("scan_halves") as halves:
                    s = Steps(dve, m)
                    dve.reg_mov(items, 0)
                    dve.reg_mov(halves, 0)
                    dve.reg_mov(nch, 1)
                    dve.sem_inc(q["chunks_taken"], 2)
                    dve.sem_inc(q["rounds_taken"], 2)
                    for i in range(2):
                        s.done(nc.vector.memset(row[i][:, :], 1.0))
                        s.done(nc.vector.memset(row1[i][:, :], 1.0))
                    s.done(nc.vector.memset(rowinfo[:, I_ONE:I_ONE + 1], 1.0))
                    s.done(nc.vector.memset(ncsum, 0.0))
                    s.done(nc.vector.memset(tile_no[:, :], 0.0))
                    nc.vector.memset(rec[:, :, :], 0).then_inc(q["record_ready"], 1)
                    s.done(nc.vector.tensor_scalar(rowinfo[:, I_ROW:I_ROW + 1], m.iota_col[:, :], 1.0, None, ALU.add))
                    dve.wait_ge(q["summed"], 3)
                    s.done(nc.vector.tensor_copy(place_row[:, :], place_row_i[:, :]))
                    s.done(nc.vector.tensor_copy(place_col[:, :], place_col_i[:, :]))

                    def ready_rounds(i, part):
                        if part == 0:
                            s.done(nc.vector.tensor_reduce(mx[0:1, :], ps_deg[0:1, 0:P], AX.X, ALU.max))
                        elif part == 1:
                            s.done(nc.vector.tensor_scalar(mx2[0:1, :], mx[0:1, :], (SLOTS - 1) / 2, 1.0 / SLOTS, ALU.add, ALU.mult))
                        else:
                            nc.vector.tensor_scalar(ints[0:1, 2 + i % 2:3 + i % 2], mx2[0:1, :], 1.0, None, ALU.max).then_inc(q["rounds_ready"], 1)

                    def count(remaining):
                        nc.vector.tensor_scalar(cnt[:, :], remaining, 0.0, float(SLOTS), ALU.max, ALU.min).then_inc(q["count_ready"], 1)
                        s.done(nc.vector.tensor_scalar(left[:, :], remaining, float(SLOTS), None, ALU.subtract))

                    def after_start(run, to):
                        return nc.vector.tensor_scalar(to[:, :], place_row[:, :], run[:, 0:1], None, ALU.is_ge)

                    def in_run(run, started):
                        return nc.vector.scalar_tensor_tensor(hot[:, :], place_row[:, :], run[:, 1:2], started[:, :], ALU.is_lt, ALU.mult)

                    def finish():
                        it = dve.snap(items)
                        records(0, it)
                        with dve.If(dve.snap(nch, min_val=1, max_val=ITEM_CHUNKS) > HALF):
                            run = rowinfo[:, I_START:I_END + 1]
                            s.done(nc.vector.tensor_scalar(run, run, float(HALF * P), None, ALU.subtract))
                            s.wait()
                            s.done(after_start(run, since_half))
                            s.wait()
                            in_run(run, since_half).then_inc(q["place_ready"], 1)
                            records(1, it)
                        s.wait()
                        dve.sem_inc(q["record_ready"], 1)

                    def records(h, it):
                        c = slice(h * HALF, (h + 1) * HALF)
                        s.wait()
                        dve.wait_ge(q["spread_ready"], dve.snap(halves) + 1)
                        if h == 0:
                            dve.wait_ge(q["record_stored"], it * 16)
                            dve.sem_inc(m.tick, 1)
                            s.done(nc.vector.tensor_copy(reci[:, :, W_TILE], tile_before[:, :].broadcast_to([P, ITEM_CHUNKS])))
                        slot3 = slot[:, :].rearrange("p (c o) -> p c o", o=1)
                        s.done(nc.vector.tensor_tensor(slot3, place_col[:, :].rearrange("p (c o) -> p c o", o=1),
                                                       info3[:, :, I_START:I_START + 1], ALU.subtract))
                        s.done(nc.vector.tensor_scalar(rech[:, c, H_ROW], info3[:, :, I_ROW], 1.0, None, ALU.subtract))
                        s.done(nc.vector.tensor_scalar(nowhere[:, :], info3[:, :, I_ONE], -float(NOWHERE), float(NOWHERE), ALU.mult, ALU.add))
                        s.wait()
                        pick3 = pick[:, :].rearrange("p (c k) -> p c k", k=SLOTS)
                        picked3 = picked[:, :].rearrange("p (c k) -> p c k", k=SLOTS)
                        s.done(nc.vector.tensor_tensor(pick3, m.iota_row[:, None, 0:SLOTS].broadcast_to([P, HALF, SLOTS]),
                                                       slot3.broadcast_to([P, HALF, SLOTS]), ALU.is_equal))
                        s.done(nc.vector.tensor_copy(rech[:, c, H_SLOT], slot[:, :]))
                        s.wait()
                        s.done(nc.vector.tensor_tensor(picked3, pick3, info3[:, :, 0:SLOTS], ALU.mult))
                        s.wait()
                        s.done(nc.vector.tensor_reduce(jf[:, :], picked3, AX.X, ALU.add))
                        s.wait()
                        s.done(nc.vector.tensor_tensor(reci[:, c, W_J], jf[:, :], nowhere[:, :], ALU.add))
                        dve.reg_add(halves, halves, 1)
                        s.fold()

                    def item(T, i, last):
                        it = dve.snap(items)
                        s.wait()
                        dve.wait_ge(q["prefix_ready"], it + 1)
                        dve.wait_ge(q["chunks_taken"], it * 2 + 2)
                        s.done(nc.vector.tensor_scalar(nchf, ps_pre[:, 1:2], (P - 1) / 2, 1.0 / P, ALU.add, ALU.mult))
                        s.done(nc.vector.tensor_copy(run_of[:, 0:1], ps_pre[:, 0:1]))
                        s.done(nc.vector.tensor_scalar(vals[:, :], m.iota_row[:, 0:SLOTS], cnt[:, 0:1], None, ALU.is_lt))
                        s.done(nc.vector.tensor_tensor(run_of[:, 1:2], ps_pre[:, 0:1], cnt[:, :], ALU.add))
                        s.wait()
                        nc.vector.tensor_scalar(ints[:, 0:1], nchf, 1.0, None, ALU.max).then_inc(q["chunks_ready"], 1)
                        if last:
                            s.done(nc.vector.tensor_copy(m.degree[:, bass.ds(T, 1)], degc[i][:, :]))
                        dve.wait_ge(q["chunks_ready"], it + 1)
                        s.done(nc.vector.tensor_copy(nchf, ints[:, 0:1]))
                        s.wait()
                        s.done(nc.vector.tensor_tensor(ncsum, ncsum, nchf, ALU.add))
                        s.done(after_start(run_of, since))
                        s.fold()
                        if i == 0:
                            with dve.If(it > 0):
                                finish()
                        else:
                            finish()
                        s.wait()
                        s.done(nc.vector.tensor_copy(rowinfo[:, I_START:I_END + 1], run_of[:, :]))
                        if last:
                            dve.wait_ge(q["deg_row_ready"], T + 2)
                            dve.sem_inc(m.tick, 1)
                            dve.wait_ge(q["rounds_taken"], T * 2 + 2)
                            dve.sem_inc(m.tick, 1)
                            ready_rounds(i + 1, 0)
                        count(degc[(i + 1) % BUFS][:, :] if last else left[:, :])
                        if last:
                            s.wait()
                            ready_rounds(i + 1, 1)
                        s.done(nc.vector.tensor_copy(tile_before[:, :], tile_no[:, :]))
                        s.done(in_run(run_of, since))
                        if last:
                            s.done(nc.vector.tensor_scalar(tile_no[:, :], tile_no[:, :], 1.0, None, ALU.add))
                        s.wait()
                        if last:
                            ready_rounds(i + 1, 2)
                        dve.sem_inc(m.tick, 1)
                        s.done(nc.vector.max_index(J[:, :], vals[:, :], A[i]))
                        dve.reg_load(nch, ints[0:1, 0:1])
                        if last:
                            dve.wait_ge(q["rounds_ready"], T + 2)
                            dve.sem_inc(m.tick, 1)
                            dve.reg_load(nr, ints[0:1, 2 + (i + 1) % 2:3 + (i + 1) % 2])
                        s.wait()
                        nc.vector.tensor_copy(rowinfo[:, 0:SLOTS], J[:, :]).then_inc(q["place_ready"], 1)
                        if last:
                            dve.sem_inc(q["adj_free"], 1)
                        else:
                            s.done(nc.vector.match_replace(A[i], vals[:, :], A[i], 0.0))
                        dve.reg_add(items, items, 1)
                        s.fold()

                    dve.wait_ge(q["deg_row_ready"], 1)
                    ready_rounds(0, 0)
                    s.wait()
                    ready_rounds(0, 1)
                    s.wait()
                    ready_rounds(0, 2)
                    count(degc[0][:, :])
                    dve.wait_ge(q["rounds_ready"], 1)
                    dve.reg_load(nr, ints[0:1, 2:3])
                    s.fold()
                    with dve.Fori(0, NT // BUFS) as t4:
                        for i in range(BUFS):
                            T = t4 * BUFS + i
                            n = dve.snap(nr, min_val=1, max_val=N // SLOTS)
                            with dve.If(n > 1):
                                with dve.Fori(1, n):
                                    item(T, i, False)
                            item(T, i, True)
                    finish()
                    it = dve.snap(items)
                    s.wait()
                    dve.wait_ge(q["record_stored"], it * 16 + 16)
                    s.done(nc.vector.tensor_scalar(mx, ncsum, (PAD - 1) / 2, 1.0 / PAD, ALU.add, ALU.mult))
                    s.done(nc.vector.tensor_scalar(mx2, ncsum, (2 * PAD - 1) / 2, 0.5 / PAD, ALU.add, ALU.mult))
                    s.done(nc.vector.memset(reci[:, :, W_J], NOWHERE))
                    s.done(nc.vector.memset(rech[:, :, H_ROW], -1.0))
                    s.done(nc.vector.memset(rech[:, :, H_SLOT], 0.0))
                    s.done(nc.vector.memset(reci[:, :, W_TILE], 0))
                    s.wait()
                    s.done(nc.vector.tensor_scalar(m.passes[:, :], mx, 1.0, None, ALU.max))
                    s.done(nc.vector.tensor_scalar(m.double_passes[:, :], mx2, 1.0, None, ALU.max))
                    s.wait()
                    dve.sem_inc(q["record_ready"], 1)
                    dve.wait_ge(q["mean_ready"], 1)
                    s.done(nc.vector.tensor_scalar(m.mean0[:, :], ps_product[:, 0:H0], 1.0 / N, None, ALU.mult))
                    s.done(nc.vector.tensor_scalar(m.mean1[:, :], ps_row1[:, 0:ROW1], 1.0 / N, None, ALU.mult))
                    s.fold()


def grouped(t, width):
    return t[:, :].rearrange("p (u w) -> p u w", w=width)


def clear_sums(nc, m, cleared):
    nc.scalar.activation(m.acc[:, :].rearrange("p (a b) -> p a b", b=P), m.iota_row[:, None, :].broadcast_to([P, NT * H0 // P, P]),
                         ACT.Copy, scale=0.0).then_inc(cleared, 1)


def attend(nc, m, sem, psum, tag, edges, table, heads, width, extra, row_table, row_width, slope, running, acc):
    names = ["taken", "place_ready", "place_full", "turned", "turned_used", "own_ready", "spread_ready", "slots_ready", "max_ready",
             "growth_ready", "top_ready", "score_ready", "weight_ready", "fade_ready", "faded", "scaled_ready", "sum_ready", "merged", "acc_clear"]
    q = {n: sem(f"{tag}_{n}") for n in names}
    rec_in = sem(f"{tag}_rec_in")
    gathered = [sem(f"{tag}_gathered{i}") for i in range(SETS)]
    hw = heads * width
    wide = hw + extra
    e1 = heads + 1
    c_slots = GROUP * row_width
    c_top = c_slots + GROUP * SLOTS * e1
    assert c_top + GROUP * heads <= 512
    with ExitStack() as ctx:
        def sb(name, shape, dt=F32):
            return [ctx.enter_context(nc.sbuf_tensor(f"{tag}_{name}{i}", shape, dt)) for i in range(SETS)]
        rec_all = ctx.enter_context(nc.sbuf_tensor(f"{tag}_rec", [P, PAD, WORDS], I32))
        rec = [rec_all[:, i * GROUP:(i + 1) * GROUP, :] for i in range(SETS)]
        G = [m.gathered_rows[:, i * GROUP * wide:(i + 1) * GROUP * wide] for i in range(SETS)]
        GW = sb("GW", [P, GROUP * hw])
        place = sb("place", [P, GROUP * P])
        place_h = sb("place_h", [P, GROUP * P], BF16)
        back = sb("back", [P, GROUP * P])
        slot1 = sb("slot1", [P, GROUP * SLOTS])
        z = sb("z", [P, GROUP * heads])
        zl = sb("zl", [P, GROUP * heads])
        zs = sb("zs", [P, GROUP * heads])
        wgt = sb("wgt", [P, GROUP * heads])
        spread = sb("spread", [P, GROUP * SLOTS * e1])
        absent = sb("absent", [P, GROUP * SLOTS])
        zm = sb("zm", [P, GROUP * heads * SLOTS])
        top, old, newmax, growth, fade = (ctx.enter_context(nc.sbuf_tensor(f"{tag}_{name}", [P, PAD * heads], F32))
                                          for name in ("top", "old", "newmax", "growth", "fade"))
        prod = sb("prod", [P, GROUP * row_width])
        bank_back = [psum[0], psum[1]]
        bank_small = [psum[2 + i] for i in range(SETS)]
        bank_sum = [psum[0], psum[1], psum[6], psum[7]]

        def load_tile(eng, regs, i, u):
            eng.reg_load(regs[i][u], rec[i][0:1, u, W_TILE:W_TILE + 1])

        def first_tiles(eng, regs):
            eng.wait_ge(rec_in, 16)
            for i in range(SETS):
                for u in range(GROUP):
                    load_tile(eng, regs, i, u)

        def tiles_of(eng, regs):
            return [[eng.snap(r, min_val=0, max_val=NT - 1) for r in of_set] for of_set in regs]

        with nc.Block() as block:
            @block.sync
            def _(sp):
                with sp.register(f"{tag}_passes") as passes:
                    sp.reg_load(passes, m.passes[0:1, 0:1])
                    sp.dma_start(rec_all[:, :, :], edges[:, 0:PAD, :]).then_inc(rec_in, 16)
                    with sp.Fori(0, sp.snap(passes, min_val=1, max_val=MAX_PASSES)) as it:
                        sp.wait_ge(q["taken"], it * 3 + 3)
                        sp.dma_start(rec_all[:, :, :], edges[:, bass.ds(it * PAD + PAD, PAD), :]).then_inc(rec_in, 16)

            @block.gpsimd
            def _(pool):
                with ExitStack() as rc:
                    passes = rc.enter_context(pool.register(f"{tag}_passes"))
                    regs = [[rc.enter_context(pool.register(f"{tag}_tile{i}{u}")) for u in range(GROUP)] for i in range(SETS)]
                    pool.reg_load(passes, m.passes[0:1, 0:1])
                    pool.sem_inc(q["faded"], PAD)
                    with pool.Fori(0, pool.snap(passes, min_val=1, max_val=MAX_PASSES)) as it:
                        pool.wait_ge(rec_in, it * 16 + 16)
                        pool.sem_inc(m.tick, 1)
                        for i in range(SETS):
                            pool.wait_ge(q["scaled_ready"], it * SETS + (i + 1))
                            pool.sem_inc(m.tick, 1)
                            for u in range(GROUP):
                                nc.gpsimd.indirect_dma_start(
                                    G[i][:, u * wide:(u + 1) * wide], None, table[:, :],
                                    bass.IndirectOffsetOnAxis(ap=rec[i][:, u, W_J:W_J + 1].bitcast(U32), axis=0),
                                    bounds_check=N - 1, oob_is_err=False).then_inc(gathered[i], 16)
                                load_tile(pool, regs, i, u)
                        pool.sem_inc(q["taken"], 1)
                        tiles = tiles_of(pool, regs)
                        pool.wait_ge(q["acc_clear"], 1)
                        pool.wait_ge(q["merged"], it * PAD + GROUP)
                        pool.sem_inc(m.tick, 1)
                        for c in range(PAD):
                            if c % GROUP == 0:
                                pool.wait_ge(q["fade_ready"], it * SETS + (c // GROUP + 1))
                                pool.sem_inc(m.tick, 1)
                            mine = tile_of(acc, tiles[c // GROUP][c % GROUP], hw).rearrange("p (h d) -> p h d", h=heads)
                            by = fade[:, c * heads:(c + 1) * heads].rearrange("p (h o) -> p h o", o=1).broadcast_to([P, heads, width])
                            pool.wait_ge(q["faded"], it * PAD + (PAD + c))
                            pool.sem_inc(m.tick, 1)
                            nc.gpsimd.tensor_tensor(mine, mine, by, ALU.mult).then_inc(q["faded"], 1)

            @block.scalar
            def _(act):
                with act.register(f"{tag}_passes") as passes:
                    act.reg_load(passes, m.passes[0:1, 0:1])
                    clear_sums(nc, m, q["acc_clear"])
                    with act.Fori(0, act.snap(passes, min_val=1, max_val=MAX_PASSES)) as it:
                        for i in range(SETS):
                            act.wait_ge(q["turned"], it * SETS + (i + 1))
                            nc.scalar.activation(back[i][:, :], bank_back[i % 2][:, :], ACT.Copy).then_inc(q["turned_used"], 1)
                            act.wait_ge(q["place_ready"], it * SETS + (i + 1))
                            act.wait_ge(q["sum_ready"], it * PAD + 1)
                            nc.scalar.activation(place[i][:, :], place_h[i][:, :], ACT.Copy).then_inc(q["place_full"], 1)
                        for i in range(SETS):
                            cols = slice(i * GROUP * heads, (i + 1) * GROUP * heads)
                            act.wait_ge(q["growth_ready"], it * SETS + (i + 1))
                            act.wait_ge(q["faded"], it * PAD + PAD)
                            nc.scalar.activation(fade[:, cols], growth[:, cols], ACT.Exp).then_inc(q["fade_ready"], 1)
                        for i in range(SETS):
                            act.wait_ge(q["score_ready"], it * SETS + (i + 1))
                            nc.scalar.activation(wgt[i][:, :], zs[i][:, :], ACT.Exp).then_inc(q["weight_ready"], 1)

            @block.tensor
            def _(pe):
                with ExitStack() as rc:
                    passes = rc.enter_context(pe.register(f"{tag}_passes"))
                    regs = [[rc.enter_context(pe.register(f"{tag}_tile{i}{u}")) for u in range(GROUP)] for i in range(SETS)]
                    pe.reg_load(passes, m.passes[0:1, 0:1])
                    first_tiles(pe, regs)
                    pe.sem_inc(q["sum_ready"], 1)
                    pe.sem_inc(q["taken"], 1)
                    with pe.Fori(0, pe.snap(passes, min_val=1, max_val=MAX_PASSES)) as it:
                        tiles = tiles_of(pe, regs)

                        def turn(i):
                            if i == 0:
                                pe.wait_ge(q["merged"], it * PAD + (GROUP - 2))
                            if i >= 2:
                                pe.wait_ge(q["turned_used"], it * SETS + (i - 1))
                            pe.wait_ge(q["place_ready"], it * SETS + (i + 1))
                            for u in range(GROUP):
                                last = nc.tensor.matmul(bank_back[i % 2][:, u * P:(u + 1) * P], place_h[i][:, u * P:(u + 1) * P], m.ident_h[:, :],
                                                        start=True, stop=True)
                            last.then_inc(q["turned"], 1)

                        def own_part(i):
                            pe.wait_ge(q["turned_used"], it * SETS + (i + 1))
                            for u in range(GROUP):
                                last = nc.tensor.matmul(bank_small[i][:, u * row_width:(u + 1) * row_width],
                                                        back[i][:, u * P:(u + 1) * P], tile_of(row_table, tiles[i][u], row_width),
                                                        start=True, stop=True)
                            last.then_inc(q["own_ready"], 1)

                        def slots_part(i):
                            pe.wait_ge(q["spread_ready"], it * SETS + (i + 1))
                            pe.wait_ge(q["place_full"], it * SETS + (i + 1))
                            for u in range(GROUP):
                                last = nc.tensor.matmul(bank_small[i][:, c_slots + u * SLOTS * e1:c_slots + (u + 1) * SLOTS * e1],
                                                        place[i][:, u * P:(u + 1) * P],
                                                        spread[i][:, u * SLOTS * e1:(u + 1) * SLOTS * e1], start=True, stop=True)
                            last.then_inc(q["slots_ready"], 1)

                        for i in range(SETS + 2):
                            if i < SETS:
                                turn(i)
                            if 0 < i <= SETS:
                                own_part(i - 1)
                            if i > 1:
                                slots_part(i - 2)
                        pe.wait_ge(q["max_ready"], it + 1)
                        for i in range(SETS):
                            for u in range(GROUP):
                                last = nc.tensor.matmul(bank_small[i][:, c_top + u * heads:c_top + (u + 1) * heads],
                                                        back[i][:, u * P:(u + 1) * P], tile_of(running, tiles[i][u], heads),
                                                        start=True, stop=True)
                            last.then_inc(q["top_ready"], 1)
                        pe.wait_ge(rec_in, it * 16 + 32)
                        pe.sem_inc(m.tick, 1)
                        for i in range(SETS):
                            pe.wait_ge(q["scaled_ready"], it * SETS + (i + 1 + SETS))
                            for u in range(GROUP):
                                pe.wait_ge(q["merged"], it * PAD + (i * GROUP + u + 1))
                                nc.tensor.matmul(bank_sum[u][:, 0:hw], place[i][:, u * P:(u + 1) * P],
                                                 GW[i][:, u * hw:(u + 1) * hw], start=True, stop=True).then_inc(q["sum_ready"], 1)
                                load_tile(pe, regs, i, u)
                        pe.sem_inc(q["taken"], 1)

            @block.vector
            def _(dve):
                with ExitStack() as rc:
                    passes = rc.enter_context(dve.register(f"{tag}_passes"))
                    regs = [[rc.enter_context(dve.register(f"{tag}_tile{i}{u}")) for u in range(GROUP)] for i in range(SETS)]
                    s = Steps(dve, m)
                    dve.reg_load(passes, m.passes[0:1, 0:1])
                    s.done(nc.vector.memset(running[:, :], -NEVER))
                    dve.sem_inc(q["scaled_ready"], SETS)
                    dve.sem_inc(q["merged"], GROUP)
                    s.fold()
                    def places():
                        for i in range(SETS):
                            half = rec[i].bitcast(BF16)
                            nc.vector.tensor_tensor(grouped(place_h[i], P), m.iota_row_h[:, None, :].broadcast_to([P, GROUP, P]),
                                                    half[:, :, H_ROW:H_ROW + 1].broadcast_to([P, GROUP, P]),
                                                    ALU.is_equal).then_inc(q["place_ready"], 1)
                            s.done(nc.vector.tensor_tensor(grouped(slot1[i], SLOTS), m.iota_row[:, None, 0:SLOTS].broadcast_to([P, GROUP, SLOTS]),
                                                           half[:, :, H_SLOT:H_SLOT + 1].broadcast_to([P, GROUP, SLOTS]), ALU.is_equal))
                    first_tiles(dve, regs)
                    places()
                    s.fold()
                    with dve.Fori(0, dve.snap(passes, min_val=1, max_val=MAX_PASSES)) as it:
                        tiles = tiles_of(dve, regs)
                        def scores(i):
                            g3 = grouped(G[i], wide)
                            s.wait()
                            dve.wait_ge(gathered[i], it * (16 * GROUP) + 16 * GROUP)
                            dve.wait_ge(q["own_ready"], it * SETS + (i + 1))
                            own = bank_small[i][:, 0:GROUP * row_width].rearrange("p (u w) -> p u w", w=row_width)
                            if row_width == heads:
                                s.done(nc.vector.tensor_tensor(grouped(z[i], heads), own, g3[:, :, hw:hw + heads], ALU.add))
                            else:
                                s.done(nc.vector.tensor_tensor(grouped(prod[i], row_width), own, g3[:, :, hw:hw + row_width], ALU.mult))
                                s.wait()
                                s.done(nc.vector.tensor_reduce(z[i][:, :], grouped(prod[i], row_width), AX.X, ALU.add))
                            s.wait()
                            s.done(nc.vector.scalar_tensor_tensor(zl[i][:, :], z[i][:, :], slope, z[i][:, :], ALU.mult, ALU.max))
                            sp4 = spread[i][:, :].rearrange("p (u k e) -> p u k e", u=GROUP, e=e1)
                            hot = slot1[i][:, :].rearrange("p (u k o) -> p u k o", u=GROUP, o=1)
                            s.done(nc.vector.tensor_copy(sp4[:, :, :, heads:heads + 1], hot))
                            s.wait()
                            nc.vector.tensor_tensor(sp4[:, :, :, 0:heads], zl[i][:, :].rearrange("p (u o h) -> p u o h", u=GROUP, o=1)
                                                    .broadcast_to([P, GROUP, SLOTS, heads]),
                                                    hot.broadcast_to([P, GROUP, SLOTS, heads]), ALU.mult).then_inc(q["spread_ready"], 1)

                        def maxima(i):
                            dve.wait_ge(q["slots_ready"], it * SETS + (i + 1))
                            el = bank_small[i][:, c_slots:c_top].rearrange("p (u k e) -> p u k e", u=GROUP, e=e1)
                            s.done(nc.vector.tensor_scalar(absent[i][:, :].rearrange("p (u k o) -> p u k o", u=GROUP, o=1),
                                                           el[:, :, :, heads:heads + 1], 1.0, NEVER, ALU.subtract, ALU.mult))
                            s.wait()
                            s.done(nc.vector.tensor_tensor(zm[i][:, :].rearrange("p (u h k) -> p u h k", u=GROUP, k=SLOTS),
                                                           el[:, :, :, 0:heads].rearrange("p u k h -> p u h k"),
                                                           absent[i][:, :].rearrange("p (u o k) -> p u o k", u=GROUP, o=1)
                                                           .broadcast_to([P, GROUP, heads, SLOTS]), ALU.add))
                            s.wait()
                            s.done(nc.vector.tensor_reduce(top[:, i * GROUP * heads:(i + 1) * GROUP * heads],
                                                           zm[i][:, :].rearrange("p (a k) -> p a k", k=SLOTS), AX.X, ALU.max))
                            for c in range(i * GROUP, (i + 1) * GROUP):
                                cols = slice(c * heads, (c + 1) * heads)
                                mine = tile_of(running, tiles[i][c - i * GROUP], heads)
                                s.wait()
                                nc.vector.tensor_scalar(old[:, cols], mine, 0.0, None, ALU.add)
                                ins = nc.vector.tensor_tensor(mine, mine, top[:, cols], ALU.max)
                                if c < PAD - 1:
                                    s.done(ins)
                                else:
                                    ins.then_inc(q["max_ready"], 1)
                                    dve.wait_ge(q["max_ready"], it + 1)
                            cols = slice(i * GROUP * heads, (i + 1) * GROUP * heads)
                            if i < SETS - 1:
                                s.wait()
                            s.done(nc.vector.tensor_tensor(newmax[:, cols], old[:, cols], top[:, cols], ALU.max))
                            s.wait()
                            nc.vector.tensor_tensor(growth[:, cols], old[:, cols], newmax[:, cols], ALU.subtract).then_inc(q["growth_ready"], 1)

                        scores(0)
                        for i in range(1, SETS):
                            scores(i)
                            maxima(i - 1)
                        dve.wait_ge(q["spread_ready"], it * SETS + SETS)
                        dve.sem_inc(q["taken"], 1)
                        maxima(SETS - 1)

                        def score(i):
                            dve.wait_ge(q["top_ready"], it * SETS + (i + 1))
                            s.done(nc.vector.tensor_tensor(z[i][:, :], zl[i][:, :], bank_small[i][:, c_top:c_top + GROUP * heads], ALU.subtract))
                            s.wait()
                            nc.vector.tensor_scalar(zs[i][:, :], z[i][:, :], 0.0, None, ALU.min).then_inc(q["score_ready"], 1)

                        def weigh(i):
                            g3 = grouped(G[i], wide)
                            if heads == 1:
                                src = g3[:, :, 0:hw]
                                dst = grouped(GW[i], hw)
                                w = wgt[i][:, :].rearrange("p (u o) -> p u o", o=1).broadcast_to([P, GROUP, hw])
                            else:
                                src = g3[:, :, 0:hw].rearrange("p u (h d) -> p u h d", h=heads)
                                dst = GW[i][:, :].rearrange("p (u h d) -> p u h d", u=GROUP, h=heads)
                                w = wgt[i][:, :].rearrange("p (u h o) -> p u h o", u=GROUP, o=1).broadcast_to([P, GROUP, heads, width])
                            dve.wait_ge(q["weight_ready"], it * SETS + (i + 1))
                            nc.vector.tensor_tensor(dst, src, w, ALU.mult).then_inc(q["scaled_ready"], 1)
                            if i == 0:
                                dve.wait_ge(rec_in, it * 16 + 32)
                                dve.sem_inc(m.tick, 1)
                            for u in range(GROUP):
                                load_tile(dve, regs, i, u)

                        score(0)
                        for i in range(1, SETS):
                            score(i)
                            weigh(i - 1)
                        weigh(SETS - 1)
                        places()
                        dve.wait_ge(q["faded"], it * PAD + 2 * PAD)
                        dve.sem_inc(m.tick, 1)
                        for i in range(SETS):
                            for u in range(GROUP):
                                mine = tile_of(acc, tiles[i][u], hw)
                                dve.wait_ge(q["merged"], it * PAD + (i * GROUP + u + GROUP))
                                dve.wait_ge(q["sum_ready"], it * PAD + (i * GROUP + u + 2))
                                nc.vector.tensor_tensor(mine, mine, bank_sum[u][:, 0:hw], ALU.add).then_inc(q["merged"], 1)
                        dve.wait_ge(q["merged"], it * PAD + (PAD + GROUP))
                        dve.sem_inc(m.tick, 1)
                        s.fold()


def gather_sum(nc, m, sem, psum, tag, edges, table, width, acc):
    q = {n: sem(f"{tag}_{n}") for n in ["taken", "place_ready", "sum_ready", "merged", "acc_clear"]}
    rec_in = [sem(f"{tag}_rec_in{b}") for b in range(2)]
    gathered = [sem(f"{tag}_gathered{i}") for i in range(SETS)]
    with ExitStack() as ctx:
        def sb(name, shape, dt=F32):
            return [ctx.enter_context(nc.sbuf_tensor(f"{tag}_{name}{i}", shape, dt)) for i in range(SETS)]
        recs = [ctx.enter_context(nc.sbuf_tensor(f"{tag}_rec{b}", [P, PAD, WORDS], I32)) for b in range(2)]
        G = [m.gathered_rows[:, i * GROUP * width:(i + 1) * GROUP * width] for i in range(SETS)]
        place = sb("place", [P, GROUP * P])

        def rec_of(j):
            return recs[j // SETS][:, j % SETS * GROUP:(j % SETS + 1) * GROUP, :]

        def bank(i, u):
            return psum[i % 2 * GROUP + u][:, 0:width]

        with nc.Block() as block:
            @block.sync
            def _(sp):
                with sp.register(f"{tag}_passes") as passes:
                    sp.reg_load(passes, m.double_passes[0:1, 0:1])
                    with sp.Fori(0, sp.snap(passes, min_val=1, max_val=MAX_PASSES // 2 + 1)) as it:
                        for b in range(2):
                            sp.wait_ge(q["taken"], it * 2 + (b + 1))
                            sp.sem_inc(m.tick, 1)
                            sp.wait_ge(q["sum_ready"], it * TURNS + (SETS * b + SETS))
                            sp.sem_inc(m.tick, 1)
                            sp.dma_start(recs[b][:, :, :], edges[:, bass.ds(it * (2 * PAD) + b * PAD, PAD), :]).then_inc(rec_in[b], 16)

            @block.gpsimd
            def _(pool):
                with pool.register(f"{tag}_passes") as passes:
                    pool.reg_load(passes, m.double_passes[0:1, 0:1])
                    with pool.Fori(0, pool.snap(passes, min_val=1, max_val=MAX_PASSES // 2 + 1)) as it:
                        for j in range(TURNS):
                            i = j % SETS
                            rec = rec_of(j)
                            if i == 0:
                                pool.wait_ge(rec_in[j // SETS], it * 16 + 16)
                                pool.sem_inc(m.tick, 1)
                            pool.wait_ge(q["sum_ready"], it * TURNS + (j + SETS + 1))
                            pool.sem_inc(m.tick, 1)
                            for u in range(GROUP):
                                nc.gpsimd.indirect_dma_start(
                                    G[i][:, u * width:(u + 1) * width], None, table[:, :],
                                    bass.IndirectOffsetOnAxis(ap=rec[:, u, W_J:W_J + 1].bitcast(U32), axis=0),
                                    bounds_check=N - 1, oob_is_err=False).then_inc(gathered[i], 16)

            @block.scalar
            def _(act):
                clear_sums(nc, m, q["acc_clear"])

            @block.tensor
            def _(pe):
                with pe.register(f"{tag}_passes") as passes:
                    pe.reg_load(passes, m.double_passes[0:1, 0:1])
                    pe.sem_inc(q["sum_ready"], TURNS)
                    with pe.Fori(0, pe.snap(passes, min_val=1, max_val=MAX_PASSES // 2 + 1)) as it:
                        for j in range(TURNS):
                            i = j % SETS
                            pe.wait_ge(q["place_ready"], it * TURNS + (j + 1))
                            pe.wait_ge(gathered[i], it * (2 * 16 * GROUP) + 16 * GROUP * (j // SETS + 1))
                            pe.wait_ge(q["merged"], it * TURNS + (j + 1))
                            for u in range(GROUP):
                                last = nc.tensor.matmul(bank(i, u), place[i][:, u * P:(u + 1) * P],
                                                        G[i][:, u * width:(u + 1) * width], start=True, stop=True)
                            last.then_inc(q["sum_ready"], 1)

            @block.vector
            def _(dve):
                with ExitStack() as rc:
                    passes = rc.enter_context(dve.register(f"{tag}_passes"))
                    regs = [[rc.enter_context(dve.register(f"{tag}_tile{i}{u}")) for u in range(GROUP)] for i in range(SETS)]
                    s = Steps(dve, m)
                    dve.reg_load(passes, m.double_passes[0:1, 0:1])
                    dve.sem_inc(q["merged"], 2)
                    dve.sem_inc(q["taken"], 2)
                    s.fold()
                    with dve.Fori(0, dve.snap(passes, min_val=1, max_val=MAX_PASSES // 2 + 1)) as it:
                        for b in range(2):
                            dve.wait_ge(rec_in[b], it * 16 + 16)
                            dve.sem_inc(m.tick, 1)
                            for i in range(SETS):
                                j = b * SETS + i
                                half = rec_of(j).bitcast(BF16)
                                dve.wait_ge(q["sum_ready"], it * TURNS + (j + SETS + 1))
                                dve.sem_inc(m.tick, 1)
                                nc.vector.tensor_tensor(grouped(place[i], P), m.iota_row[:, None, :].broadcast_to([P, GROUP, P]),
                                                        half[:, :, H_ROW:H_ROW + 1].broadcast_to([P, GROUP, P]),
                                                        ALU.is_equal).then_inc(q["place_ready"], 1)
                            for i in range(SETS):
                                for u in range(GROUP):
                                    dve.reg_load(regs[i][u], rec_of(b * SETS + i)[0:1, u, W_TILE:W_TILE + 1])
                            tiles = [[dve.snap(r, min_val=0, max_val=NT - 1) for r in of_set] for of_set in regs]
                            dve.wait_ge(q["place_ready"], it * TURNS + (b * SETS + SETS))
                            dve.sem_inc(q["taken"], 1)
                            dve.wait_ge(q["acc_clear"], 1)
                            for i in range(SETS):
                                j = b * SETS + i
                                for u in range(GROUP):
                                    mine = tile_of(acc, tiles[i][u], width)
                                    s.wait()
                                    if u == 0:
                                        dve.wait_ge(q["sum_ready"], it * TURNS + (j + 1 + TURNS))
                                    ins = nc.vector.tensor_tensor(mine, mine, bank(i, u), ALU.add)
                                    if u < GROUP - 1:
                                        s.done(ins)
                                    else:
                                        ins.then_inc(q["merged"], 1)
                                dve.wait_ge(q["merged"], it * TURNS + (j + 1 + 2))
                                dve.sem_inc(m.tick, 1)
                        s.fold()


def in_turns(eng, tile, unroll=4):
    with eng.Fori(0, NT // unroll - 1) as t:
        for k in range(unroll):
            tile(t * unroll + k, k % 2, False)
    for k in range(unroll):
        tile(NT - unroll + k, k % 2, k == unroll - 1)


def after0(nc, m, sem, psum, acc):
    names = ["summed", "sum_ready", "centred", "squared", "var_ready", "root_ready", "gain_ready", "scaled",
             "h_ready", "turned", "turned_used", "hid_ready", "tanh_ready", "product", "product_used"]
    q = {n: sem("a0_" + n) for n in names}
    parts = 4
    each = NT // parts
    with ExitStack() as ctx:
        def sb(name, shape):
            return ctx.enter_context(nc.sbuf_tensor("a0_" + name, shape, F32))
        hb = [sb(f"hb{i}", [P, D]) for i in range(2)]
        hT = [sb(f"hT{i}", [P, 2 * P]) for i in range(2)]
        hid = [sb(f"hid{i}", [HID, P]) for i in range(2)]
        fx = [sb(f"fx{i}", [P, OUT1]) for i in range(2)]
        den = sb("den", [P, NT * HEADS])
        rden = sb("rden", [P, NT * HEADS])
        tile_sum = sb("tile_sum", [P, D])
        mean = sb("mean", [P, D])
        var = sb("var", [P, D])
        root = sb("root", [P, D])
        gain = sb("gain", [P, D])
        acc4 = acc[:, :].rearrange("p (t h d) -> p t h d", t=NT, h=HEADS)
        acc3 = acc[:, :].rearrange("p (a d) -> p a d", d=DH + 1)
        squares = acc[:, 0:NT * D]

        def part(t, k):
            return t[:, k * each * D:(k + 1) * each * D].rearrange("p (t d) -> p t d", d=D)

        def for_tiles(row):
            return row.rearrange("p (o d) -> p o d", o=1).broadcast_to([P, each, D])

        with nc.Block() as block:
            @block.tensor
            def _(pe):
                for k in range(2):
                    pe.wait_ge(q["summed"], k + 1)
                    nc.tensor.matmul(psum[k][:, 0:D], m.ones[:, :], tile_sum[:, :], start=True, stop=True).then_inc(q["sum_ready"], 1)

                def turn(T, i):
                    pe.wait_ge(q["h_ready"], T + 1)
                    for c in range(2):
                        last = nc.tensor.transpose(psum[i][:, c * P:c * P + P], hb[i][:, c * P:c * P + P], m.ident[:, :])
                    last.then_inc(q["turned"], 1)

                def tile(T, i, last_tile):
                    if not last_tile:
                        turn(T + 1, 1 - i)
                    pe.wait_ge(q["turned_used"], T + 1)
                    for c in range(2):
                        last = nc.tensor.matmul(psum[2 + i][0:HID, 0:P], m.Wx1[:, c, :], hT[i][:, c * P:c * P + P],
                                                start=(c == 0), stop=(c == 1))
                    last.then_inc(q["hid_ready"], 1)
                    pe.wait_ge(q["product_used"], T + 1)
                    for c in range(2):
                        nc.tensor.matmul(psum[4 + i][:, HID:HID + OUT1], hT[i][:, c * P:c * P + P], m.Wfx[:, c, :], start=(c == 0), stop=(c == 1))
                    pe.wait_ge(q["tanh_ready"], T + 1)
                    nc.tensor.matmul(psum[4 + i][:, 0:HID], hid[i][:, :], m.Wx2[:, :], start=True, stop=True).then_inc(q["product"], 1)
                turn(0, 0)
                in_turns(pe, tile)

            @block.scalar
            def _(act):
                for k in range(parts):
                    act.wait_ge(q["centred"], k + 1)
                    nc.scalar.activation(part(squares, k), part(m.hbuf, k), ACT.Square).then_inc(q["squared"], 1)
                act.wait_ge(q["var_ready"], 1)
                nc.scalar.activation(root[:, :], var[:, :], ACT.Sqrt).then_inc(q["root_ready"], 1)
                act.wait_ge(m.ln_var_ready, 2)
                nc.scalar.activation(m.root[:, :], m.var[:, :], ACT.Sqrt).then_inc(m.ln_root_ready, 1)
                act.wait_ge(m.ln_shift_ready, 1)

                def h_of(T, i):
                    nc.scalar.activation(hb[i][:, :], tile_of(m.x, T, D), ACT.Relu, scale=m.rstd[:, bass.ds(T, 1)],
                                         bias=m.shift[:, bass.ds(T, 1)]).then_inc(q["h_ready"], 1)

                def tile(T, i, last):
                    if not last:
                        act.wait_ge(q["turned"], T + 1)
                        act.sem_inc(m.tick, 1)
                        h_of(T + 1, 1 - i)
                    act.wait_ge(q["turned"], T + 1)
                    act.wait_ge(q["product"], T + 1)
                    nc.scalar.activation(hT[i][:, :], psum[i][:, 0:2 * P], ACT.Copy).then_inc(q["turned_used"], 1)
                    act.wait_ge(q["hid_ready"], T + 1)
                    nc.scalar.activation(hid[i][:, :], psum[2 + i][0:HID, 0:P], ACT.Tanh, bias=m.bx1[:, :]).then_inc(q["tanh_ready"], 1)
                h_of(0, 0)
                in_turns(act, tile)

            @block.gpsimd
            def _(pool):
                pool.wait_ge(q["gain_ready"], 1)
                for k in range(parts // 2, parts):
                    nc.gpsimd.tensor_tensor(part(m.hbuf, k), part(m.hbuf, k), for_tiles(gain[:, :]), ALU.mult).then_inc(q["scaled"], 1)

            @block.vector
            def _(dve):
                s = Steps(dve, m)
                s.done(nc.vector.tensor_scalar(m.empty[:, :], m.degree[:, :], 0.0, None, ALU.is_equal))
                s.wait()
                s.done(nc.vector.tensor_tensor(den[:, :].rearrange("p (t h o) -> p t h o", t=NT, o=1), acc4[:, :, :, DH:DH + 1],
                                               m.empty[:, :].rearrange("p (t h o) -> p t h o", h=1, o=1).broadcast_to([P, NT, HEADS, 1]), ALU.add))
                s.wait()
                s.done(nc.vector.reciprocal(rden[:, :], den[:, :]))
                s.wait()
                s.done(nc.vector.tensor_tensor(m.hbuf[:, :].rearrange("p (a d) -> p a d", d=DH), acc3[:, :, 0:DH],
                                               rden[:, :].rearrange("p (a o) -> p a o", o=1).broadcast_to([P, NT * HEADS, DH]), ALU.mult))
                s.wait()
                dve.sem_inc(m.tick, 1)
                s.fold()
                with dve.Fori(0, NT // 4) as t4:
                    for i in range(4):
                        T = t4 * 4 + i
                        mine = tile_of(m.hbuf, T, D).rearrange("p (h d) -> p h d", h=HEADS)
                        s.done(nc.vector.scalar_tensor_tensor(mine, m.mean0[:, :].rearrange("p (h d) -> p h d", h=HEADS)[:, :, 0:DH],
                                                              m.empty[:, bass.ds(T, 1)], mine, ALU.mult, ALU.add))
                    s.fold()
                s.wait()
                nc.vector.tensor_reduce(tile_sum[:, :], m.hbuf[:, :].rearrange("p (t d) -> p d t", d=D), AX.X, ALU.add).then_inc(q["summed"], 1)
                dve.wait_ge(q["sum_ready"], 1)
                s.done(nc.vector.tensor_scalar(mean[:, :], psum[0][:, 0:D], 1.0 / N, None, ALU.mult))
                s.wait()
                for k in range(parts):
                    nc.vector.tensor_tensor(part(m.hbuf, k), part(m.hbuf, k), for_tiles(mean[:, :]), ALU.subtract).then_inc(q["centred"], 1)
                dve.wait_ge(q["squared"], parts)
                nc.vector.tensor_reduce(tile_sum[:, :], squares.rearrange("p (t d) -> p d t", d=D), AX.X, ALU.add).then_inc(q["summed"], 1)
                dve.wait_ge(q["sum_ready"], 2)
                nc.vector.tensor_scalar(var[:, :], psum[1][:, 0:D], 1.0 / N, EPS, ALU.mult, ALU.add).then_inc(q["var_ready"], 1)
                dve.wait_ge(q["root_ready"], 1)
                s.done(nc.vector.reciprocal(mean[:, :], root[:, :]))
                s.wait()
                nc.vector.tensor_tensor(gain[:, :], mean[:, :], m.norm[:, 0:D], ALU.mult).then_inc(q["gain_ready"], 1)
                dve.wait_ge(q["gain_ready"], 1)
                for k in range(parts // 2):
                    s.done(nc.vector.tensor_tensor(part(m.hbuf, k), part(m.hbuf, k), for_tiles(gain[:, :]), ALU.mult))
                for k in range(parts):
                    s.wait()
                    if k >= parts // 2:
                        dve.wait_ge(q["scaled"], k + 1 - parts // 2)
                    s.done(nc.vector.tensor_tensor(part(m.hbuf, k), part(m.hbuf, k), for_tiles(m.norm[:, D:2 * D]), ALU.add))
                    s.wait()
                    s.done(nc.vector.scalar_tensor_tensor(part(m.x, k), part(m.hbuf, k), 0.0, part(m.x, k), ALU.max, ALU.add))
                s.wait()
                dve.sem_inc(m.tick, 1)
                s.fold()
                x_stats(nc, m, s)
                layernorm_scale(nc, m, s, 2)
                dve.sem_inc(m.ln_shift_ready, 1)
                dve.sem_inc(q["product_used"], 2)
                dve.sem_inc(q["product"], 2)
                s.fold()
                with dve.Fori(0, NT // 2) as t2:
                    for i in range(2):
                        T = t2 * 2 + i
                        dve.wait_ge(q["product"], T + 3)
                        nc.vector.tensor_tensor(tile_of(m.row1, T, HID), psum[4 + i][:, 0:HID], m.bias_x_rows[:, 0:HID], ALU.add)
                        nc.vector.tensor_tensor(fx[i][:, :], psum[4 + i][:, HID:HID + OUT1], m.bias_x_rows[:, HID:HID + OUT1],
                                                ALU.add).then_inc(q["product_used"], 1)
                        mine = m.x[:, bass.ds(T * D, OUT1)]
                        dve.wait_ge(q["product_used"], T + 3)
                        nc.vector.tensor_tensor(mine, mine, fx[i][:, :], ALU.add)


def after1(nc, m, sem, acc, table2):
    q = {n: sem("a1_" + n) for n in ["h_ready", "stored"]}
    with ExitStack() as ctx:
        den = ctx.enter_context(nc.sbuf_tensor("a1_den", [P, NT], F32))
        rden = ctx.enter_context(nc.sbuf_tensor("a1_rden", [P, NT], F32))
        parts = 4
        each = NT // parts
        with nc.Block() as block:
            @block.scalar
            def _(act):
                for k in range(parts):
                    mine = slice(k * each, (k + 1) * each)
                    act.wait_ge(m.ln_var_ready, 3 + k)
                    nc.scalar.activation(m.root[:, mine], m.var[:, mine], ACT.Sqrt).then_inc(m.ln_root_ready, 1)
                    act.wait_ge(m.ln_shift_ready, 2 + k)
                    with act.Fori(0, each // 4) as t4:
                        for j in range(4):
                            T = t4 * 4 + (k * each + j)
                            nc.scalar.activation(tile_of(m.hbuf, T, D), tile_of(m.x, T, D), ACT.Relu, scale=m.rstd[:, bass.ds(T, 1)],
                                                 bias=m.shift[:, bass.ds(T, 1)]).then_inc(q["h_ready"], 1)

            @block.sync
            def _(sp):
                for i in range(parts):
                    sp.wait_ge(q["h_ready"], (i + 1) * each)
                    sp.dma_start(table2[i * each * P:(i + 1) * each * P, :].rearrange("(t p) d -> p t d", p=P),
                                 m.hbuf[:, i * each * D:(i + 1) * each * D].rearrange("p (t d) -> p t d", d=D)).then_inc(q["stored"], 16)
                sp.wait_ge(q["stored"], 16 * parts)

            @block.vector
            def _(dve):
                s = Steps(dve, m)
                acc3 = acc[:, :].rearrange("p (t w) -> p t w", w=H1)
                s.done(nc.vector.tensor_tensor(den[:, :].rearrange("p (t o) -> p t o", o=1), acc3[:, :, OUT1:H1],
                                               m.empty[:, :].rearrange("p (t o) -> p t o", o=1), ALU.add))
                s.wait()
                s.done(nc.vector.reciprocal(rden[:, :], den[:, :]))
                s.fold()
                s.wait()
                dve.sem_inc(m.tick, 1)
                for k in range(parts):
                    with dve.Fori(0, each // 4) as t4:
                        for i in range(4):
                            T = t4 * 4 + (k * each + i)
                            mine = m.x[:, bass.ds(T * D + OUT1, OUT1)]
                            s.done(nc.vector.scalar_tensor_tensor(mine, acc[:, bass.ds(T * H1, OUT1)], rden[:, bass.ds(T, 1)], mine, ALU.mult, ALU.add))
                        s.fold()
                    s.wait()
                    dve.sem_inc(m.tick, 1)
                    with dve.Fori(0, each // 4) as t4:
                        for i in range(4):
                            T = t4 * 4 + (k * each + i)
                            mine = m.x[:, bass.ds(T * D + OUT1, OUT1)]
                            s.done(nc.vector.scalar_tensor_tensor(mine, m.mean1[:, 0:OUT1], m.empty[:, bass.ds(T, 1)], mine, ALU.mult, ALU.add))
                        s.fold()
                    s.wait()
                    dve.sem_inc(m.tick, 1)
                    x_stats(nc, m, s, first=k * each, tiles=each)
                    layernorm_scale(nc, m, s, 3 + k, first=k * each, tiles=each)
                    dve.sem_inc(m.ln_shift_ready, 1)
                    s.fold()


def after2(nc, m, sem, psum, acc, table3):
    names = ["mean_ready", "pair_ready", "turned", "turned_used", "product", "product_used", "h_ready",
             "turned3", "turned3_used", "product3", "product3_used", "column", "column_turned", "column_ready", "stored"]
    q = {n: sem("a2_" + n) for n in names}
    with ExitStack() as ctx:
        def sb(name, shape):
            return ctx.enter_context(nc.sbuf_tensor("a2_" + name, shape, F32))
        pair = [sb(f"pair{i}", [P, 2 * D]) for i in range(2)]
        pairT = [sb(f"pairT{i}", [P, 2 * D]) for i in range(2)]
        biased = [sb(f"biased{i}", [P, D]) for i in range(2)]
        rdeg = sb("rdeg", [P, NT])
        deg1 = sb("deg1", [P, NT])
        col = sb("col", [P, NT])
        colT = sb("colT", [NT, P])
        with nc.Block() as block:
            @block.sync
            def _(sp):
                sp.wait_ge(q["column_ready"], 1)
                sp.dma_start(table3.rearrange("(t p) o -> t (p o)", p=P), colT[:, :]).then_inc(q["stored"], 16)
                sp.wait_ge(q["stored"], 16)

            @block.scalar
            def _(act):
                act.wait_ge(q["mean_ready"], 1)

                def pair_of(T, i):
                    nc.scalar.activation(pair[i][:, 0:D], tile_of(m.hbuf, T, D), ACT.Copy)
                    nc.scalar.activation(pair[i][:, D:2 * D], tile_of(acc, T, D), ACT.Copy, scale=rdeg[:, bass.ds(T, 1)]).then_inc(q["pair_ready"], 1)

                def tile(T, i, last):
                    if not last:
                        act.wait_ge(q["turned"], T + 1)
                        act.sem_inc(m.tick, 1)
                        pair_of(T + 1, 1 - i)
                pair_of(0, 0)
                in_turns(act, tile)
                act.wait_ge(m.ln_var_ready, 7)
                nc.scalar.activation(m.root[:, :], m.var[:, :], ACT.Sqrt).then_inc(m.ln_root_ready, 1)
                act.wait_ge(m.ln_shift_ready, 6)

                def h_of(T, i):
                    nc.scalar.activation(pair[i][:, 0:D], tile_of(m.x, T, D), ACT.Relu, scale=m.rstd[:, bass.ds(T, 1)],
                                         bias=m.shift[:, bass.ds(T, 1)]).then_inc(q["h_ready"], 1)

                def tile3(T, i, last):
                    if not last:
                        act.wait_ge(q["turned3"], T + 1)
                        act.wait_ge(q["column"], T + 1)
                        act.sem_inc(m.tick, 1)
                        h_of(T + 1, 1 - i)
                    act.wait_ge(q["turned3"], T + 1)
                    act.wait_ge(q["product3"], T + 1)
                    nc.scalar.activation(pairT[i][:, 0:D], psum[i][:, 0:D], ACT.Copy).then_inc(q["turned3_used"], 1)
                h_of(0, 0)
                in_turns(act, tile3)

            @block.tensor
            def _(pe):
                def turn(T, i):
                    pe.wait_ge(q["pair_ready"], T + 1)
                    pe.wait_ge(q["turned_used"], T + 1)
                    for c in range(4):
                        last = nc.tensor.transpose(psum[i][:, c * P:c * P + P], pair[i][:, c * P:c * P + P], m.ident[:, :])
                    last.then_inc(q["turned"], 1)

                def tile(T, i, last):
                    if not last:
                        turn(T + 1, 1 - i)
                    pe.wait_ge(q["turned_used"], T + 3)
                    pe.wait_ge(q["product_used"], T + 1)
                    for c in range(4):
                        w = (m.W2s, m.W2n)[c // 2][:, c % 2, :]
                        last_one = nc.tensor.matmul(psum[2 + i][:, 0:D], pairT[i][:, c * P:c * P + P], w, start=(c == 0), stop=(c == 3))
                    last_one.then_inc(q["product"], 1)
                turn(0, 0)
                in_turns(pe, tile)

                def turn3(T, i):
                    pe.wait_ge(q["h_ready"], T + 1)
                    for c in range(2):
                        last = nc.tensor.transpose(psum[i][:, c * P:c * P + P], pair[i][:, c * P:c * P + P], m.ident[:, :])
                    last.then_inc(q["turned3"], 1)

                def tile3(T, i, last):
                    if not last:
                        turn3(T + 1, 1 - i)
                    pe.wait_ge(q["turned3_used"], T + 1)
                    pe.wait_ge(q["product3_used"], T + 1)
                    for c in range(2):
                        last_one = nc.tensor.matmul(psum[2 + i][:, 0:D], pairT[i][:, c * P:c * P + P], m.S3T[:, c, :], start=(c == 0), stop=(c == 1))
                    last_one.then_inc(q["product3"], 1)
                turn3(0, 0)
                in_turns(pe, tile3)
                pe.wait_ge(q["column"], NT + 1)
                nc.tensor.matmul(psum[4][0:NT, 0:P], col[:, :], m.ident[:, :], start=True, stop=True).then_inc(q["column_turned"], 1)

            @block.vector
            def _(dve):
                s = Steps(dve, m)
                s.done(nc.vector.tensor_scalar(deg1[:, :], m.degree[:, :], 1.0, None, ALU.max))
                s.wait()
                nc.vector.reciprocal(rdeg[:, :], deg1[:, :]).then_inc(q["mean_ready"], 1)
                dve.sem_inc(q["turned_used"], 2)
                dve.sem_inc(q["product_used"], 2)
                s.fold()

                def copy_turned(T, i):
                    dve.wait_ge(q["turned"], T + 1)
                    nc.vector.tensor_copy(pairT[i][:, :], psum[i][:, :]).then_inc(q["turned_used"], 1)

                def tile(T, i, last):
                    if not last:
                        copy_turned(T + 1, 1 - i)
                    mine = tile_of(m.x, T, D)
                    dve.wait_ge(q["product"], T + 1)
                    nc.vector.tensor_tensor(biased[i][:, :], psum[2 + i][:, 0:D], m.bias_2_rows[:, :], ALU.add).then_inc(q["product_used"], 1)
                    dve.wait_ge(q["product_used"], T + 3)
                    s.done(nc.vector.scalar_tensor_tensor(mine, biased[i][:, :], 0.0, mine, ALU.max, ALU.add))
                    s.fold()
                copy_turned(0, 0)
                in_turns(dve, tile)
                s.wait()
                dve.sem_inc(m.tick, 1)
                x_stats(nc, m, s)
                layernorm_scale(nc, m, s, 7)
                dve.sem_inc(m.ln_shift_ready, 1)
                dve.sem_inc(q["product3_used"], 2)
                dve.sem_inc(q["product3"], 2)
                dve.sem_inc(q["column"], 1)

                def column(T, i):
                    dve.wait_ge(q["h_ready"], T + 1)
                    nc.vector.tensor_copy(col[:, bass.ds(T, 1)], pair[i][:, 0:1]).then_inc(q["column"], 1)

                def tile3(T, i, last):
                    if not last:
                        column(T + 1, 1 - i)
                    dve.wait_ge(q["product3"], T + 3)
                    nc.vector.tensor_copy(tile_of(m.hbuf, T, D), psum[2 + i][:, 0:D]).then_inc(q["product3_used"], 1)
                column(0, 0)
                in_turns(dve, tile3)
                dve.wait_ge(q["column_turned"], 1)
                nc.vector.tensor_copy(colT[:, :], psum[4][0:NT, 0:P]).then_inc(q["column_ready"], 1)


def after3(nc, m, sem, acc, out):
    q = {n: sem("a3_" + n) for n in ["x_ready", "stored"]}
    parts = 4
    each = NT // parts
    with nc.Block() as block:
        @block.sync
        def _(sp):
            for i in range(parts):
                sp.wait_ge(q["x_ready"], i + 1)
                sp.dma_start(out[i * each * P:(i + 1) * each * P, :].rearrange("(t p) d -> p t d", p=P),
                             m.x[:, i * each * D:(i + 1) * each * D].rearrange("p (t d) -> p t d", d=D)).then_inc(q["stored"], 16)
            sp.wait_ge(q["stored"], 16 * parts)

        @block.vector
        def _(dve):
            s = Steps(dve, m)
            for k in range(parts):
                with dve.Fori(0, each // 4) as t4:
                    for i in range(4):
                        T = t4 * 4 + (k * each + i)
                        own = tile_of(m.hbuf, T, D)
                        s.done(nc.vector.scalar_tensor_tensor(own, m.neigh_sum[:, :], acc[:, bass.ds(T, 1)], own, ALU.mult, ALU.add))
                    s.fold()
                s.wait()
                mine, own = (t[:, k * each * D:(k + 1) * each * D] for t in (m.x, m.hbuf))
                nc.vector.scalar_tensor_tensor(mine, own, 0.0, mine, ALU.max, ALU.add).then_inc(q["x_ready"], 1)


def build(nc, a, out):
    def scratch(name, shape, dt=F32):
        return nc.dram_tensor(name, shape, dt, kind="Internal").ap()
    edges = scratch("edges", (P, MAX_CHUNKS, WORDS), I32)
    table0 = scratch("table0", (N, ROW0))
    table1 = scratch("table1", (N, ROW1))
    table2 = scratch("table2", (N, D))
    table3 = scratch("table3", (N, 1))
    with ExitStack() as ctx:
        m = Mem()
        def sem(name):
            return ctx.enter_context(nc.semaphore(name))
        def keep(name, shape, dt=F32):
            return ctx.enter_context(nc.sbuf_tensor(name, shape, dt))
        m.iota_row_i = keep("iota_row_i", [P, P], I32)
        m.iota_col_i = keep("iota_col_i", [P, 1], I32)
        m.iota_row = keep("iota_row", [P, P])
        m.iota_col = keep("iota_col", [P, 1])
        m.iota_row_h = keep("iota_row_h", [P, P], BF16)
        m.ident_h = keep("ident_h", [P, P], BF16)
        m.ident = keep("ident", [P, P])
        m.tri = keep("tri", [P, P])
        m.ones = keep("ones", [P, P])
        m.degree = keep("degree", [P, NT])
        m.passes = keep("passes", [P, 1], I32)
        m.double_passes = keep("double_passes", [P, 1], I32)
        m.x = keep("x", [P, NT * D])
        m.hbuf = keep("hbuf", [P, NT * D])
        m.acc = keep("acc", [P, NT * H0])
        m.adj_rows = [t[:, k * N:(k + 1) * N].bitcast(I32) for t in (m.hbuf, m.acc) for k in range(2)]
        m.adj_in = [sem(f"adj_in{i}") for i in range(BUFS)]
        m.gathered_rows = keep("gathered_rows", [P, PAD * ROW0])
        m.W0T = keep("W0T", [P, 2, D + 2 * HEADS])
        m.Wx1 = keep("Wx1", [P, 2, HID])
        m.Wx2 = keep("Wx2", [HID, HID])
        m.Wn1 = keep("Wn1", [P, 2, HID])
        m.Wn2 = keep("Wn2", [HID, HID])
        m.Wv = keep("Wv", [P, 2, OUT1])
        m.Wfx = keep("Wfx", [P, 2, OUT1])
        m.W2s = keep("W2s", [P, 2, D])
        m.W2n = keep("W2n", [P, 2, D])
        m.S3T = keep("S3T", [P, 2, D])
        m.bias_n = keep("bias_n", [1, OUT1 + HID])
        m.bias_x = keep("bias_x", [1, OUT1 + HID])
        m.norm_in = keep("norm_in", [1, 2 * D])
        m.norm = keep("norm", [P, 2 * D])
        m.bias_2 = keep("bias_2", [1, D])
        m.bias_x_rows = keep("bias_x_rows", [P, HID + OUT1])
        m.bias_2_rows = keep("bias_2_rows", [P, D])
        m.neigh_sum = keep("neigh_sum", [P, D])
        m.bx1 = keep("bx1", [HID, 1])
        m.bn1 = keep("bn1", [HID, 1])
        m.stats = keep("stats", [P, NT * 6])
        m.mean_sum = keep("mean_sum", [P, NT])
        m.mean_gap = keep("mean_gap", [P, NT])
        m.dev_sum = keep("dev_sum", [P, NT])
        m.var = keep("var", [P, NT])
        m.root = keep("root", [P, NT])
        m.rstd = keep("rstd", [P, NT])
        m.shift = keep("shift", [P, NT])
        m.score_i = keep("score_i", [P, NT * HEADS])
        m.row1 = keep("row1", [P, NT * HID])
        m.mean0 = keep("mean0", [P, H0])
        m.mean1 = keep("mean1", [P, ROW1])
        m.empty = keep("empty", [P, NT])
        m.running = keep("running", [P, NT * HEADS])
        psum = [ctx.enter_context(nc.psum_tensor(f"bank{i}", [P, 512], F32)) for i in range(8)]
        m.tick = sem("tick")
        m.vec_steps = sem("vec_steps")
        m.ln_var_ready = sem("ln_var_ready")
        m.ln_root_ready = sem("ln_root_ready")
        m.ln_shift_ready = sem("ln_shift_ready")
        m.vec_open = 0
        m.vec_count = ctx.enter_context(nc.vector.register("vec_count"))
        constants(nc, m, sem)
        weights(nc, m, sem, psum, a)
        scan(nc, m, sem, psum, a["adj"], edges, a["L1_gnn_neigh"], table0, table1)
        attend(nc, m, sem, psum, "l0", edges, table0, HEADS, DH + 1, HEADS, m.score_i, HEADS, 0.2, m.running, m.acc)
        after0(nc, m, sem, psum, m.acc)
        acc1 = m.acc[:, 0:NT * H1]
        attend(nc, m, sem, psum, "l1", edges, table1, 1, H1, HID, m.row1, HID, 0.01, m.running[:, 0:NT], acc1)
        after1(nc, m, sem, acc1, table2)
        acc2 = m.acc[:, 0:NT * D]
        gather_sum(nc, m, sem, psum, "l2", edges, table2, D, acc2)
        after2(nc, m, sem, psum, acc2, table3)
        acc3 = m.acc[:, 0:NT]
        gather_sum(nc, m, sem, psum, "l3", edges, table3, 1, acc3)
        after3(nc, m, sem, acc3, out)


_INS = ["x", "adj", "L0_gnn_W", "L0_gnn_a", "L0_gnn_gamma", "L0_gnn_beta", "L1_gnn_neigh", "L1_gnn_Wx1", "L1_gnn_bx1", "L1_gnn_Wx2",
        "L1_gnn_bx2", "L1_gnn_Wn1", "L1_gnn_bn1", "L1_gnn_Wn2", "L1_gnn_bn2", "L1_gnn_Wv", "L1_gnn_bv", "L1_gnn_Wfx", "L1_gnn_bfx",
        "L2_gnn_W_self", "L2_gnn_b_self", "L2_gnn_W_nb", "L2_gnn_b_nb", "L2_gnn_W_comb", "L2_gnn_b_comb", "L3_gnn_w_self",
        "L3_gnn_w_neigh"]


def kernel(**inputs):
    import numpy as _np
    import concourse.bacc as _bacc
    from concourse import mybir as _mybir
    from concourse.bass_utils import run_bass_kernel_spmd as _run

    nc = _bacc.Bacc("TRN2", target_bir_lowering=False, num_devices=1)
    arrays, args = {}, {}
    for name in _INS:
        a = _np.ascontiguousarray(inputs[name])
        arrays[f"in_{name}_dram"] = a
        args[name] = nc.dram_tensor(f"in_{name}_dram", a.shape, _mybir.dt.from_np(a.dtype), kind="ExternalInput").ap()
    out = nc.dram_tensor("out_0_dram", (N, D), F32, kind="ExternalOutput").ap()
    build(nc, args, out)
    r = _run(nc, [arrays], core_ids=[0])
    return r.results[0]["out_0_dram"]
```
